# Optimizing a Trainium2 kernel written in Bass

```python
import numpy as np
import jax
import jax.numpy as jnp

def _softmax(x, axis=-1):
    return jax.nn.softmax(x, axis=axis)

def _gelu(x):
    return jax.nn.gelu(x, approximate=True)

def _silu(x):
    return jax.nn.silu(x)

def _sigmoid(x):
    return jax.nn.sigmoid(x)

def _layernorm(x, axis=-1, eps=1e-05):
    m = jnp.mean(x, axis=axis, keepdims=True)
    v = jnp.var(x, axis=axis, keepdims=True)
    return (x - m) / jnp.sqrt(v + eps)

def _scatter_add(tgt, idx, src, axis=0):
    return tgt.at[idx].add(src)

def _segment_sum(src, seg, n):
    return jax.ops.segment_sum(src, seg, n)
kernel_name = 'mk_lm_tower_d2_tok_ids1024_r4_94862c'

def setup_inputs(seed: int=0):
    np.random.seed(seed)
    _w = jnp.asarray

    def _rec_inputs():
        import jax
        import jax.numpy as jnp
        _rk = jax.random.key(seed)
        x = jax.random.randint(jax.random.fold_in(_rk, 1), (4, 512), 0, 267694, jnp.int32)
        return x
    x = _rec_inputs()

    def _L0_tok_setup():
        import jax, jax.numpy as jnp
        import numpy as np
        N_TOKEN = 267735
        CUTOFFS = [0, 5000, 10000, 50000, N_TOKEN]
        D_PROJ = 256
        D_EMBED = 256
        DIV = 4
        B, S = (8, 512)
        key = jax.random.key(seed)
        ks = jax.random.split(key, 9)
        tokens = jax.random.randint(ks[0], (B, S), 0, N_TOKEN, dtype=jnp.int64 if jax.config.jax_enable_x64 else jnp.int32)
        inp = {'tokens': tokens}
        for i in range(4):
            l, r = (CUTOFFS[i], CUTOFFS[i + 1])
            de = D_EMBED // DIV ** i
            inp[f'emb{i}'] = jax.random.normal(ks[1 + i], (r - l, de), dtype=jnp.float32) * 0.02
            if de != D_PROJ:
                inp[f'proj{i}'] = jax.random.normal(ks[5 + i], (de, D_PROJ), dtype=jnp.float32) * 0.02
        return inp
    _L0_tok_all = _L0_tok_setup()
    _L0_tok_in = {k: v for k, v in _L0_tok_all.items() if k in ('emb0', 'emb1', 'emb2', 'emb3', 'proj1', 'proj2', 'proj3')}
    del _L0_tok_all

    def _L0_attn_setup():
        import jax, jax.numpy as jnp
        import numpy as np
        import math
        B, L, D = (2, 1024, 256)
        H, DK, DV = (4, 64, 64)
        CHUNK = 32
        PROB_FLOOR = 0.02

        def _l2norm(x, eps=1e-06):
            return x * jax.lax.rsqrt(jnp.sum(x * x, -1, keepdims=True) + eps)

        def _silu(x):
            return x * jax.nn.sigmoid(x)

        def _short_conv(x, w):
            K = w.shape[-1]
            xp = jnp.pad(x, ((0, 0), (K - 1, 0), (0, 0)))
            y = sum((xp[:, j:j + x.shape[1], :] * w[:, j] for j in range(K)))
            return _silu(y)

        def _fir_conv(x, filt):
            b, l, h, d = x.shape
            K = filt.shape[-1]
            xf = jnp.pad(x.reshape(b, l, h * d).transpose(0, 2, 1), ((0, 0), (0, 0), (K - 1, 0)))
            w = filt.reshape(h * d, 1, K)
            y = jax.lax.conv_general_dilated(xf, w, (1,), 'VALID', dimension_numbers=('NCH', 'OIH', 'NCH'), feature_group_count=h * d)
            return y.transpose(0, 2, 1).reshape(b, l, h, d)

        def _delta_rule_chunkwise(q, k, v, beta, chunk=CHUNK):
            b, h, Lq, dk = q.shape
            dv = v.shape[-1]
            n = Lq // chunk
            q = _l2norm(q)
            k = _l2norm(k)
            v = v * beta[..., None]
            kb = k * beta[..., None]
            rs = lambda t: t.reshape(b, h, n, chunk, t.shape[-1])
            qc, kc, vc, kbc = (rs(q), rs(k), rs(v), rs(kb))
            strict_lower = jnp.tril(jnp.ones((chunk, chunk), bool), -1)
            M = jnp.where(strict_lower, jnp.einsum('bhncd,bhnmd->bhncm', kbc, kc), 0.0)
            eye = jnp.eye(chunk, dtype=q.dtype)
            T = jax.scipy.linalg.solve_triangular(eye + M, jnp.broadcast_to(eye, M.shape), lower=True, unit_diagonal=True)
            u = T @ vc
            w = T @ kbc
            incl_lower = jnp.tril(jnp.ones((chunk, chunk), bool), 0)

            def step(S, xs):
                q_i, k_i, u_i, w_i = xs
                attn = jnp.where(incl_lower, q_i @ k_i.swapaxes(-1, -2), 0.0)
                u_adj = u_i - w_i @ S
                out_i = q_i @ S + attn @ u_adj
                S = S + k_i.swapaxes(-1, -2) @ u_adj
                return (S, out_i)
            S0 = jnp.zeros((b, h, dk, dv), q.dtype)
            xs = tuple((jnp.moveaxis(t, 2, 0) for t in (qc, kc, u, w)))
            S, out = jax.lax.scan(step, S0, xs)
            out = jnp.moveaxis(out, 0, 2).reshape(b, h, Lq, dv)
            return (out, S)

        def _rmsnorm(x, w, eps=1e-05):
            return x * jax.lax.rsqrt(jnp.mean(x * x, -1, keepdims=True) + eps) * w

        def _per_head_stats(x):
            mean = jnp.mean(x, -1, keepdims=True)
            var = jnp.var(x, -1, keepdims=True)
            am = jnp.mean(jnp.abs(x), -1, keepdims=True)
            l2 = jnp.sqrt(jnp.sum(x * x, -1, keepdims=True))
            return jnp.concatenate([mean, var, am, l2], -1)

        def _forward(hidden_states, q_w, k_w, v_w, b_w, q_cw, k_cw, v_cw, fir_short_w, fir_long_w, mlp1_w, mlp1_b, mlp2_w, mlp2_b, logit_temp, conv_res_logit, norm_w, o_w):
            b, l, _ = hidden_states.shape
            q_in = _short_conv(hidden_states @ q_w.T, q_cw)
            k_in = _short_conv(hidden_states @ k_w.T, k_cw)
            v_in = _short_conv(hidden_states @ v_w.T, v_cw)
            q = q_in.reshape(b, l, H, DK)
            k = k_in.reshape(b, l, H, DK)
            v_direct = v_in.reshape(b, l, H, DV)
            beta = jnp.maximum(jax.nn.sigmoid(hidden_states @ b_w.T), 1e-06)
            delta_out, _S = _delta_rule_chunkwise(q.transpose(0, 2, 1, 3), k.transpose(0, 2, 1, 3), v_direct.transpose(0, 2, 1, 3), beta.transpose(0, 2, 1))
            delta_out = delta_out.transpose(0, 2, 1, 3)
            local_short = _fir_conv(v_direct, fir_short_w)
            local_long = _fir_conv(v_direct, fir_long_w)
            stats = jnp.concatenate([_per_head_stats(local_short), _per_head_stats(local_long), _per_head_stats(delta_out), _per_head_stats(v_direct)], -1)
            hs_exp = jnp.broadcast_to(hidden_states[:, :, None, :], (b, l, H, hidden_states.shape[-1]))
            gate_in = jnp.concatenate([hs_exp, stats], -1)
            h1 = jax.nn.gelu(gate_in @ mlp1_w.T + mlp1_b)
            logits = h1 @ mlp2_w.T + mlp2_b
            temp = jax.nn.softplus(logit_temp)
            p = jax.nn.softmax(logits / temp, -1)
            p = jnp.maximum(p, PROB_FLOOR)
            p = p / jnp.sum(p, -1, keepdims=True)
            o = p[..., 0:1] * local_short + p[..., 1:2] * local_long + p[..., 2:3] * delta_out + p[..., 3:4] * v_direct
            o = o + jax.nn.sigmoid(conv_res_logit)[None, None, :, None] * local_short
            o = _rmsnorm(o, norm_w)
            o = o.reshape(b, l, H * DV) @ o_w.T
            return o
        key = jax.random.key(seed)
        ks = jax.random.split(key, 16)
        s = 0.02
        hidden_gate = D * 2 // 2
        gate_in_dim = D + 16
        inp = {'hidden_states': jax.random.normal(ks[0], (B, L, D), jnp.float32), 'q_w': jax.random.normal(ks[1], (D, D), jnp.float32) * s, 'k_w': jax.random.normal(ks[2], (D, D), jnp.float32) * s, 'v_w': jax.random.normal(ks[3], (D, D), jnp.float32) * s, 'b_w': jax.random.normal(ks[4], (H, D), jnp.float32) * s, 'q_cw': jax.random.normal(ks[5], (D, 4), jnp.float32) * s, 'k_cw': jax.random.normal(ks[6], (D, 4), jnp.float32) * s, 'v_cw': jax.random.normal(ks[7], (D, 4), jnp.float32) * s, 'fir_short_w': jax.random.normal(ks[8], (H, DV, 5), jnp.float32) * s, 'fir_long_w': jax.random.normal(ks[9], (H, DV, 64), jnp.float32) * s, 'mlp1_w': jax.random.normal(ks[10], (hidden_gate, gate_in_dim), jnp.float32) * s, 'mlp1_b': jnp.zeros((hidden_gate,), jnp.float32), 'mlp2_w': jax.random.normal(ks[11], (4, hidden_gate), jnp.float32) * s, 'mlp2_b': jnp.array([-0.5, -0.5, 1.0, 3.0], jnp.float32), 'logit_temp': jnp.full((1,), math.log(math.expm1(0.7)), jnp.float32), 'conv_res_logit': jnp.full((H,), -2.0, jnp.float32), 'norm_w': jnp.ones((DV,), jnp.float32), 'o_w': jax.random.normal(ks[12], (D, D), jnp.float32) * s}
        return inp
    _L0_attn_all = _L0_attn_setup()
    _L0_attn_in = {k: v for k, v in _L0_attn_all.items() if k in ('q_w', 'k_w', 'v_w', 'b_w', 'q_cw', 'k_cw', 'v_cw', 'fir_short_w', 'fir_long_w', 'mlp1_w', 'mlp1_b', 'mlp2_w', 'mlp2_b', 'logit_temp', 'conv_res_logit', 'norm_w', 'o_w')}
    del _L0_attn_all

    def _L0_ffn_setup():
        import jax, jax.numpy as jnp
        import numpy as np
        DIM = 256
        HEADS = 8
        NUM_EXPERTS = 16384
        NUM_KEYS = 64
        DIM_KEY = 128
        TOPK = 16

        def _rmsnorm(v, g):
            scale = jnp.sqrt(jnp.asarray(v.shape[-1], v.dtype))
            n = jnp.maximum(jnp.linalg.norm(v, axis=-1, keepdims=True), 1e-12)
            return v / n * g * scale
        key = jax.random.key(seed)
        ks = jax.random.split(key, 6)
        B, N = (2, 128)
        x = jax.random.normal(ks[0], (B, N, DIM), dtype=jnp.float32)
        gamma = jnp.ones((DIM,), dtype=jnp.float32)
        wq = jax.random.normal(ks[1], (2 * HEADS * DIM_KEY, DIM), dtype=jnp.float32) * 0.02
        keys = jax.random.normal(ks[2], (HEADS, NUM_KEYS, 2, DIM_KEY), dtype=jnp.float32) * 0.02
        table_down = jax.random.normal(ks[3], (NUM_EXPERTS, DIM), dtype=jnp.float32) * 0.02
        table_up = jax.random.normal(ks[4], (NUM_EXPERTS, DIM), dtype=jnp.float32) * 0.02
        return {'x': x, 'gamma': gamma, 'wq': wq, 'keys': keys, 'table_down': table_down, 'table_up': table_up}
    _L0_ffn_all = _L0_ffn_setup()
    _L0_ffn_in = {k: v for k, v in _L0_ffn_all.items() if k in ('gamma', 'wq', 'keys', 'table_down', 'table_up')}
    del _L0_ffn_all

    def _L1_attn_setup():
        import jax, jax.numpy as jnp
        import numpy as np
        BATCH, T, D_MODEL, D_STATE, EXPAND = (4, 1024, 256, 16, 2)
        D_INNER = D_MODEL * EXPAND
        key = jax.random.key(seed)
        ks = jax.random.split(key, 6)
        s = 0.02
        return {'x': jax.random.normal(ks[0], (BATCH, T, D_MODEL), jnp.float32), 'W_in': jax.random.normal(ks[1], (2 * D_INNER, D_MODEL), jnp.float32) * s, 'b_in': jnp.zeros((2 * D_INNER,), jnp.float32), 'W_B': jax.random.normal(ks[2], (D_STATE, D_INNER), jnp.float32) * s, 'W_C': jax.random.normal(ks[3], (D_INNER, D_STATE), jnp.float32) * s, 'D': jnp.ones((D_INNER,), jnp.float32), 'W_out': jax.random.normal(ks[4], (D_MODEL, D_INNER), jnp.float32) * s, 'b_out': jnp.zeros((D_MODEL,), jnp.float32)}
    _L1_attn_all = _L1_attn_setup()
    _L1_attn_in = {k: v for k, v in _L1_attn_all.items() if k in ('W_in', 'b_in', 'W_B', 'W_C', 'D', 'W_out', 'b_out')}
    del _L1_attn_all

    def _L1_ffn_setup():
        import jax, jax.numpy as jnp
        import numpy as np
        D_MODEL = 256
        D_FF = 1024
        NUM_M = 2
        E_ROUTER = 8 * NUM_M - 1
        D_FF_R = D_FF // NUM_M
        TOP_K = NUM_M * 2 - 1
        B, T = (2, 512)

        def _expert_stack(x, W1, b1, W2, b2):
            h = jax.nn.gelu(jnp.einsum('btd,edf->ebtf', x, W1) + b1[:, None, None, :], approximate=False)
            return jnp.einsum('ebtf,efd->ebtd', h, W2) + b2[:, None, None, :]
        key = jax.random.key(seed)
        ks = jax.random.split(key, 12)
        s = lambda fan_in: 1.0 / np.sqrt(fan_in)
        x = jax.random.normal(ks[0], (B, T, D_MODEL), dtype=jnp.float32)
        sW1 = jax.random.uniform(ks[1], (1, D_MODEL, D_FF), jnp.float32, -s(D_MODEL), s(D_MODEL))
        sb1 = jax.random.uniform(ks[2], (1, D_FF), jnp.float32, -s(D_MODEL), s(D_MODEL))
        sW2 = jax.random.uniform(ks[3], (1, D_FF, D_MODEL), jnp.float32, -s(D_FF), s(D_FF))
        sb2 = jax.random.uniform(ks[4], (1, D_MODEL), jnp.float32, -s(D_FF), s(D_FF))
        rW1 = jax.random.uniform(ks[5], (E_ROUTER, D_MODEL, D_FF_R), jnp.float32, -s(D_MODEL), s(D_MODEL))
        rb1 = jax.random.uniform(ks[6], (E_ROUTER, D_FF_R), jnp.float32, -s(D_MODEL), s(D_MODEL))
        rW2 = jax.random.uniform(ks[7], (E_ROUTER, D_FF_R, D_MODEL), jnp.float32, -s(D_FF_R), s(D_FF_R))
        rb2 = jax.random.uniform(ks[8], (E_ROUTER, D_MODEL), jnp.float32, -s(D_FF_R), s(D_FF_R))
        gW = jax.random.uniform(ks[9], (D_MODEL, E_ROUTER), jnp.float32, -s(D_MODEL), s(D_MODEL))
        gb = jax.random.uniform(ks[10], (E_ROUTER,), jnp.float32, -s(D_MODEL), s(D_MODEL))
        return {'x': x, 'sW1': sW1, 'sb1': sb1, 'sW2': sW2, 'sb2': sb2, 'rW1': rW1, 'rb1': rb1, 'rW2': rW2, 'rb2': rb2, 'gW': gW, 'gb': gb}
    _L1_ffn_all = _L1_ffn_setup()
    _L1_ffn_in = {k: v for k, v in _L1_ffn_all.items() if k in ('sW1', 'sb1', 'sW2', 'sb2', 'rW1', 'rb1', 'rW2', 'rb2', 'gW', 'gb')}
    del _L1_ffn_all
    return {'x': x, 'L0_tok_emb0': _L0_tok_in['emb0'], 'L0_tok_emb1': _L0_tok_in['emb1'], 'L0_tok_emb2': _L0_tok_in['emb2'], 'L0_tok_emb3': _L0_tok_in['emb3'], 'L0_tok_proj1': _L0_tok_in['proj1'], 'L0_tok_proj2': _L0_tok_in['proj2'], 'L0_tok_proj3': _L0_tok_in['proj3'], 'L0_attn_q_w': _L0_attn_in['q_w'], 'L0_attn_k_w': _L0_attn_in['k_w'], 'L0_attn_v_w': _L0_attn_in['v_w'], 'L0_attn_b_w': _L0_attn_in['b_w'], 'L0_attn_q_cw': _L0_attn_in['q_cw'], 'L0_attn_k_cw': _L0_attn_in['k_cw'], 'L0_attn_v_cw': _L0_attn_in['v_cw'], 'L0_attn_fir_short_w': _L0_attn_in['fir_short_w'], 'L0_attn_fir_long_w': _L0_attn_in['fir_long_w'], 'L0_attn_mlp1_w': _L0_attn_in['mlp1_w'], 'L0_attn_mlp1_b': _L0_attn_in['mlp1_b'], 'L0_attn_mlp2_w': _L0_attn_in['mlp2_w'], 'L0_attn_mlp2_b': _L0_attn_in['mlp2_b'], 'L0_attn_logit_temp': _L0_attn_in['logit_temp'], 'L0_attn_conv_res_logit': _L0_attn_in['conv_res_logit'], 'L0_attn_norm_w': _L0_attn_in['norm_w'], 'L0_attn_o_w': _L0_attn_in['o_w'], 'L0_ffn_gamma': _L0_ffn_in['gamma'], 'L0_ffn_wq': _L0_ffn_in['wq'], 'L0_ffn_keys': _L0_ffn_in['keys'], 'L0_ffn_table_down': _L0_ffn_in['table_down'], 'L0_ffn_table_up': _L0_ffn_in['table_up'], 'L1_attn_W_in': _L1_attn_in['W_in'], 'L1_attn_b_in': _L1_attn_in['b_in'], 'L1_attn_W_B': _L1_attn_in['W_B'], 'L1_attn_W_C': _L1_attn_in['W_C'], 'L1_attn_D': _L1_attn_in['D'], 'L1_attn_W_out': _L1_attn_in['W_out'], 'L1_attn_b_out': _L1_attn_in['b_out'], 'L1_ffn_sW1': _L1_ffn_in['sW1'], 'L1_ffn_sb1': _L1_ffn_in['sb1'], 'L1_ffn_sW2': _L1_ffn_in['sW2'], 'L1_ffn_sb2': _L1_ffn_in['sb2'], 'L1_ffn_rW1': _L1_ffn_in['rW1'], 'L1_ffn_rb1': _L1_ffn_in['rb1'], 'L1_ffn_rW2': _L1_ffn_in['rW2'], 'L1_ffn_rb2': _L1_ffn_in['rb2'], 'L1_ffn_gW': _L1_ffn_in['gW'], 'L1_ffn_gb': _L1_ffn_in['gb']}

def reference(x, L0_tok_emb0, L0_tok_emb1, L0_tok_emb2, L0_tok_emb3, L0_tok_proj1, L0_tok_proj2, L0_tok_proj3, L0_attn_q_w, L0_attn_k_w, L0_attn_v_w, L0_attn_b_w, L0_attn_q_cw, L0_attn_k_cw, L0_attn_v_cw, L0_attn_fir_short_w, L0_attn_fir_long_w, L0_attn_mlp1_w, L0_attn_mlp1_b, L0_attn_mlp2_w, L0_attn_mlp2_b, L0_attn_logit_temp, L0_attn_conv_res_logit, L0_attn_norm_w, L0_attn_o_w, L0_ffn_gamma, L0_ffn_wq, L0_ffn_keys, L0_ffn_table_down, L0_ffn_table_up, L1_attn_W_in, L1_attn_b_in, L1_attn_W_B, L1_attn_W_C, L1_attn_D, L1_attn_W_out, L1_attn_b_out, L1_ffn_sW1, L1_ffn_sb1, L1_ffn_sW2, L1_ffn_sb2, L1_ffn_rW1, L1_ffn_rb1, L1_ffn_rW2, L1_ffn_rb2, L1_ffn_gW, L1_ffn_gb):
    import jax
    import jax.numpy as jnp

    def _L0_tok_ref(tokens, emb0, emb1, emb2, emb3, proj1, proj2, proj3):
        import jax, jax.numpy as jnp
        import numpy as np
        N_TOKEN = 267735
        CUTOFFS = [0, 5000, 10000, 50000, N_TOKEN]
        D_PROJ = 256
        D_EMBED = 256
        DIV = 4
        B, S = (8, 512)
        embs = [emb0, emb1, emb2, emb3]
        projs = [None, proj1, proj2, proj3]
        out = jnp.zeros(tokens.shape + (D_PROJ,), dtype=emb0.dtype)
        for i in range(4):
            l, r = (CUTOFFS[i], CUTOFFS[i + 1])
            mask = (tokens >= l) & (tokens < r)
            idx = jnp.clip(tokens - l, 0, r - l - 1)
            x = embs[i][idx]
            if projs[i] is not None:
                x = x @ projs[i]
            out = out + jnp.where(mask[..., None], x, jnp.zeros((), dtype=x.dtype))
        emb_scale = jnp.sqrt(jnp.asarray(D_PROJ, dtype=out.dtype))
        return out * emb_scale

    def _L0_attn_ref(hidden_states, q_w, k_w, v_w, b_w, q_cw, k_cw, v_cw, fir_short_w, fir_long_w, mlp1_w, mlp1_b, mlp2_w, mlp2_b, logit_temp, conv_res_logit, norm_w, o_w):
        import jax, jax.numpy as jnp
        import numpy as np
        import math
        B, L, D = (2, 1024, 256)
        H, DK, DV = (4, 64, 64)
        CHUNK = 32
        PROB_FLOOR = 0.02

        def _l2norm(x, eps=1e-06):
            return x * jax.lax.rsqrt(jnp.sum(x * x, -1, keepdims=True) + eps)

        def _silu(x):
            return x * jax.nn.sigmoid(x)

        def _short_conv(x, w):
            K = w.shape[-1]
            xp = jnp.pad(x, ((0, 0), (K - 1, 0), (0, 0)))
            y = sum((xp[:, j:j + x.shape[1], :] * w[:, j] for j in range(K)))
            return _silu(y)

        def _fir_conv(x, filt):
            b, l, h, d = x.shape
            K = filt.shape[-1]
            xf = jnp.pad(x.reshape(b, l, h * d).transpose(0, 2, 1), ((0, 0), (0, 0), (K - 1, 0)))
            w = filt.reshape(h * d, 1, K)
            y = jax.lax.conv_general_dilated(xf, w, (1,), 'VALID', dimension_numbers=('NCH', 'OIH', 'NCH'), feature_group_count=h * d)
            return y.transpose(0, 2, 1).reshape(b, l, h, d)

        def _delta_rule_chunkwise(q, k, v, beta, chunk=CHUNK):
            b, h, Lq, dk = q.shape
            dv = v.shape[-1]
            n = Lq // chunk
            q = _l2norm(q)
            k = _l2norm(k)
            v = v * beta[..., None]
            kb = k * beta[..., None]
            rs = lambda t: t.reshape(b, h, n, chunk, t.shape[-1])
            qc, kc, vc, kbc = (rs(q), rs(k), rs(v), rs(kb))
            strict_lower = jnp.tril(jnp.ones((chunk, chunk), bool), -1)
            M = jnp.where(strict_lower, jnp.einsum('bhncd,bhnmd->bhncm', kbc, kc), 0.0)
            eye = jnp.eye(chunk, dtype=q.dtype)
            T = jax.scipy.linalg.solve_triangular(eye + M, jnp.broadcast_to(eye, M.shape), lower=True, unit_diagonal=True)
            u = T @ vc
            w = T @ kbc
            incl_lower = jnp.tril(jnp.ones((chunk, chunk), bool), 0)

            def step(S, xs):
                q_i, k_i, u_i, w_i = xs
                attn = jnp.where(incl_lower, q_i @ k_i.swapaxes(-1, -2), 0.0)
                u_adj = u_i - w_i @ S
                out_i = q_i @ S + attn @ u_adj
                S = S + k_i.swapaxes(-1, -2) @ u_adj
                return (S, out_i)
            S0 = jnp.zeros((b, h, dk, dv), q.dtype)
            xs = tuple((jnp.moveaxis(t, 2, 0) for t in (qc, kc, u, w)))
            S, out = jax.lax.scan(step, S0, xs)
            out = jnp.moveaxis(out, 0, 2).reshape(b, h, Lq, dv)
            return (out, S)

        def _rmsnorm(x, w, eps=1e-05):
            return x * jax.lax.rsqrt(jnp.mean(x * x, -1, keepdims=True) + eps) * w

        def _per_head_stats(x):
            mean = jnp.mean(x, -1, keepdims=True)
            var = jnp.var(x, -1, keepdims=True)
            am = jnp.mean(jnp.abs(x), -1, keepdims=True)
            l2 = jnp.sqrt(jnp.sum(x * x, -1, keepdims=True))
            return jnp.concatenate([mean, var, am, l2], -1)

        def _forward(hidden_states, q_w, k_w, v_w, b_w, q_cw, k_cw, v_cw, fir_short_w, fir_long_w, mlp1_w, mlp1_b, mlp2_w, mlp2_b, logit_temp, conv_res_logit, norm_w, o_w):
            b, l, _ = hidden_states.shape
            q_in = _short_conv(hidden_states @ q_w.T, q_cw)
            k_in = _short_conv(hidden_states @ k_w.T, k_cw)
            v_in = _short_conv(hidden_states @ v_w.T, v_cw)
            q = q_in.reshape(b, l, H, DK)
            k = k_in.reshape(b, l, H, DK)
            v_direct = v_in.reshape(b, l, H, DV)
            beta = jnp.maximum(jax.nn.sigmoid(hidden_states @ b_w.T), 1e-06)
            delta_out, _S = _delta_rule_chunkwise(q.transpose(0, 2, 1, 3), k.transpose(0, 2, 1, 3), v_direct.transpose(0, 2, 1, 3), beta.transpose(0, 2, 1))
            delta_out = delta_out.transpose(0, 2, 1, 3)
            local_short = _fir_conv(v_direct, fir_short_w)
            local_long = _fir_conv(v_direct, fir_long_w)
            stats = jnp.concatenate([_per_head_stats(local_short), _per_head_stats(local_long), _per_head_stats(delta_out), _per_head_stats(v_direct)], -1)
            hs_exp = jnp.broadcast_to(hidden_states[:, :, None, :], (b, l, H, hidden_states.shape[-1]))
            gate_in = jnp.concatenate([hs_exp, stats], -1)
            h1 = jax.nn.gelu(gate_in @ mlp1_w.T + mlp1_b)
            logits = h1 @ mlp2_w.T + mlp2_b
            temp = jax.nn.softplus(logit_temp)
            p = jax.nn.softmax(logits / temp, -1)
            p = jnp.maximum(p, PROB_FLOOR)
            p = p / jnp.sum(p, -1, keepdims=True)
            o = p[..., 0:1] * local_short + p[..., 1:2] * local_long + p[..., 2:3] * delta_out + p[..., 3:4] * v_direct
            o = o + jax.nn.sigmoid(conv_res_logit)[None, None, :, None] * local_short
            o = _rmsnorm(o, norm_w)
            o = o.reshape(b, l, H * DV) @ o_w.T
            return o
        return _forward(hidden_states, q_w, k_w, v_w, b_w, q_cw, k_cw, v_cw, fir_short_w, fir_long_w, mlp1_w, mlp1_b, mlp2_w, mlp2_b, logit_temp, conv_res_logit, norm_w, o_w)

    def _L0_ffn_ref(x, gamma, wq, keys, table_down, table_up):
        import jax, jax.numpy as jnp
        import numpy as np
        DIM = 256
        HEADS = 8
        NUM_EXPERTS = 16384
        NUM_KEYS = 64
        DIM_KEY = 128
        TOPK = 16

        def _rmsnorm(v, g):
            scale = jnp.sqrt(jnp.asarray(v.shape[-1], v.dtype))
            n = jnp.maximum(jnp.linalg.norm(v, axis=-1, keepdims=True), 1e-12)
            return v / n * g * scale
        B, N, D = x.shape
        xn = _rmsnorm(x, gamma)
        gate = xn
        q = gate @ wq.T
        q = q.reshape(B, N, 2, HEADS, DIM_KEY).transpose(2, 0, 1, 3, 4)
        sim = jnp.einsum('pbnhd,hkpd->pbnhk', q, keys)
        sx, ix = jax.lax.top_k(sim[0], TOPK)
        sy, iy = jax.lax.top_k(sim[1], TOPK)
        all_scores = (sx[..., :, None] + sy[..., None, :]).reshape(B, N, HEADS, TOPK * TOPK)
        all_indices = (ix[..., :, None] * NUM_KEYS + iy[..., None, :]).reshape(B, N, HEADS, TOPK * TOPK)
        scores, pk = jax.lax.top_k(all_scores, TOPK)
        indices = jnp.take_along_axis(all_indices, pk, axis=-1)
        wd = table_down[indices]
        wu = table_up[indices]
        h = jnp.einsum('bnd,bnhkd->bnhk', xn, wd)
        h = jax.nn.gelu(h, approximate=False) * jax.nn.softmax(scores, axis=-1)
        out = jnp.einsum('bnhk,bnhkd->bnd', h, wu)
        return out

    def _L1_attn_ref(x, W_in, b_in, W_B, W_C, D, W_out, b_out):
        import jax, jax.numpy as jnp
        import numpy as np
        BATCH, T, D_MODEL, D_STATE, EXPAND = (4, 1024, 256, 16, 2)
        D_INNER = D_MODEL * EXPAND
        xz = jnp.einsum('btd,ed->bte', x, W_in) + b_in
        x_proj, z = jnp.split(xz, 2, axis=-1)
        x_proj = jax.nn.silu(x_proj)
        b = jnp.einsum('bte,se->bts', x_proj, W_B)

        def step(h, b_t):
            h = 0.9 * h + 0.1 * b_t
            return (h, h)
        h0 = jnp.zeros((x.shape[0], W_B.shape[0]), x.dtype)
        _, hs = jax.lax.scan(step, h0, jnp.swapaxes(b, 0, 1))
        hs = jnp.swapaxes(hs, 0, 1)
        c = jnp.einsum('bts,es->bte', hs, W_C)
        y = c + D * x_proj
        y = y * jax.nn.silu(z)
        return jnp.einsum('bte,de->btd', y, W_out) + b_out

    def _L1_ffn_ref(x, sW1, sb1, sW2, sb2, rW1, rb1, rW2, rb2, gW, gb):
        import jax, jax.numpy as jnp
        import numpy as np
        D_MODEL = 256
        D_FF = 1024
        NUM_M = 2
        E_ROUTER = 8 * NUM_M - 1
        D_FF_R = D_FF // NUM_M
        TOP_K = NUM_M * 2 - 1
        B, T = (2, 512)

        def _expert_stack(x, W1, b1, W2, b2):
            h = jax.nn.gelu(jnp.einsum('btd,edf->ebtf', x, W1) + b1[:, None, None, :], approximate=False)
            return jnp.einsum('ebtf,efd->ebtd', h, W2) + b2[:, None, None, :]
        shared_enc = _expert_stack(x, sW1, sb1, sW2, sb2).sum(0)
        weights = jax.nn.softmax(x @ gW + gb, axis=-1)
        topv, topi = jax.lax.top_k(weights, TOP_K)
        gated = (jax.nn.one_hot(topi, E_ROUTER, dtype=weights.dtype) * topv[..., None]).sum(axis=-2)
        router_out = _expert_stack(x, rW1, rb1, rW2, rb2)
        router_enc = jnp.einsum('ebtd,bte->btd', router_out, gated)
        return shared_enc + router_enc + x
    h = _L0_tok_ref(x, L0_tok_emb0, L0_tok_emb1, L0_tok_emb2, L0_tok_emb3, L0_tok_proj1, L0_tok_proj2, L0_tok_proj3)
    h = h + _L0_attn_ref(_layernorm(h, axis=-1), L0_attn_q_w, L0_attn_k_w, L0_attn_v_w, L0_attn_b_w, L0_attn_q_cw, L0_attn_k_cw, L0_attn_v_cw, L0_attn_fir_short_w, L0_attn_fir_long_w, L0_attn_mlp1_w, L0_attn_mlp1_b, L0_attn_mlp2_w, L0_attn_mlp2_b, L0_attn_logit_temp, L0_attn_conv_res_logit, L0_attn_norm_w, L0_attn_o_w)
    h = h + _L0_ffn_ref(_layernorm(h, axis=-1), L0_ffn_gamma, L0_ffn_wq, L0_ffn_keys, L0_ffn_table_down, L0_ffn_table_up)
    h = h + _L1_attn_ref(_layernorm(h, axis=-1), L1_attn_W_in, L1_attn_b_in, L1_attn_W_B, L1_attn_W_C, L1_attn_D, L1_attn_W_out, L1_attn_b_out)
    h = h + _L1_ffn_ref(_layernorm(h, axis=-1), L1_ffn_sW1, L1_ffn_sb1, L1_ffn_sW2, L1_ffn_sb2, L1_ffn_rW1, L1_ffn_rb1, L1_ffn_rW2, L1_ffn_rb2, L1_ffn_gW, L1_ffn_gb)
    return h

_drawn_inputs = setup_inputs


def setup_inputs(seed=0):
    import zlib

    import numpy as np

    out = dict(_drawn_inputs(seed))
    spreads = {'L0_attn_mlp1_b': (0.0, 0.8),
     'L0_attn_conv_res_logit': (-2.0, 0.6),
     'L0_attn_norm_w': (1.0, 0.2),
     'L0_ffn_gamma': (1.0, 0.6),
     'L1_attn_b_in': (0.0, 0.403),
     'L1_attn_D': (1.0, 0.6),
     'L1_attn_b_out': (0.0, 0.1)}
    factors = {'L0_attn_b_w': 8.0,
     'L0_attn_fir_short_w': 8.0,
     'L0_attn_fir_long_w': 8.0,
     'L0_attn_mlp1_w': 8.0,
     'L0_attn_mlp2_w': 8.0,
     'L0_ffn_wq': 6.365,
     'L0_ffn_keys': 6.403,
     'L0_ffn_table_down': 6.452,
     'L0_ffn_table_up': 6.253,
     'L1_attn_W_B': 8.0,
     'L1_attn_W_C': 8.0,
     'L1_ffn_sb1': 5.911,
     'L1_ffn_sb2': 4.145,
     'L1_ffn_rb1': 27.981,
     'L1_ffn_rb2': 8.0,
     'L1_ffn_gb': 7.457}
    for name, (base, spread) in spreads.items():
        noise = np.random.default_rng([zlib.crc32(name.encode()), seed]).standard_normal(out[name].shape)
        drawn = base * np.exp(spread * noise) if base else spread * noise
        out[name] = jnp.asarray(drawn.astype(out[name].dtype))
    for name, factor in factors.items():
        out[name] = (out[name] * factor).astype(out[name].dtype)
    return out
```

```python
from contextlib import ExitStack

import numpy as np

import concourse.bass as bass
from concourse import mybir

F32 = mybir.dt.float32
BF16 = mybir.dt.bfloat16
I32 = mybir.dt.int32
U32 = mybir.dt.uint32
ALU = mybir.AluOpType
ACT = mybir.ActivationFunctionType
AX_X = mybir.AxisListType.X

P = 128
BATCH, T = 4, 512
NT = T // P
D = 256
KD = D // P
CUTOFFS = [0, 5000, 10000, 50000, 267735]
EMB = [D // 4**i for i in range(4)]
EMB_AT = [sum(EMB[:i]) for i in range(4)]
EMB_ALL = sum(EMB)
EMB_LOW = EMB_ALL - D
H, DH = 4, 64
TAPS, SHORT, LONG = 4, 5, 64
PH, NK, TOPK = 8, 64, 16
NX = NK * NK
XC = NX // P
YC = NK // 2
ROWLEN = [TOPK // (i + 1) for i in range(TOPK)]
ROWAT = [sum(ROWLEN[:i]) for i in range(TOPK)]
PAIRS = sum(ROWLEN)
TB = 32
DI, DS = 512, 16
NE, FF = 15, 512
NU = NE + 2
FC = FF // P
LEVELS = 7
LOWEST = -3.0e38
HEAD_ORDER = [0, 2, 1, 3]


class Chain:

    def __init__(self, eng, sem):
        self.eng, self.sem, self.n = eng, sem, 0

    def step(self, ins):
        ins.then_inc(self.sem, 1)
        self.n += 1

    def settle(self):
        self.eng.wait_ge(self.sem, self.n)

    def link(self, ins):
        self.step(ins)
        self.settle()


class Arena:

    def __init__(self, tensor, at, end):
        self.tensor, self.at, self.end = tensor, at, end

    def take(self, *shape, dtype=F32, parts=P):
        n = int(np.prod(shape))
        words = n if dtype != BF16 else n // 2
        view = self.tensor[0:parts, self.at:self.at + words]
        self.at += words
        assert self.at <= self.end, (self.at, self.end)
        if dtype != F32:
            view = view.bitcast(dtype)
        names = "abcde"[:len(shape)]
        if len(shape) > 1:
            sizes = {c: s for c, s in zip(names, shape)}
            view = view.rearrange(f"p ({' '.join(names)}) -> p {' '.join(names)}", **sizes)
        return view


def spread(ap, axis, n):
    shape = list(ap.shape)
    shape.insert(axis, n)
    return ap.unsqueeze(axis).broadcast_to(shape)


def build(nc, ins, out, stages="EAPSM"):
    ctx = ExitStack()
    with ctx:
        def sb(name, shape, dt=F32):
            return ctx.enter_context(nc.sbuf_tensor(name, shape, dt))

        def sem(name):
            return ctx.enter_context(nc.semaphore(name))

        B = [ctx.enter_context(nc.psum_tensor(f"bank{i}", [P, 512], F32)) for i in range(8)]

        w_qkv = sb("w_qkv", [P, 3, KD, D])
        w_beta = sb("w_beta", [P, KD, H])
        conv_w = sb("conv_w", [P, 3 * KD, TAPS])
        short_w = sb("short_w", [P, KD, SHORT])
        mlp1_a = sb("mlp1_a", [P, KD, D])
        mlp1_s = sb("mlp1_s", [H * 16, H, D])
        mlp1_b = sb("mlp1_b", [P, KD])
        mlp2_w = sb("mlp2_w", [P, KD, 4])
        mlp2_b = sb("mlp2_b", [P, 4])
        temp = sb("temp", [P, 4])
        res_gate = sb("res_gate", [P, H])
        norm_w = sb("norm_w", [P, DH])
        o_w = sb("o_w", [P, KD, D])
        proj = sb("proj", [EMB_LOW, D])
        gamma = sb("gamma", [P, D])
        w_sim = sb("w_sim", [P, KD, 2 * PH * NK])
        w_in = sb("w_in", [P, KD, 2 * DI])
        b_in = sb("b_in", [P, 2 * DI // P])
        w_B = sb("w_B", [P, DI // P, DS])
        w_C = sb("w_C", [DS, DI])
        skip_D = sb("skip_D", [P, DI // P])
        w_out = sb("w_out", [P, DI // P, D])
        b_out = sb("b_out", [P, D])
        gate_w = sb("gate_w", [P, KD, NE])
        gate_b = sb("gate_b", [P, NE])
        b1_all = sb("b1_all", [P, NU, FC])
        b2_all = sb("b2_all", [NE + 1, D])
        ident = sb("ident", [P, P])
        level_mask = sb("level_mask", [P, LEVELS, P])
        causal = sb("causal", [P, P])
        flips = sb("flips", [P, 3, P])
        iota_x = sb("iota_x", [P, P, TB], BF16)
        iota_y = sb("iota_y", [P, YC, TB], BF16)
        iota16 = sb("iota16", [P, TOPK])
        row_at = sb("row_at", [P, TOPK])
        row_len = sb("row_len", [P, TOPK])
        decay = sb("decay", [DS, T])

        hid = sb("hid", [P, NT, D])
        xn = sb("xn", [P, NT, D])
        xT = sb("xT", [P, KD, T])
        ids = sb("ids", [P, NT], I32)
        ids_f = sb("ids_f", [P, NT])
        id_low = sb("id_low", [P, 4, NT])
        id_ge = sb("id_ge", [P, 4, NT])
        id_mask = sb("id_mask", [P, 4, NT])
        id_row = sb("id_row", [P, 4, NT], U32)
        ln_part = sb("ln_part", [P, NT, 6])
        ln_mv = sb("ln_mv", [P, NT, 2])
        ln_ve = sb("ln_ve", [P, NT])
        ln_sd = sb("ln_sd", [P, NT])
        ln_r = sb("ln_r", [P, NT])
        moe_w1 = sb("moe_w1", [P, 2, KD, FF])
        moe_w2 = sb("moe_w2", [P, 2, FC, D])
        moe_h = sb("moe_h", [P, 2, FC, T])

        ARENA = 26500
        arena_t = sb("arena", [P, ARENA])

        loads = sem("loads")
        made = sem("made")
        iter_done = sem("iter_done")
        go_on = sem("go_on")
        names = [
            "dve_step", "act_step", "pool_step",
            "ids_in", "rows_ready", "low_ready", "low_ps", "lowT_ready", "proj_ps",
            "ln_var", "ln_std", "ln_out", "turn_ps", "turn_sb",
            "toep_in0", "toep_in1", 
            "qkv_ps", "pre_ready", "conv_ready", "silu_ready", "beta_ps", "beta_ready", "tok_ps", "tok_ready",
            "ss_ready", "ss_root", "unit_ready", "unitT_ps", "unitT_ready", "window_ps", "window_ready",
            "short_ready", "short_ps", "short_tok", "fir_ps", "fir_ready",
            "gram_ps", "gram_ready", "lm_ready", "u0_ready", "t0_ps", "t0_ready", "p_ps", "p_ready",
            "d_ps", "tu_ready", "w_ps", "w_ready", "attn_ps", "attn_ready", "ua_ps", "ua_ready",
            "do_ps", "do_ready", "ds_ps", "ds_ready",
            "l2_ready", "l2_root", "stat_ready", "stat_ps", "statT_ready", "h1_ps", "h1_ready", "logit_ps",
            "lg_ready", "lg_exp", "mix_ss", "mix_root", "mix_ready", "o_ps", "hid_attn",
            "xss_ready", "xss_root", "sim_ps", "sim_ready", "sim_used", "score_ready", "score_exp", "entry_ready",
            "entry_ps", "entry_T", "hot_ready", "cell_ps", "cell_ready",
            "tab_in0", "tab_in1", "tab_used", "down_ps", "down_act", "down_ready", "up_ps", "hid_peer",
            "xz_ps", "xz_ready", "state_ps", "drive_ready", "state_ready", "c_ps", "y_ready", "so_ps", "hid_ssm",
            "gl_ps", "gl_ready", "gl_exp", "gate_ready", "gate_ps", "gateT_ready", "ew_in0", "ew_in1",
            "e1_ps", "e1_ready", "e2_ps", "e2_used", "bias_ps", "hid_out", "stored",
        ]
        S = {n: sem(n) for n in names}
        rows_in = sem("rows_in")


        toep_in, tab_in, ew_in = (S["toep_in0"], S["toep_in1"]), (S["tab_in0"], S["tab_in1"]), (S["ew_in0"], S["ew_in1"])

        block = ctx.enter_context(nc.Block())

        a = Arena(arena_t, 0, ARENA)
        feats = a.take(NT, 4, D)
        win = a.take(2 * NT, D)
        vpad = a.take(KD, T + SHORT - 1)
        qk_tok = a.take(2, NT, D)
        kb = a.take(NT, D)
        vb = a.take(NT, D)
        unitT = a.take(3, KD, T)
        neg_wT = a.take(NT, KD, P)
        u_adj = a.take(D)
        state = a.take(KD, DH)
        beta = a.take(NT * H)
        ss = a.take(2 * NT * H)
        ss_sd = a.take(2 * NT * H)
        unit = a.take(2 * NT * H)
        stats = a.take(NT, H, 4, 4)
        st_sum, st_abs, st_css, st_mean2, st_l2 = (a.take(NT, 4, H) for _ in range(5))
        stats_mean = a.take(NT, 4, H)
        statT = a.take(T, parts=H * 16)
        lg, lg_e, lg_p = (a.take(NT, H, 4) for _ in range(3))
        lg_m, lg_s, lg_r = (a.take(NT, H) for _ in range(3))
        attn_m = a.take(2, H, P)
        scratch = a.at

        a = Arena(arena_t, scratch, ARENA)
        pre = a.take(3 * KD, T + TAPS - 1)
        conv = a.take(3 * KD, T)
        embed = Arena(arena_t, 0, ARENA)
        rows = embed.take(NT, EMB_ALL)
        low = embed.take(NT, EMB_LOW)
        lowT = embed.take(T, parts=EMB_LOW)
        sq = Arena(arena_t, scratch, ARENA).take(2, NT, D)
        a = Arena(arena_t, scratch, ARENA)
        toep = a.take(2, 64, 64)
        a = Arena(arena_t, scratch, ARENA)
        T_m = a.take(NT, H, P)
        U_m = a.take(NT, H, P)
        M_T = a.take(NT, H, P)
        L_T = a.take(NT, H, P)
        P_m = win[:, :, :].rearrange("p w c -> p (w c)").rearrange("p (t h c) -> p t h c", t=NT, h=H)
        a = Arena(arena_t, scratch, ARENA)
        cent = a.take(NT, 4 * H, DH)
        h1 = a.take(2, KD, T)
        short_T = a.take(KD, T)
        mix = cent[:, :, :, :].rearrange("p t (k h) d -> p t k h d", k=4)
        o_tok = h1[:, :, :, :].rearrange("p a b c -> p (a b c)")[:, 0:NT * D].rearrange("p (t c) -> p t c", t=NT)
        o_sq = h1[:, :, :, :].rearrange("p a b c -> p (a b c)")[:, NT * D:2 * NT * D].rearrange("p (t c) -> p t c", t=NT)
        oT = short_T

        a = Arena(arena_t, 0, ARENA)
        grid = a.take(XC, T)
        entT_x = a.take(T, dtype=BF16)
        entT_y = a.take(T, dtype=BF16)
        entT_w = a.take(3, T, dtype=BF16)
        w_rest, w_rest2 = grid[:, XC - 2, :], grid[:, XC - 1, :]
        hot_at = a.at
        hot_x = a.take(P, TB, dtype=BF16)
        hot_y = a.take(YC, TB, dtype=BF16)
        hot_w = a.take(3, YC, TB, dtype=BF16)
        hot_x2 = a.take(P, TB, dtype=BF16)
        hot_y2 = a.take(YC, TB, dtype=BF16)
        hot_w2 = a.take(3, YC, TB, dtype=BF16)
        hots = [(hot_x, hot_y, hot_w), (hot_x2, hot_y2, hot_w2)]
        a = Arena(arena_t, hot_at, ARENA)
        tab_d = a.take(2, 2, KD, P)
        tab_u = a.take(2, 2, D)
        down = a.take(2, T)
        a = Arena(arena_t, 0, hot_at)
        sim = a.take(2, 2 * PH, NK)
        val = a.take(2, NT, PH, TOPK)
        key = a.take(2, NT, PH, TOPK, dtype=U32)
        key_f = a.take(2, NT, PH, TOPK)
        key_d = a.take(2, NT, PH, TOPK)
        cand = a.take(NT * PH, PAIRS)
        top = a.take(NT * PH, TOPK)
        pos = a.take(NT * PH, TOPK, dtype=U32)
        pos_f = a.take(NT * PH, TOPK)
        e_w = a.take(NT * PH, TOPK)
        e_x, e_y = a.take(NT * PH, TOPK), a.take(NT * PH, TOPK)
        e_s = a.take(NT * PH)
        e_r = a.take(NT * PH)
        e_i = a.take(NT * PH, TOPK, dtype=I32)
        x_sq, x_sd, x_r = a.take(NT), a.take(NT), a.take(NT)
        look_a = Arena(arena_t, hot_at, ARENA).take(PH, TOPK, TOPK)
        look_b = Arena(arena_t, hot_at + PH * TOPK * TOPK, ARENA).take(PH, TOPK, TOPK)
        xx = Arena(arena_t, hot_at, ARENA).take(NT, D)

        a = Arena(arena_t, 0, ARENA)
        xz = a.take(2 * DI // P, T)
        y = a.take(DI // P, T)
        drive = a.take(T, parts=DS)
        states = a.take(T, parts=DS)

        a = Arena(arena_t, 0, ARENA)
        gl = a.take(NT, NE)
        gm = a.take(NT)
        ge = a.take(NT, NE)
        gs, gr = a.take(NT), a.take(NT)
        garr = a.take(NT, NE + 5)
        gtop = a.take(NT, 8)
        gtake = a.take(NT, 8)
        gated = a.take(NT, NE + 1)
        gatedT = a.take(T, parts=NE + 1)

        n_loads = [0]

        def load(eng, dst, src):
            eng.dma_start(dst, src).then_inc(loads, 16)
            n_loads[0] += 16

        def setup_sync(sp):
            for i, n in enumerate(("q_wT", "k_wT", "v_wT")):
                load(sp, w_qkv[:, i], ins[n].rearrange("(k p) n -> p k n", p=P))
            load(sp, w_beta[:, :, :], ins["b_wT"].rearrange("(k p) n -> p k n", p=P))
            for i, n in enumerate(("q_cw", "k_cw", "v_cw")):
                load(sp, conv_w[:, KD * i:KD * (i + 1), :], ins[n].rearrange("(k p) n -> p k n", p=P))
            load(sp, short_w[:, :, :], ins["fir_short"].rearrange("(k p) n -> p k n", p=P))
            load(sp, mlp1_a[:, :, :], ins["mlp1_aT"].rearrange("(k p) n -> p k n", p=P))
            load(sp, mlp1_s[:, :, :], ins["mlp1_sT"].rearrange("h p n -> p h n"))
            load(sp, mlp1_b[:, :], ins["mlp1_b"])
            load(sp, mlp2_w[:, :, :], ins["mlp2_wT"].rearrange("(k p) n -> p k n", p=P))
            load(sp, mlp2_b[:, :], ins["mlp2_b"].partition_broadcast(P))
            load(sp, temp[:, 0:1], ins["logit_temp"].partition_broadcast(P))
            load(sp, res_gate[:, :], ins["conv_res"].partition_broadcast(P))
            load(sp, norm_w[:, :], ins["norm_w"].partition_broadcast(P))
            load(sp, o_w[:, :, :], ins["o_wT"].rearrange("(k p) n -> p k n", p=P))
            load(sp, proj[:, :], ins["proj"])
            load(sp, gamma[:, :], ins["gamma"].partition_broadcast(P))
            load(sp, w_in[:, :, :], ins["W_inT"].rearrange("(k p) n -> p k n", p=P))
            load(sp, b_in[:, :], ins["b_in"])
            load(sp, w_B[:, :, :], ins["W_BT"].rearrange("(k p) n -> p k n", p=P))
            load(sp, w_C[:, :], ins["W_CT"])
            load(sp, skip_D[:, :], ins["D"])
            load(sp, w_out[:, :, :], ins["W_outT"].rearrange("(k p) n -> p k n", p=P))
            load(sp, b_out[:, :], ins["b_out"].partition_broadcast(P))
            load(sp, gate_w[:, :, :], ins["gW"].rearrange("(k p) n -> p k n", p=P))
            load(sp, gate_b[:, :], ins["gb"].partition_broadcast(P))
            load(sp, b1_all[:, :, :], ins["b1"])
            load(sp, b2_all[:, :], ins["b2"])
            load(sp, ident[:, :], ins["c_ident"])
            load(sp, level_mask[:, :, :], ins["c_levels"].rearrange("l p n -> p l n"))
            load(sp, causal[:, :], ins["c_causal"])
            load(sp, flips[:, :, :], ins["c_flips"])
            load(sp, iota, ins["c_iota"].partition_broadcast(P))
            load(sp, iota16[:, :], ins["c_rows"][0].partition_broadcast(P))
            load(sp, row_at[:, :], ins["c_rows"][1].partition_broadcast(P))
            load(sp, row_len[:, :], ins["c_rows"][2].partition_broadcast(P))
            load(sp, wq_sb, ins["wq"].rearrange("(c p) n -> p c n", p=P))
            load(sp, keys_sb, ins["keysT"].rearrange("c p n -> p c n"))

        a = Arena(arena_t, 0, ARENA)
        wq_sb = a.take(2 * PH, D)
        keys_sb = a.take(2 * PH, NK)
        iota = a.take(P)

        def setup_tensor(pe):
            pe.wait_ge(loads, n_loads[0])
            for c in range(2 * PH):
                for k in range(KD):
                    last = nc.tensor.matmul(B[2 * k + c // PH][:, (c % PH) * NK:(c % PH + 1) * NK],
                                            wq_sb[:, c, k * P:(k + 1) * P], keys_sb[:, c, :],
                                            start=True, stop=True)
            last.then_inc(made, 1)

        def setup_scalar(act):
            act.wait_ge(loads, n_loads[0])
            act.wait_ge(made, 1)
            for k in range(KD):
                for half in range(2):
                    nc.scalar.copy(w_sim[:, k, half * 512:(half + 1) * 512], B[2 * k + half][:, :]).then_inc(made, 1)
            nc.scalar.activation(temp[:, 1:2], temp[:, 0:1], ACT.Abs).then_inc(made, 1)
            act.wait_ge(made, 6)
            nc.scalar.activation(temp[:, 2:3], temp[:, 1:2], ACT.Exp, scale=-1.0).then_inc(made, 1)
            act.wait_ge(made, 7)
            nc.scalar.activation(temp[:, 3:4], temp[:, 2:3], ACT.Ln, bias=1.0).then_inc(made, 1)
            nc.scalar.activation(res_gate[:, :], res_gate[:, :], ACT.Sigmoid).then_inc(made, 1)

        def setup_vector(dve):
            dve.wait_ge(loads, n_loads[0])
            dve.wait_ge(made, 9)
            nc.vector.scalar_tensor_tensor(temp[:, 1:2], temp[:, 0:1], 0.0, temp[:, 3:4],
                                           ALU.max, ALU.add).then_inc(made, 1)
            dve.wait_ge(made, 10)
            nc.vector.reciprocal(temp[:, 0:1], temp[:, 1:2]).then_inc(made, 1)
            nc.vector.memset(decay[:, :], 0.9).then_inc(made, 1)
            nc.vector.tensor_copy(iota_x[:, :, :], spread(iota, 2, TB)).then_inc(made, 1)
            nc.vector.tensor_copy(iota_y[:, :, :], spread(iota[:, 0:YC], 2, TB)).then_inc(made, 1)

        MADE = 14
        inv_temp = temp[:, 0:1]

        def embed_sync(sp, b):
            sp.dma_start(ids[:, :], ins["x"][bass.ds(b, 1)].rearrange("a p t -> p (a t)")).then_inc(S["ids_in"], 16)

        def embed_vector(dve, v, b):
            dve.wait_ge(S["ids_in"], 16)
            v.link(nc.vector.tensor_copy(ids_f[:, :], ids[:, :]))
            for i in range(4):
                lo, hi = CUTOFFS[i], CUTOFFS[i + 1]
                v.step(nc.vector.tensor_scalar(id_low[:, i], ids_f[:, :], float(-lo), 0.0, ALU.add, ALU.max))
                v.step(nc.vector.tensor_scalar(id_ge[:, i], ids_f[:, :], float(lo), None, ALU.is_ge))
            v.settle()
            for i in range(4):
                lo, hi = CUTOFFS[i], CUTOFFS[i + 1]
                v.step(nc.vector.scalar_tensor_tensor(id_mask[:, i], ids_f[:, :], float(hi), id_ge[:, i],
                                                      ALU.is_lt, ALU.mult))
                nc.vector.tensor_scalar(id_row[:, i], id_low[:, i], float(hi - lo - 1), None,
                                        ALU.min).then_inc(S["rows_ready"], 1)
            v.settle()
            dve.wait_ge(rows_in, (b + 1) * (16 * 4 * NT))
            for t in range(NT):
                for i in range(4):
                    dst = hid[:, t, :] if i == 0 else low[:, t, EMB_AT[i] - D:EMB_AT[i] - D + EMB[i]]
                    ins_ = nc.vector.tensor_scalar(dst, rows[:, t, EMB_AT[i]:EMB_AT[i] + EMB[i]],
                                                   id_mask[:, i, t:t + 1], 16.0, ALU.mult, ALU.mult)
                    if i < 3:
                        v.step(ins_)
                    else:
                        ins_.then_inc(S["low_ready"], 1)
            v.settle()
            for half in range(2):
                dve.wait_ge(S["proj_ps"], half + 1)
                t2 = slice(2 * half, 2 * half + 2)
                v.step(nc.vector.tensor_tensor(hid[:, t2, :], hid[:, t2, :],
                                               B[1 + half][:, :].rearrange("p (t c) -> p t c", t=2), ALU.add))
            v.settle()

        def embed_gpsimd(pool):
            pool.wait_ge(S["rows_ready"], 4)
            for t in range(NT):
                for i in range(4):
                    nc.gpsimd.indirect_dma_start(
                        rows[:, t, EMB_AT[i]:EMB_AT[i] + EMB[i]], None, ins[f"emb{i}"],
                        bass.IndirectOffsetOnAxis(ap=id_row[:, i, t:t + 1], axis=0)).then_inc(rows_in, 16)

        def embed_tensor(pe):
            for t in range(NT):
                pe.wait_ge(S["low_ready"], t + 1)
                nc.tensor.transpose(B[0][0:EMB_LOW, t * P:(t + 1) * P], low[:, t, :], ident[:, :]).then_inc(S["low_ps"], 1)
            pe.wait_ge(S["lowT_ready"], 1)
            for t in range(NT):
                nc_i = nc.tensor.matmul(B[1 + t // 2][:, (t % 2) * D:(t % 2 + 1) * D], lowT[:, t * P:(t + 1) * P],
                                        proj[:, :], start=True, stop=True)
                if t % 2:
                    nc_i.then_inc(S["proj_ps"], 1)

        def embed_scalar(act):
            act.wait_ge(S["low_ps"], NT)
            nc.scalar.copy(lowT, B[0][0:EMB_LOW, :]).then_inc(S["lowT_ready"], 1)

        def norm_vector(dve, v, use):
            for t in range(NT):
                v.step(nc.vector.bn_stats(ln_part[:, t, :], hid[:, t, :]))
            v.settle()
            for t in range(NT):
                v.step(nc.vector.bn_aggr(ln_mv[:, t, :], ln_part[:, t, :]))
            v.settle()
            nc.vector.tensor_scalar(ln_ve[:, :], ln_mv[:, :, 1], 1e-5, None, ALU.add).then_inc(S["ln_var"], 1)
            dve.wait_ge(S["ln_std"], use + 1)
            v.link(nc.vector.reciprocal(ln_r[:, :], ln_sd[:, :]))
            for t in range(NT):
                nc.vector.tensor_scalar(xn[:, t, :], hid[:, t, :], ln_mv[:, t, 0:1], ln_r[:, t:t + 1],
                                        ALU.subtract, ALU.mult).then_inc(S["ln_out"], 1)

        def norm_scalar(act, use):
            act.wait_ge(S["ln_var"], use + 1)
            nc.scalar.activation(ln_sd[:, :], ln_ve[:, :], ACT.Sqrt).then_inc(S["ln_std"], 1)

        def turn_tensor(pe, src, turn, first, second):
            for k in range(KD):
                bank = (first, second)[k]
                for t in range(NT):
                    last = nc.tensor.transpose(B[bank][:, t * P:(t + 1) * P], src[:, t, k * P:(k + 1) * P], ident[:, :])
                last.then_inc(S["turn_ps"], 1)

        def turn_scalar(act, dst, turn, first, second):
            for k in range(KD):
                act.wait_ge(S["turn_ps"], KD * turn + k + 1)
                nc.scalar.copy(dst[:, k, :], B[(first, second)[k]][:, :]).then_inc(S["turn_sb"], 1)

        def turned(eng, turn):
            eng.wait_ge(S["turn_sb"], KD * (turn + 1))

        def attn_sync(sp):
            for q in range(4):
                if q < 2:
                    sp.wait_ge(S["unit_ready"], 1)
                else:
                    sp.wait_ge(S["fir_ps"], q - 1)
                f = ins["fir_long"]
                src = bass.AP(tensor=f.tensor, offset=64 * q * 192 + 1, ap=[[1, P], [192, 64], [1, 64]])
                sp.dma_start(toep[:, q % 2], src).then_inc(toep_in[q % 2], 16)

        def attn_tensor(pe):
            turned(pe, 0)
            for i in range(3):
                for c in range(KD):
                    for k in range(KD):
                        last = nc.tensor.matmul(B[2 * i + c][:, :], w_qkv[:, i, k, c * P:(c + 1) * P], xT[:, k, :],
                                                start=(k == 0), stop=(k == KD - 1))
                    last.then_inc(S["qkv_ps"], 1)
            for t in range(NT):
                for k in range(KD):
                    last = nc.tensor.matmul(B[6][:, t * H:(t + 1) * H], xT[:, k, t * P:(t + 1) * P], w_beta[:, k, :],
                                            start=(k == 0), stop=(k == KD - 1))
            last.then_inc(S["beta_ps"], 1)
            pe.wait_ge(S["pre_ready"], 6)
            for i in range(3):
                pe.wait_ge(S["silu_ready"], KD * (i + 1))
                for half in range(2):
                    for t in range(2 * half, 2 * half + 2):
                        for c in range(KD):
                            src = (conv[:, 2 * i + c, t * P:(t + 1) * P] if i < 2 else
                                   vpad[:, c, SHORT - 1 + t * P:SHORT - 1 + (t + 1) * P])
                            last = nc.tensor.transpose(B[2 * i + half][:, (t % 2) * D + c * P:(t % 2) * D + (c + 1) * P],
                                                       src, ident[:, :])
                    last.then_inc(S["tok_ps"], 1)
            pe.wait_ge(S["tok_ready"], 6)
            v_tok = lambda t: feats[:, t:t + 2, 3, :]
            for n in range(2):
                nc.tensor.matmul(B[n][:, :], flips[:, 0, :], v_tok(2 * n), start=True, stop=True).then_inc(S["window_ps"], 1)
            nc.tensor.matmul(B[2][:, 0:D], flips[:, 1, :], feats[:, 0, 3, :], start=True, stop=True)
            nc.tensor.matmul(B[2][:, D:2 * D], flips[:, 1, :], feats[:, 1, 3, :], start=True, stop=False)
            nc.tensor.matmul(B[2][:, D:2 * D], flips[:, 2, :], feats[:, 0, 3, :], start=False, stop=True)\
                .then_inc(S["window_ps"], 1)
            nc.tensor.matmul(B[3][:, :], flips[:, 1, :], v_tok(2), start=True, stop=False)
            nc.tensor.matmul(B[3][:, :], flips[:, 2, :], v_tok(1), start=False, stop=True).then_inc(S["window_ps"], 1)
            pe.wait_ge(S["window_ready"], 4)
            pe.wait_ge(S["unit_ready"], 1)
            for i in range(3):
                for c in range(KD):
                    for t in range(NT):
                        src = qk_tok[:, i, t, c * P:(c + 1) * P] if i < 2 else kb[:, t, c * P:(c + 1) * P]
                        last = nc.tensor.transpose(B[2 * i + c][:, t * P:(t + 1) * P], src, ident[:, :])
                    last.then_inc(S["unitT_ps"], 1)
            for q in range(4):
                pe.wait_ge(toep_in[q % 2], 16 * (q // 2 + 1))
                pe.wait_ge(S["unitT_ready"], min(q, 3) + 1)
                for c in range(64):
                    last = nc.tensor.matmul(B[q][0:64, c * 8:(c + 1) * 8], toep[:, q % 2, c, :],
                                            win[:, :, 64 * q + c], start=True, stop=True)
                last.then_inc(S["fir_ps"], 1)
            pe.wait_ge(S["unitT_ready"], 6)
            for n in range(4):
                pe.wait_ge(S["fir_ready"], 2 * n + 2)
                odd = n % 2
                r = slice(64 * odd, 64 * odd + 64)
                for t in range(2 * (n // 2), 2 * (n // 2) + 2):
                    tt = slice(t * P, (t + 1) * P)
                    for c in range(KD):
                        at = (KD * (t % 2) + c) * P
                        last = nc.tensor.matmul(B[n][:, at:at + P], unitT[r, 1, c, tt], unitT[r, 2, c, tt],
                                                start=True, stop=True)
                last.then_inc(S["gram_ps"], 1)
            for t in range(NT):
                pe.wait_ge(S["u0_ready"], t + 1)
                if t >= 2:
                    pe.wait_ge(S["t0_ready"], t - 1)
                for h in range(H):
                    last = nc.tensor.transpose(B[4 + t % 2][:, h * P:(h + 1) * P], U_m[:, t, h, :], ident[:, :])
                last.then_inc(S["t0_ps"], 1)
            for lv in range(1, LEVELS):
                n = (lv - 1) * NT
                for t in range(NT):
                    pe.wait_ge(S["lm_ready"], n + t + 1)
                    if lv == 1:
                        pe.wait_ge(S["t0_ready"], NT)
                    else:
                        pe.wait_ge(S["tu_ready"], n - NT + t + 1)
                    if n + t >= 2:
                        pe.wait_ge(S["p_ready"], n + t - 1)
                    for h in range(H):
                        last = nc.tensor.matmul(B[4 + t % 2][:, h * P:(h + 1) * P], L_T[:, t, h, :], T_m[:, t, h, :],
                                                start=True, stop=True)
                    last.then_inc(S["p_ps"], 1)
                    if t >= 1:
                        delta_products(pe, lv, t - 1)
                delta_products(pe, lv, NT - 1)
            for t in range(NT):
                pe.wait_ge(S["tu_ready"], (LEVELS - 2) * NT + t + 1)
                for h in range(H):
                    r = slice(64 * (h % 2), 64 * (h % 2) + 64)
                    last = nc.tensor.matmul(B[4 + t // 2][r, (t % 2) * D + (h // 2) * P:(t % 2) * D + (h // 2 + 1) * P],
                                            kb[:, t, h * DH:(h + 1) * DH], U_m[:, t, h, :], start=True, stop=True)
                last.then_inc(S["w_ps"], 1)
            for t in range(NT):
                tt = slice(t * P, (t + 1) * P)
                if t == 0:
                    pe.wait_ge(S["w_ready"], NT)
                else:
                    pe.wait_ge(S["ds_ready"], t)
                    pe.wait_ge(S["attn_ready"], 2 * t)
                for h in HEAD_ORDER:
                    r = slice(64 * (h % 2), 64 * (h % 2) + 64)
                    c = h // 2
                    last = nc.tensor.matmul(B[(3, 6)[h % 2]][:, c * P:(c + 1) * P], unitT[r, 1, c, tt],
                                            unitT[r, 0, c, tt], start=True, stop=True)
                last.then_inc(S["attn_ps"], 1)
                for h in HEAD_ORDER:
                    r = slice(64 * (h % 2), 64 * (h % 2) + 64)
                    c = slice((h // 2) * DH, (h // 2 + 1) * DH)
                    last = nc.tensor.matmul(B[(0, 4)[h % 2]][:, c], U_m[:, t, h, :], vb[:, t, h * DH:(h + 1) * DH],
                                            start=True, stop=(t == 0))
                    if t:
                        last = nc.tensor.matmul(B[(0, 4)[h % 2]][:, c], neg_wT[r, t, h // 2, :], state[r, h // 2, :],
                                                start=False, stop=True)
                last.then_inc(S["ua_ps"], 1)
                pe.wait_ge(S["ua_ready"], 2 * (t + 1))
                if t:
                    pe.wait_ge(S["do_ready"], 2 * t)
                if t < NT - 1:
                    for h in HEAD_ORDER:
                        r = slice(64 * (h % 2), 64 * (h % 2) + 64)
                        hh = slice(h * DH, (h + 1) * DH)
                        last = nc.tensor.matmul(B[2][r, (h // 2) * DH:(h // 2 + 1) * DH], qk_tok[:, 1, t, hh],
                                                u_adj[:, hh], start=True, stop=True)
                    last.then_inc(S["ds_ps"], 1)
                pe.wait_ge(S["attn_ready"], 2 * (t + 1))
                for h in HEAD_ORDER:
                    r = slice(64 * (h % 2), 64 * (h % 2) + 64)
                    c = slice((h // 2) * DH, (h // 2 + 1) * DH)
                    last = nc.tensor.matmul(B[(1, 5)[h % 2]][:, c], attn_m[:, t % 2, h, :], u_adj[:, h * DH:(h + 1) * DH],
                                            start=True, stop=(t == 0))
                    if t:
                        last = nc.tensor.matmul(B[(1, 5)[h % 2]][:, c], unitT[r, 0, h // 2, tt], state[r, h // 2, :],
                                                start=False, stop=True)
                last.then_inc(S["do_ps"], 1)
            pe.wait_ge(S["short_ready"], KD)
            pe.wait_ge(S["do_ready"], 2 * NT)
            for half in range(2):
                for t in range(2 * half, 2 * half + 2):
                    for c in range(KD):
                        last = nc.tensor.transpose(B[4 + half][:, (t % 2) * D + c * P:(t % 2) * D + (c + 1) * P],
                                                   short_T[:, c, t * P:(t + 1) * P], ident[:, :])
                last.then_inc(S["short_ps"], 1)
            pe.wait_ge(S["stat_ready"], 1)
            for t in range(NT):
                last = nc.tensor.transpose(B[6][0:H * 16, t * P:(t + 1) * P],
                                           stats[:, t].rearrange("p h k s -> p (h k s)"), ident[:, :])
            last.then_inc(S["stat_ps"], 1)
            pe.wait_ge(S["statT_ready"], 1)
            pe.wait_ge(S["do_ready"], 2 * NT)

            def logits(h):
                pe.wait_ge(S["h1_ready"], KD * (h + 1))
                for t in range(NT):
                    for k in range(KD):
                        last = nc.tensor.matmul(B[7][:, (t * H + h) * 4:(t * H + h + 1) * 4],
                                                h1[:, h % 2, k, t * P:(t + 1) * P], mlp2_w[:, k, :],
                                                start=(k == 0), stop=(k == KD - 1))
                last.then_inc(S["logit_ps"], 1)

            for h in range(H):
                for c in range(KD):
                    n = KD * h + c
                    if n >= 4:
                        pe.wait_ge(S["h1_ready"], n - 3)
                    for k in range(KD):
                        nc.tensor.matmul(B[n % 4][:, :], mlp1_a[:, k, c * P:(c + 1) * P], xT[:, k, :],
                                         start=(k == 0), stop=False)
                    nc.tensor.matmul(B[n % 4][:, :], mlp1_s[:, h, c * P:(c + 1) * P], statT,
                                     start=False, stop=True).then_inc(S["h1_ps"], 1)
                if h:
                    logits(h - 1)
            logits(H - 1)
            pe.wait_ge(S["mix_ready"], 1)
            turn_tensor(pe, o_tok, 1, 0, 1)
            turned(pe, 1)
            for t in range(NT):
                for k in range(KD):
                    last = nc.tensor.matmul(B[2 + t // 2][:, (t % 2) * D:(t % 2 + 1) * D], oT[:, k, t * P:(t + 1) * P],
                                            o_w[:, k, :], start=(k == 0), stop=(k == KD - 1))
                if t % 2:
                    last.then_inc(S["o_ps"], 1)

        def delta_products(pe, lv, t):
            n = (lv - 1) * NT + t
            pe.wait_ge(S["p_ready"], n + 1)
            if n >= 2:
                pe.wait_ge(S["tu_ready"], n - 1)
            if lv < LEVELS - 1:
                for h in range(H):
                    nc.tensor.matmul(B[t % 2][:, h * P:(h + 1) * P], U_m[:, t, h, :], P_m[:, t, h, :],
                                     start=True, stop=True)
            for h in range(H):
                last = nc.tensor.matmul(B[2 + t % 2][:, h * P:(h + 1) * P], P_m[:, t, h, :], U_m[:, t, h, :],
                                        start=True, stop=True)
            last.then_inc(S["d_ps"], 1)

        def attn_scalar(act, c):
            for i in range(6):
                act.wait_ge(S["qkv_ps"], i + 1)
                nc.scalar.copy(pre[:, i, TAPS - 1:], B[i][:, :]).then_inc(S["pre_ready"], 1)
            for i in range(6):
                act.wait_ge(S["conv_ready"], i + 1)
                dst = conv[:, i, :] if i < 4 else vpad[:, i - 4, SHORT - 1:]
                nc.scalar.activation(dst, conv[:, i, :], ACT.Silu).then_inc(S["silu_ready"], 1)
            act.wait_ge(S["beta_ps"], 1)
            nc.scalar.activation(beta, B[6][:, 0:NT * H], ACT.Sigmoid).then_inc(S["beta_ready"], 1)
            for i in range(6):
                act.wait_ge(S["tok_ps"], i + 1)
                half = i % 2
                src = B[i][:, :].rearrange("p (t c) -> p t c", t=2)
                dst = qk_tok[:, i // 2, 2 * half:2 * half + 2, :] if i < 4 else feats[:, 2 * half:2 * half + 2, 3, :]
                nc.scalar.copy(dst, src).then_inc(S["tok_ready"], 1)
            for n in range(4):
                act.wait_ge(S["window_ps"], n + 1)
                first = (1, 5, 0, 4)[n]
                nc.scalar.copy(win[:, first:first + 3:2, :], B[n][:, :].rearrange("p (w c) -> p w c", w=2))\
                    .then_inc(S["window_ready"], 1)
            act.wait_ge(S["ss_ready"], 1)
            nc.scalar.activation(ss_sd, ss, ACT.Sqrt).then_inc(S["ss_root"], 1)
            for i in range(6):
                act.wait_ge(S["unitT_ps"], i + 1)
                nc.scalar.copy(unitT[:, i // 2, i % 2, :], B[i][:, :]).then_inc(S["unitT_ready"], 1)
            for q in range(4):
                act.wait_ge(S["fir_ps"], q + 1)
                for half in range(2):
                    src = B[q][0:64, :].rearrange("p (c t w) -> p w t c", t=NT, w=2)[:, half]
                    nc.scalar.copy(feats[64 * half:64 * half + 64, :, 1, 64 * q:64 * (q + 1)], src)\
                        .then_inc(S["fir_ready"], 1)
            act.wait_ge(S["fir_ps"], 4)
            for n in range(4):
                act.wait_ge(S["gram_ps"], n + 1)
                t = 2 * (n // 2)
                nc.scalar.copy(M_T[:, t:t + 2, n % 2:H:2],
                               B[n][:, :].rearrange("p (t h c) -> p t h c", t=2, h=KD)).then_inc(S["gram_ready"], 1)
            for t in range(NT):
                act.wait_ge(S["t0_ps"], t + 1)
                nc.scalar.copy(T_m[:, t], B[4 + t % 2][:, :].rearrange("p (h c) -> p h c", h=H)).then_inc(S["t0_ready"], 1)
            for lv in range(1, LEVELS):
                for t in range(NT):
                    n = (lv - 1) * NT + t
                    act.wait_ge(S["p_ps"], n + 1)
                    if n >= NT:
                        act.wait_ge(S["d_ps"], n - NT + 1)
                    nc.scalar.copy(P_m[:, t], B[4 + t % 2][:, :].rearrange("p (h c) -> p h c", h=H))\
                        .then_inc(S["p_ready"], 1)
            for t in range(NT):
                act.wait_ge(S["w_ps"], 2 * (t // 2) + 2)
                nc.scalar.mul(neg_wT[:, t], B[4 + t // 2][:, (t % 2) * D:(t % 2 + 1) * D]
                              .rearrange("p (k c) -> p k c", k=KD), -1.0).then_inc(S["w_ready"], 1)
            for t in range(NT):
                act.wait_ge(S["ua_ps"], t + 1)
                if t:
                    act.wait_ge(S["do_ps"], t)
                by_head = lambda x: x.rearrange("p (h d) -> p h d", d=DH)
                for odd in range(2):
                    nc.scalar.copy(by_head(u_adj)[:, odd:H:2], by_head(B[(0, 4)[odd]][:, 0:P])).then_inc(S["ua_ready"], 1)
                act.wait_ge(S["do_ps"], t + 1)
                for odd in range(2):
                    nc.scalar.copy(by_head(feats[:, t, 2, :])[:, odd:H:2], by_head(B[(1, 5)[odd]][:, 0:P]))\
                        .then_inc(S["do_ready"], 1)
            for half in range(2):
                act.wait_ge(S["short_ps"], half + 1)
                nc.scalar.copy(feats[:, 2 * half:2 * half + 2, 0, :], B[4 + half][:, :].rearrange("p (t c) -> p t c", t=2))\
                    .then_inc(S["short_tok"], 1)
            act.wait_ge(S["l2_ready"], 1)
            nc.scalar.activation(st_l2, st_mean2, ACT.Sqrt).then_inc(S["l2_root"], 1)
            act.wait_ge(S["stat_ps"], 1)
            nc.scalar.copy(statT, B[6][0:H * 16, :]).then_inc(S["statT_ready"], 1)
            for h in range(H):
                for k in range(KD):
                    n = KD * h + k
                    act.wait_ge(S["h1_ps"], n + 1)
                    if h >= 2:
                        act.wait_ge(S["logit_ps"], h - 1)
                    nc.scalar.activation(h1[:, h % 2, k, :], B[n % 4][:, :], ACT.Gelu_apprx_tanh,
                                         bias=mlp1_b[:, k:k + 1]).then_inc(S["h1_ready"], 1)
            act.wait_ge(S["lg_ready"], 1)
            nc.scalar.activation(lg_e, lg_p, ACT.Exp, scale=inv_temp).then_inc(S["lg_exp"], 1)
            act.wait_ge(S["mix_ss"], 1)
            nc.scalar.activation(ss_sd[:, 0:NT * H], ss[:, 0:NT * H], ACT.Sqrt).then_inc(S["mix_root"], 1)
            turn_scalar(act, oT, 1, 0, 1)

        def attn_vector(dve, v):
            V = nc.vector
            v.step(V.memset(pre[:, :, 0:TAPS - 1], 0.0))
            v.step(V.memset(vpad[:, :, 0:SHORT - 1], 0.0))
            v.settle()
            for i in range(0, 6, 2):
                dve.wait_ge(S["pre_ready"], i + 2)
                for tap in range(TAPS):
                    for j in (i, i + 1):
                        x = pre[:, j, tap:tap + T]
                        w = conv_w[:, j, tap:tap + 1]
                        if tap == 0:
                            v.step(V.tensor_scalar(conv[:, j, :], x, w, None, ALU.mult))
                        elif tap < TAPS - 1:
                            v.step(V.scalar_tensor_tensor(conv[:, j, :], x, w, conv[:, j, :], ALU.mult, ALU.add))
                        else:
                            V.scalar_tensor_tensor(conv[:, j, :], x, w, conv[:, j, :], ALU.mult, ALU.add)\
                                .then_inc(S["conv_ready"], 1)
                    v.settle()
            dve.wait_ge(S["beta_ready"], 1)
            v.step(V.tensor_scalar(beta, beta, 1e-6, None, ALU.max))
            dve.wait_ge(S["tok_ready"], 4)
            v.link(V.tensor_tensor(sq, qk_tok, qk_tok, ALU.mult))
            v.link(V.tensor_reduce(ss, sq.rearrange("p i t (h d) -> p (i t h) d", h=H), AX_X, ALU.add))
            V.tensor_scalar(ss, ss, 1e-6, None, ALU.add).then_inc(S["ss_ready"], 1)
            dve.wait_ge(S["ss_root"], 1)
            v.link(V.reciprocal(unit, ss_sd))
            heads = qk_tok.rearrange("p i t (h d) -> p (i t h) d", h=H)
            v.link(V.tensor_tensor(heads, heads, spread(unit, 2, DH), ALU.mult))
            k_heads = qk_tok[:, 1].rearrange("p t (h d) -> p (t h) d", h=H)
            dve.wait_ge(S["tok_ready"], 6)
            v_heads = feats[:, :, 3, :].rearrange("p t (h d) -> p t h d", h=H)
            v.step(V.tensor_tensor(vb.rearrange("p t (h d) -> p t h d", h=H), v_heads,
                                   spread(beta.rearrange("p (t h) -> p t h", t=NT), 3, DH), ALU.mult))
            V.tensor_tensor(kb.rearrange("p t (h d) -> p (t h) d", h=H), k_heads, spread(beta, 2, DH), ALU.mult)\
                .then_inc(S["unit_ready"], 1)
            for t in range(NT):
                dve.wait_ge(S["gram_ready"], 2 * (t // 2) + 2)
                v.link(V.tensor_tensor(U_m[:, t], M_T[:, t], spread(level_mask[:, 0, :], 1, H), ALU.mult))
                V.tensor_tensor(U_m[:, t], spread(ident[:, :], 1, H), U_m[:, t], ALU.subtract).then_inc(S["u0_ready"], 1)
            for lv in range(1, LEVELS):
                for t in range(NT):
                    n = (lv - 1) * NT + t
                    dve.wait_ge(S["d_ps"], n + 1)
                    if lv == 1:
                        dve.wait_ge(S["u0_ready"], NT)
                        dve.wait_ge(S["t0_ready"], NT)
                    else:
                        dve.wait_ge(S["tu_ready"], n - NT + 1)
                    if lv < LEVELS - 1:
                        v.step(V.tensor_tensor(T_m[:, t], T_m[:, t], B[t % 2][:, :].rearrange("p (h c) -> p h c", h=H),
                                               ALU.subtract))
                    V.tensor_tensor(U_m[:, t], U_m[:, t], B[2 + t % 2][:, :].rearrange("p (h c) -> p h c", h=H),
                                    ALU.subtract).then_inc(S["tu_ready"], 1)
            for t in range(NT):
                dve.wait_ge(S["attn_ps"], t + 1)
                if t >= 2:
                    dve.wait_ge(S["do_ps"], t - 1)
                for odd in range(2):
                    V.tensor_tensor(attn_m[:, t % 2, odd:H:2], B[(3, 6)[odd]][:, 0:D].rearrange("p (h c) -> p h c", h=KD),
                                    spread(causal[:, :], 1, KD), ALU.mult).then_inc(S["attn_ready"], 1)
                if t < NT - 1:
                    dve.wait_ge(S["ds_ps"], t + 1)
                    if t:
                        dve.wait_ge(S["do_ps"], t + 1)
                        dve.wait_ge(S["ds_ready"], t)
                        V.tensor_tensor(state, state, B[2][:, 0:P].rearrange("p (k c) -> p k c", k=KD), ALU.add)\
                            .then_inc(S["ds_ready"], 1)
                    else:
                        V.tensor_copy(state, B[2][:, 0:P].rearrange("p (k c) -> p k c", k=KD)).then_inc(S["ds_ready"], 1)
            for tap in range(SHORT):
                for c in range(KD):
                    x = vpad[:, c, tap:tap + T]
                    w = short_w[:, c, tap:tap + 1]
                    if tap == 0:
                        if c == 0:
                            dve.wait_ge(S["do_ps"], NT)
                        v.step(V.tensor_scalar(short_T[:, c, :], x, w, None, ALU.mult))
                    elif tap < SHORT - 1:
                        v.step(V.scalar_tensor_tensor(short_T[:, c, :], x, w, short_T[:, c, :], ALU.mult, ALU.add))
                    else:
                        V.scalar_tensor_tensor(short_T[:, c, :], x, w, short_T[:, c, :], ALU.mult, ALU.add)\
                            .then_inc(S["short_ready"], 1)
                v.settle()
            dve.wait_ge(S["short_tok"], 2)
            dve.wait_ge(S["do_ready"], 2 * NT)
            f = feats.rearrange("p t k (h d) -> p (t k h) d", h=H)
            cc = cent.rearrange("p t g d -> p (t g) d")
            flat = lambda x: x.rearrange("p t k h -> p (t k h)")
            v.step(V.tensor_reduce(flat(st_sum), f, AX_X, ALU.add))
            v.step(V.tensor_reduce(flat(st_abs), f, AX_X, ALU.add, apply_absolute_value=True))
            v.settle()
            v.link(V.tensor_scalar(flat(stats_mean), flat(st_sum), 1.0 / DH, None, ALU.mult))
            v.link(V.tensor_tensor(cc, f, spread(flat(stats_mean), 2, DH), ALU.subtract))
            v.link(V.tensor_tensor(cc, cc, cc, ALU.mult))
            v.step(V.tensor_reduce(flat(st_css), cc, AX_X, ALU.add))
            v.step(V.tensor_tensor(flat(st_mean2), flat(st_sum), flat(stats_mean), ALU.mult))
            v.settle()
            V.tensor_tensor(flat(st_mean2), flat(st_mean2), flat(st_css), ALU.add).then_inc(S["l2_ready"], 1)
            dve.wait_ge(S["l2_root"], 1)
            for t in range(NT):
                for n, (src, mul) in enumerate(((stats_mean, 1.0), (st_css, 1.0 / DH), (st_abs, 1.0 / DH), (st_l2, 1.0))):
                    ins_ = V.tensor_scalar(stats[:, t, :, :, n].rearrange("p h k -> p k h"), src[:, t], mul, None, ALU.mult)
                    if t == NT - 1 and n == 3:
                        ins_.then_inc(S["stat_ready"], 1)
                    else:
                        v.step(ins_)
            dve.wait_ge(S["logit_ps"], H)
            L = B[7][:, 0:NT * H * 4].rearrange("p (t h k) -> p (t h) k", t=NT, h=H)
            g = lambda x: x.rearrange("p t h k -> p (t h) k")
            m = lambda x: x.rearrange("p t h -> p (t h)")
            v.link(V.tensor_tensor(g(lg), L, spread(mlp2_b[:, :], 1, NT * H), ALU.add))
            v.link(V.tensor_reduce(m(lg_m), g(lg), AX_X, ALU.max))
            V.tensor_tensor(g(lg_p), g(lg), spread(m(lg_m), 2, 4), ALU.subtract).then_inc(S["lg_ready"], 1)
            dve.wait_ge(S["lg_exp"], 1)
            v.link(V.tensor_reduce(m(lg_s), g(lg_e), AX_X, ALU.add))
            v.link(V.reciprocal(m(lg_r), m(lg_s)))
            v.link(V.tensor_tensor(g(lg_p), g(lg_e), spread(m(lg_r), 2, 4), ALU.mult))
            v.link(V.tensor_scalar(g(lg_p), g(lg_p), 0.02, None, ALU.max))
            v.link(V.tensor_reduce(m(lg_s), g(lg_p), AX_X, ALU.add))
            v.link(V.reciprocal(m(lg_r), m(lg_s)))
            v.link(V.tensor_tensor(g(lg_p), g(lg_p), spread(m(lg_r), 2, 4), ALU.mult))
            v.link(V.tensor_tensor(lg_p[:, :, :, 0], lg_p[:, :, :, 0], spread(res_gate[:, :], 1, NT), ALU.add))
            for t in range(NT):
                for k in range(4):
                    v.step(V.tensor_tensor(mix[:, t, k], feats[:, t, k, :].rearrange("p (h d) -> p h d", h=H),
                                           spread(lg_p[:, t, :, k], 2, DH), ALU.mult))
            v.settle()
            mk = lambda k: mix[:, :, k].rearrange("p t h d -> p t (h d)")
            v.step(V.tensor_tensor(mk(0), mk(0), mk(1), ALU.add))
            v.step(V.tensor_tensor(mk(2), mk(2), mk(3), ALU.add))
            v.settle()
            v.link(V.tensor_tensor(o_tok, mk(0), mk(2), ALU.add))
            v.link(V.tensor_tensor(o_sq, o_tok, o_tok, ALU.mult))
            oh = o_tok.rearrange("p t (h d) -> p (t h) d", h=H)
            v.link(V.tensor_reduce(ss[:, 0:NT * H], o_sq.rearrange("p t (h d) -> p (t h) d", h=H), AX_X, ALU.add))
            V.tensor_scalar(ss[:, 0:NT * H], ss[:, 0:NT * H], 1.0 / DH, 1e-5, ALU.mult, ALU.add).then_inc(S["mix_ss"], 1)
            dve.wait_ge(S["mix_root"], 1)
            v.link(V.reciprocal(unit[:, 0:NT * H], ss_sd[:, 0:NT * H]))
            v.link(V.tensor_tensor(oh, oh, spread(unit[:, 0:NT * H], 2, DH), ALU.mult))
            V.tensor_tensor(oh, oh, spread(norm_w[:, :], 1, NT * H), ALU.mult).then_inc(S["mix_ready"], 1)
            add_hidden(dve, v, S["o_ps"], 2, 3)

        def add_hidden(dve, v, ready, first, second):
            for half in range(2):
                dve.wait_ge(ready, half + 1)
                t2 = slice(2 * half, 2 * half + 2)
                v.step(nc.vector.tensor_tensor(hid[:, t2, :], hid[:, t2, :],
                                               B[(first, second)[half]][:, :].rearrange("p (t c) -> p t c", t=2), ALU.add))
            v.settle()

        def attn_gpsimd(pool):
            for lv in range(1, LEVELS):
                for t in range(NT):
                    n = (lv - 1) * NT + t
                    pool.wait_ge(S["gram_ready"], 2 * (t // 2) + 2)
                    if lv > 1:
                        pool.wait_ge(S["p_ps"], n - NT + 1)
                    nc.gpsimd.tensor_tensor(L_T[:, t], M_T[:, t], spread(level_mask[:, lv, :], 1, H), ALU.mult)\
                        .then_inc(S["lm_ready"], 1)

        def peer_vector(dve, v):
            V = nc.vector
            dve.wait_ge(S["ln_out"], 2 * NT)
            v.link(V.tensor_tensor(xx, xn[:, :, :], xn[:, :, :], ALU.mult))
            v.link(V.tensor_reduce(x_sq, xx, AX_X, ALU.add))
            v.link(V.tensor_copy(x_r, x_sq))
            V.tensor_copy(x_sq, x_r).then_inc(S["xss_ready"], 1)
            dve.wait_ge(S["xss_root"], 1)
            v.link(V.tensor_scalar(x_sd, x_sd, 1e-12, None, ALU.max))
            v.link(V.reciprocal(x_r, x_sd))
            for t in range(NT):
                v.step(V.tensor_scalar(xn[:, t, :], xn[:, t, :], x_r[:, t:t + 1], 16.0, ALU.mult, ALU.mult))
            v.settle()
            V.tensor_tensor(xn[:, :, :], xn[:, :, :], spread(gamma[:, :], 1, NT), ALU.mult).then_inc(S["ln_out"], 1)
            for t in range(NT):
                dve.wait_ge(S["sim_ready"], 2 * t + 2)
                segs = [(c // PH, c % PH, sim[:, t % 2, c, :]) for c in range(2 * PH)]
                for p, h, x in segs:
                    v.step(V.max(val[:, p, t, h, 0:8], x))
                v.settle()
                for p, h, x in segs:
                    v.step(V.max_index(key[:, p, t, h, 0:8], val[:, p, t, h, 0:8], x))
                v.settle()
                for p, h, x in segs:
                    v.step(V.match_replace(x, val[:, p, t, h, 0:8], x, LOWEST))
                v.settle()
                for p, h, x in segs:
                    v.step(V.max(val[:, p, t, h, 8:16], x))
                v.settle()
                for p, h, x in segs[:-1]:
                    v.step(V.max_index(key[:, p, t, h, 8:16], val[:, p, t, h, 8:16], x))
                p, h, x = segs[-1]
                V.max_index(key[:, p, t, h, 8:16], val[:, p, t, h, 8:16], x).then_inc(S["sim_used"], 1)
            dve.wait_ge(S["sim_used"], NT)
            G = NT * PH
            vx, vy = (val[:, p].rearrange("p t h k -> p (t h) k") for p in range(2))
            for i in range(8):
                n = ROWLEN[i]
                v.step(V.tensor_tensor(cand[:, :, ROWAT[i]:ROWAT[i] + n], vy[:, :, 0:n],
                                       vx[:, :, i:i + 1].broadcast_to([P, G, n]), ALU.add))
            v.step(V.tensor_tensor(cand[:, :, ROWAT[8]:PAIRS], vx[:, :, 8:16],
                                   vy[:, :, 0:1].broadcast_to([P, G, 8]), ALU.add))
            v.step(V.tensor_copy(key_f, key))
            v.settle()
            kx = key_f[:, 0].rearrange("p t h k -> p (t h) k")
            dx = key_d[:, 0].rearrange("p t h k -> p (t h) k")
            v.step(V.tensor_copy(dx[:, :, 0:1], kx[:, :, 0:1]))
            v.step(V.tensor_tensor(dx[:, :, 1:16], kx[:, :, 1:16], kx[:, :, 0:15], ALU.subtract))
            for g in range(G):
                v.step(V.max(top[:, g, 0:8], cand[:, g, :]))
            v.settle()
            for g in range(G):
                v.step(V.max_index(pos[:, g, 0:8], top[:, g, 0:8], cand[:, g, :]))
            v.settle()
            for g in range(G):
                v.step(V.match_replace(cand[:, g, :], top[:, g, 0:8], cand[:, g, :], LOWEST))
            v.settle()
            for g in range(G):
                v.step(V.max(top[:, g, 8:16], cand[:, g, :]))
            v.settle()
            for g in range(G):
                v.step(V.max_index(pos[:, g, 8:16], top[:, g, 8:16], cand[:, g, :]))
            v.settle()
            v.step(V.tensor_copy(pos_f, pos))
            V.tensor_tensor(e_w, top, top[:, :, 0:1].broadcast_to([P, G, TOPK]), ALU.subtract).then_inc(S["score_ready"], 1)
            v.settle()
            for t in range(NT):
                g8 = slice(t * PH, (t + 1) * PH)
                ky = key_f[:, 1, t]
                by_row = lambda x: spread(spread(x, 1, TOPK), 1, PH)
                by_list = lambda x: spread(x, 2, TOPK)
                by_entry = lambda x: spread(x, 3, TOPK)
                v.link(V.tensor_tensor(look_a, by_entry(pos_f[:, g8, :]), by_row(row_at[:, :]), ALU.is_ge))
                v.link(V.tensor_tensor(look_b, look_a, by_list(dx[:, g8, :]), ALU.mult))
                v.step(V.tensor_reduce(e_x[:, g8, :], look_b, AX_X, ALU.add))
                v.settle()
                v.link(V.tensor_tensor(look_b, look_a, by_row(row_len[:, :]), ALU.mult))
                v.link(V.tensor_reduce(e_y[:, g8, :], look_b, AX_X, ALU.add))
                v.link(V.tensor_tensor(e_y[:, g8, :], pos_f[:, g8, :], e_y[:, g8, :], ALU.subtract))
                v.link(V.tensor_tensor(look_a, by_entry(e_y[:, g8, :]), by_row(iota16[:, :]), ALU.is_equal))
                v.link(V.tensor_tensor(look_b, look_a, by_list(ky), ALU.mult))
                v.link(V.tensor_reduce(e_y[:, g8, :], look_b, AX_X, ALU.add))
            v.link(V.tensor_copy(e_i, e_y))
            v.link(V.tensor_scalar(pos.bitcast(I32), e_i, 1, None, ALU.bitwise_and))
            v.link(V.tensor_copy(pos_f, pos.bitcast(I32)))
            v.step(V.scalar_tensor_tensor(e_x, pos_f, float(NK), e_x, ALU.mult, ALU.add))
            v.step(V.tensor_tensor(e_y, e_y, pos_f, ALU.subtract))
            v.settle()
            v.step(V.tensor_scalar(e_y, e_y, 0.5, None, ALU.mult))
            dve.wait_ge(S["score_exp"], 1)
            v.link(V.tensor_reduce(e_s, e_w, AX_X, ALU.add))
            v.link(V.reciprocal(e_r, e_s))
            V.tensor_tensor(e_w, e_w, spread(e_r, 2, TOPK), ALU.mult).then_inc(S["entry_ready"], 1)
            dve.wait_ge(S["entry_ps"], 3)
            v.step(V.tensor_copy(entT_x, B[4][:, :]))
            v.step(V.tensor_copy(entT_y, B[5][:, :]))
            v.link(V.tensor_copy(entT_w[:, 0, :], B[6][:, :]))
            v.link(V.tensor_tensor(w_rest, B[6][:, :], entT_w[:, 0, :], ALU.subtract))
            v.link(V.tensor_copy(entT_w[:, 1, :], w_rest))
            v.link(V.tensor_tensor(w_rest2, w_rest, entT_w[:, 1, :], ALU.subtract))
            v.link(V.tensor_copy(entT_w[:, 2, :], w_rest2))
            for n in range(T // TB):
                hx, hy, hw = hots[n % 2]
                tt = slice(n * TB, (n + 1) * TB)
                if n >= 2:
                    dve.wait_ge(S["cell_ps"], (TB // 16) * (n - 1))
                v.step(V.tensor_tensor(hy, spread(entT_y[:, tt], 1, YC), iota_y[:, :, :], ALU.is_equal))
                v.step(V.tensor_tensor(hx, spread(entT_x[:, tt], 1, P), iota_x[:, :, :], ALU.is_equal))
                v.settle()
                for i in range(3):
                    ins_ = V.tensor_tensor(hw[:, i], hy, spread(entT_w[:, i, tt], 1, YC), ALU.mult)
                    if i < 2:
                        v.step(ins_)
                    else:
                        ins_.then_inc(S["hot_ready"], 1)
            dve.wait_ge(S["cell_ready"], T // 16)
            for j in range(XC):
                dve.wait_ge(S["down_act"], j + 1)
                V.tensor_tensor(down[:, j % 2, :], down[:, j % 2, :], grid[:, j, :], ALU.mult).then_inc(S["down_ready"], 1)
            add_hidden_quarters(dve, v)

        def add_hidden_quarters(dve, v):
            dve.wait_ge(S["up_ps"], XC)
            for half in range(2):
                t2 = slice(2 * half, 2 * half + 2)
                v.step(nc.vector.tensor_tensor(hid[:, t2, :], hid[:, t2, :],
                                               B[6 + half][:, :].rearrange("p (t c) -> p t c", t=2), ALU.add))
            v.settle()

        def peer_scalar(act, c):
            act.wait_ge(S["xss_ready"], 1)
            nc.scalar.activation(x_sd, x_sq, ACT.Sqrt).then_inc(S["xss_root"], 1)
            turn_scalar(act, xT, 2, 0, 1)
            for t in range(NT):
                for half in range(2):
                    n = 2 * t + half
                    act.wait_ge(S["sim_ps"], n + 1)
                    if t >= 2:
                        act.wait_ge(S["sim_used"], t - 1)
                    nc.scalar.copy(sim[:, t % 2, half * PH:(half + 1) * PH, :],
                                   B[2 + n % 2][:, :].rearrange("p (h k) -> p h k", h=PH)).then_inc(S["sim_ready"], 1)
            act.wait_ge(S["score_ready"], 1)
            nc.scalar.activation(e_w, e_w, ACT.Exp).then_inc(S["score_exp"], 1)
            for n in range(T // 16):
                act.wait_ge(S["cell_ps"], n + 1)
                dst = grid[:, :, n * 16:(n + 1) * 16].rearrange("p j t -> p t j")
                nc.scalar.copy(dst, B[n % 4][:, :].rearrange("p (t j) -> p t j", t=16)).then_inc(S["cell_ready"], 1)
            for j in range(XC):
                act.wait_ge(S["down_ps"], j + 1)
                if j >= 2:
                    act.wait_ge(S["up_ps"], j - 1)
                nc.scalar.activation(down[:, j % 2, :], B[j % 2][:, :], ACT.Gelu).then_inc(S["down_act"], 1)

        def peer_tensor(pe):
            pe.wait_ge(S["ln_out"], 2 * NT + 1)
            turn_tensor(pe, xn, 2, 0, 1)
            turned(pe, 2)
            for t in range(NT):
                for half in range(2):
                    n = 2 * t + half
                    if n >= 2:
                        pe.wait_ge(S["sim_ready"], n - 1)
                    for k in range(KD):
                        last = nc.tensor.matmul(B[2 + n % 2][:, :], xT[:, k, t * P:(t + 1) * P],
                                                w_sim[:, k, half * 512:(half + 1) * 512],
                                                start=(k == 0), stop=(k == KD - 1))
                    last.then_inc(S["sim_ps"], 1)
            pe.wait_ge(S["entry_ready"], 1)
            for i, e in enumerate((e_x, e_y, e_w)):
                for t in range(NT):
                    last = nc.tensor.transpose(B[4 + i][:, t * P:(t + 1) * P],
                                               e[:, t * PH:(t + 1) * PH, :].rearrange("p h k -> p (h k)"), ident[:, :])
                last.then_inc(S["entry_ps"], 1)
            pe.wait_ge(S["sim_ready"], 2 * NT)
            for n in range(T // TB):
                hx, hy, hw = hots[n % 2]
                pe.wait_ge(S["hot_ready"], n + 1)
                for half in range(TB // 16):
                    m = n * (TB // 16) + half
                    if m >= 4:
                        pe.wait_ge(S["cell_ready"], m - 3)
                    for t in range(16):
                        for i in range(3):
                            last = nc.tensor.matmul(B[m % 4][:, t * YC:(t + 1) * YC], hx[:, :, half * 16 + t],
                                                    hw[:, i, :, half * 16 + t], start=(i == 0), stop=(i == 2))
                    last.then_inc(S["cell_ps"], 1)
            pe.wait_ge(S["cell_ready"], T // 16)

            def up(j):
                pe.wait_ge(S["down_ready"], j + 1)
                for t in range(NT):
                    last = nc.tensor.matmul(B[6 + t // 2][:, (t % 2) * D:(t % 2 + 1) * D],
                                            down[:, j % 2, t * P:(t + 1) * P], tab_u[:, (j // 2) % 2, j % 2, :],
                                            start=(j == 0 and t % 2 == 0), stop=(j == XC - 1), skip_group_check=True)
                last.then_inc(S["up_ps"], 1)

            for j in range(XC):
                pe.wait_ge(tab_in[(j // 2) % 2], 32 * (j // 4 + 1))
                if j >= 2:
                    pe.wait_ge(S["down_act"], j - 1)
                for k in range(KD):
                    last = nc.tensor.matmul(B[j % 2][:, :], tab_d[:, (j // 2) % 2, j % 2, k, :], xT[:, k, :],
                                            start=(k == 0), stop=(k == KD - 1))
                last.then_inc(S["down_ps"], 1)
                if j:
                    up(j - 1)
            up(XC - 1)

        def peer_sync(sp):
            for j in range(XC // 2):
                if j < 2:
                    sp.wait_ge(S["cell_ps"], T // 16)
                else:
                    sp.wait_ge(S["up_ps"], 2 * (j - 1))
                sp.dma_start(tab_d[:, j % 2], ins["downT"][:, 2 * j:2 * j + 2]).then_inc(tab_in[j % 2], 16)
                sp.dma_start(tab_u[:, j % 2], ins["up"][:, 2 * j:2 * j + 2]).then_inc(tab_in[j % 2], 16)

        def ssm_tensor(pe):
            pe.wait_ge(S["ln_out"], 3 * NT + 1)
            turn_tensor(pe, xn, 3, 0, 1)
            turned(pe, 3)
            for e in range(2 * DI // P):
                if e >= 4:
                    pe.wait_ge(S["xz_ready"], e - 3)
                for k in range(KD):
                    last = nc.tensor.matmul(B[2 + e % 4][:, :], w_in[:, k, e * P:(e + 1) * P], xT[:, k, :],
                                            start=(k == 0), stop=(k == KD - 1))
                last.then_inc(S["xz_ps"], 1)
            pe.wait_ge(S["xz_ready"], 4)
            for k in range(DI // P):
                last = nc.tensor.matmul(B[6][0:DS, :], w_B[:, k, :], xz[:, k, :], start=(k == 0), stop=(k == DI // P - 1))
            last.then_inc(S["state_ps"], 1)
            pe.wait_ge(S["state_ready"], 1)
            pe.wait_ge(S["xz_ready"], 8)
            for e in range(DI // P):
                nc.tensor.matmul(B[2 + e][:, :], w_C[:, e * P:(e + 1) * P], states, start=True, stop=True)\
                    .then_inc(S["c_ps"], 1)
            pe.wait_ge(S["y_ready"], DI // P)
            for t in range(NT):
                for k in range(DI // P):
                    last = nc.tensor.matmul(B[t // 2][:, (t % 2) * D:(t % 2 + 1) * D], y[:, k, t * P:(t + 1) * P],
                                            w_out[:, k, :], start=(k == 0), stop=(k == DI // P - 1))
                if t % 2:
                    last.then_inc(S["so_ps"], 1)

        def ssm_scalar(act, c):
            turn_scalar(act, xT, 3, 0, 1)
            for e in range(2 * DI // P):
                act.wait_ge(S["xz_ps"], e + 1)
                nc.scalar.activation(xz[:, e, :], B[2 + e % 4][:, :], ACT.Silu, bias=b_in[:, e:e + 1])\
                    .then_inc(S["xz_ready"], 1)

        def ssm_vector(dve, v):
            V = nc.vector
            dve.wait_ge(S["ln_out"], 3 * NT + 1)
            v.step(V.tensor_tensor(hid[:, :, :], hid[:, :, :], spread(b_out[:, :], 1, NT), ALU.add))
            dve.wait_ge(S["state_ps"], 1)
            v.link(V.tensor_scalar(drive, B[6][0:DS, :], 0.1, None, ALU.mult))
            V.tensor_tensor_scan(states, decay[:, :], drive, 0.0, ALU.mult, ALU.add).then_inc(S["state_ready"], 1)
            dve.wait_ge(S["xz_ready"], 8)
            for e in range(DI // P):
                dve.wait_ge(S["c_ps"], e + 1)
                v.link(V.scalar_tensor_tensor(y[:, e, :], xz[:, e, :], skip_D[:, e:e + 1], B[2 + e][:, :],
                                              ALU.mult, ALU.add))
                V.tensor_tensor(y[:, e, :], y[:, e, :], xz[:, DI // P + e, :], ALU.mult).then_inc(S["y_ready"], 1)
            add_hidden(dve, v, S["so_ps"], 0, 1)

        def moe_sync(sp):
            for e in range(NU):
                if e >= 2:
                    sp.wait_ge(S["e2_ps"], NT * (e - 1))
                sp.dma_start(moe_w1[:, e % 2], ins["W1"][e]).then_inc(ew_in[e % 2], 16)
                sp.dma_start(moe_w2[:, e % 2], ins["W2"][e]).then_inc(ew_in[e % 2], 16)

        def moe_tensor(pe):
            pe.wait_ge(S["ln_out"], 4 * NT + 1)
            turn_tensor(pe, xn, 4, 2, 3)
            turned(pe, 4)
            for t in range(NT):
                for k in range(KD):
                    last = nc.tensor.matmul(B[6][:, t * NE:(t + 1) * NE], xT[:, k, t * P:(t + 1) * P], gate_w[:, k, :],
                                            start=(k == 0), stop=(k == KD - 1))
            last.then_inc(S["gl_ps"], 1)
            pe.wait_ge(S["gate_ready"], 1)
            for t in range(NT):
                last = nc.tensor.transpose(B[7][0:NE + 1, t * P:(t + 1) * P], gated[:, t, :], ident[:, :])
            last.then_inc(S["gate_ps"], 1)
            pe.wait_ge(S["gateT_ready"], 1)
            for t in range(NT):
                last = nc.tensor.matmul(B[4 + t // 2][:, (t % 2) * D:(t % 2 + 1) * D], gatedT[:, t * P:(t + 1) * P],
                                        b2_all[:, :], start=True, stop=True)
                if t % 2:
                    last.then_inc(S["bias_ps"], 1)

            def second(e):
                pe.wait_ge(S["e1_ready"], FC * (e + 1))
                for t in range(NT):
                    n = NT * e + t
                    if n >= 2 * 2:
                        pe.wait_ge(S["e2_used"], n - 3)
                    elif n == 0:
                        pe.wait_ge(S["hid_out"], 2)
                    for k in range(FC):
                        last = nc.tensor.matmul(B[4 + n % 4][:, 0:D], moe_h[:, e % 2, k, t * P:(t + 1) * P],
                                                moe_w2[:, e % 2, k, :], start=(k == 0), stop=(k == FC - 1))
                    last.then_inc(S["e2_ps"], 1)

            for e in range(NU):
                pe.wait_ge(ew_in[e % 2], 32 * (e // 2 + 1))
                for c in range(FC):
                    n = FC * e + c
                    if n >= 4:
                        pe.wait_ge(S["e1_ready"], n - 3)
                    for k in range(KD):
                        last = nc.tensor.matmul(B[n % 4][:, :], moe_w1[:, e % 2, k, c * P:(c + 1) * P], xT[:, k, :],
                                                start=(k == 0), stop=(k == KD - 1))
                    last.then_inc(S["e1_ps"], 1)
                if e:
                    second(e - 1)
            second(NU - 1)

        def moe_scalar(act, c):
            turn_scalar(act, xT, 4, 2, 3)
            act.wait_ge(S["gl_ready"], 1)
            nc.scalar.activation(ge, gl, ACT.Exp).then_inc(S["gl_exp"], 1)
            act.wait_ge(S["gate_ps"], 1)
            nc.scalar.copy(gatedT, B[7][0:NE + 1, :]).then_inc(S["gateT_ready"], 1)
            for e in range(NU):
                for k in range(FC):
                    n = FC * e + k
                    act.wait_ge(S["e1_ps"], n + 1)
                    if e >= 2:
                        act.wait_ge(S["e2_ps"], NT * (e - 1))
                    nc.scalar.activation(moe_h[:, e % 2, k, :], B[n % 4][:, :], ACT.Gelu,
                                         bias=b1_all[:, e, k:k + 1]).then_inc(S["e1_ready"], 1)

        def moe_vector(dve, v):
            V = nc.vector
            dve.wait_ge(S["ln_out"], 4 * NT + 1)
            v.step(V.tensor_tensor(hid[:, :, :], hid[:, :, :], xn[:, :, :], ALU.add))
            v.step(V.memset(garr, -1.0))
            v.step(V.memset(gtake, -1.0))
            v.step(V.memset(gated, 1.0))
            dve.wait_ge(S["gl_ps"], 1)
            v.link(V.tensor_tensor(gl, B[6][:, 0:NT * NE].rearrange("p (t e) -> p t e", t=NT),
                                   spread(gate_b[:, :], 1, NT), ALU.add))
            v.link(V.tensor_reduce(gm, gl, AX_X, ALU.max))
            V.tensor_tensor(gl, gl, spread(gm, 2, NE), ALU.subtract).then_inc(S["gl_ready"], 1)
            dve.wait_ge(S["gl_exp"], 1)
            v.link(V.tensor_reduce(gs, ge, AX_X, ALU.add))
            v.link(V.reciprocal(gr, gs))
            v.link(V.tensor_tensor(garr[:, :, 0:NE], ge, spread(gr, 2, NE), ALU.mult))
            v.link(V.tensor_copy(ge, garr[:, :, 0:NE]))
            for t in range(NT):
                v.step(V.max(gtop[:, t, :], garr[:, t, :]))
            v.settle()
            v.link(V.tensor_copy(gtake[:, :, 0:3], gtop[:, :, 0:3]))
            for t in range(NT):
                v.step(V.match_replace(garr[:, t, :], gtake[:, t, :], garr[:, t, :], -2.0))
            v.settle()
            V.scalar_tensor_tensor(gated[:, :, 0:NE], garr[:, :, 0:NE], -2.0, ge, ALU.is_equal, ALU.mult)\
                .then_inc(S["gate_ready"], 1)
            for half in range(2):
                dve.wait_ge(S["bias_ps"], half + 1)
                t2 = slice(2 * half, 2 * half + 2)
                V.tensor_tensor(hid[:, t2, :], hid[:, t2, :], B[4 + half][:, :].rearrange("p (t c) -> p t c", t=2),
                                ALU.add).then_inc(S["hid_out"], 1)
            dve.wait_ge(S["hid_out"], 2)
            for e in range(NU):
                for t in range(NT):
                    n = NT * e + t
                    dve.wait_ge(S["e2_ps"], n + 1)
                    if e:
                        dve.wait_ge(S["e2_used"], n - NT + 1)
                    gate = gated[:, t, e:e + 1] if e < NE else 1.0
                    V.scalar_tensor_tensor(hid[:, t, :], B[4 + n % 4][:, 0:D], gate, hid[:, t, :],
                                           ALU.mult, ALU.add).then_inc(S["e2_used"], 1)

        def finish_sequence(eng, b):
            eng.sem_inc(iter_done, 1)
            eng.wait_ge(go_on, b + 1)

        E, A_, PE_, S_, M_ = (c in stages for c in "EAPSM")

        @block.sync
        def _(sp):
            setup_sync(sp)
            with sp.Fori(0, BATCH) as b:
                if E:
                    embed_sync(sp, b)
                if A_:
                    attn_sync(sp)
                if PE_:
                    peer_sync(sp)
                if M_:
                    moe_sync(sp)
                sp.wait_ge(iter_done, 1)
                sp.dma_start(out[bass.ds(b, 1)].rearrange("a (t p) c -> p (a t) c", p=P), hid[:, :, :])\
                    .then_inc(S["stored"], 16)
                sp.wait_ge(S["stored"], 16)
                sp.wait_ge(iter_done, 4)
                for n in names:
                    sp.sem_clear(S[n])
                sp.sem_clear(iter_done)
                sp.sem_inc(go_on, 1)

        @block.gpsimd
        def _(pool):
            pool.wait_ge(made, 5)
            with pool.Fori(0, BATCH) as b:
                if E:
                    embed_gpsimd(pool)
                if A_:
                    attn_gpsimd(pool)
                pool.wait_ge(iter_done, 1)
                finish_sequence(pool, b)

        @block.tensor
        def _(pe):
            setup_tensor(pe)
            pe.wait_ge(made, MADE)
            with pe.Fori(0, BATCH) as b:
                if E:
                    embed_tensor(pe)
                if A_:
                    pe.wait_ge(S["ln_out"], NT)
                    turn_tensor(pe, xn, 0, 0, 1)
                    attn_tensor(pe)
                if PE_:
                    peer_tensor(pe)
                if S_:
                    ssm_tensor(pe)
                if M_:
                    moe_tensor(pe)
                pe.wait_ge(iter_done, 1)
                finish_sequence(pe, b)

        @block.scalar
        def _(act):
            setup_scalar(act)
            act.wait_ge(made, MADE)
            with act.Fori(0, BATCH) as b:
                c = Chain(act, S["act_step"])
                if E:
                    embed_scalar(act)
                if A_:
                    norm_scalar(act, 0)
                    turn_scalar(act, xT, 0, 0, 1)
                    attn_scalar(act, c)
                if PE_:
                    norm_scalar(act, 1)
                    peer_scalar(act, c)
                if S_:
                    norm_scalar(act, 2)
                    ssm_scalar(act, c)
                if M_:
                    norm_scalar(act, 3)
                    moe_scalar(act, c)
                act.wait_ge(iter_done, 1)
                finish_sequence(act, b)

        @block.vector
        def _(dve):
            setup_vector(dve)
            dve.wait_ge(made, MADE)
            with dve.Fori(0, BATCH) as b:
                v = Chain(dve, S["dve_step"])
                if E:
                    embed_vector(dve, v, b)
                if A_:
                    norm_vector(dve, v, 0)
                    attn_vector(dve, v)
                if PE_:
                    norm_vector(dve, v, 1)
                    peer_vector(dve, v)
                if S_:
                    norm_vector(dve, v, 2)
                    ssm_vector(dve, v)
                if M_:
                    norm_vector(dve, v, 3)
                    moe_vector(dve, v)
                    dve.wait_ge(S["e2_used"], NT * NU)
                finish_sequence(dve, b)


def kernel(**inputs):
    import concourse.bacc as _bacc
    from concourse.bass_utils import run_bass_kernel_spmd as _run

    nc = _bacc.Bacc("TRN2", target_bir_lowering=False, num_devices=1)
    arrays = arrange(inputs)
    ins = {n: nc.dram_tensor(f"in_{n}", a.shape, mybir.dt.from_np(a.dtype), kind="ExternalInput").ap()
           for n, a in arrays.items()}
    out = nc.dram_tensor("out_0", (BATCH, T, D), F32, kind="ExternalOutput").ap()
    build(nc, ins, out)
    r = _run(nc, [{f"in_{n}": a for n, a in arrays.items()}], core_ids=[0])
    return r.results[0]["out_0"]


def arrange(inputs):
    g = {n: np.asarray(a) for n, a in inputs.items()}
    a, p, q, m = (lambda n, pre=pre: g[pre + n] for pre in ("L0_attn_", "L0_ffn_", "L1_attn_", "L1_ffn_"))
    cols = lambda v: v.reshape(-1, P).T
    z = {"x": g["x"].reshape(BATCH, NT, P).transpose(0, 2, 1)}
    for i in range(4):
        z[f"emb{i}"] = g[f"L0_tok_emb{i}"]
    z["proj"] = np.concatenate([g["L0_tok_proj1"], g["L0_tok_proj2"], g["L0_tok_proj3"]])
    for n in "qkv":
        z[f"{n}_wT"] = a(f"{n}_w").T
        z[f"{n}_cw"] = a(f"{n}_cw")
    z["b_wT"] = a("b_w").T
    z["fir_short"] = a("fir_short_w").reshape(D, SHORT)
    z["fir_long"] = np.zeros((D, 3 * LONG), np.float32)
    z["fir_long"][:, LONG:2 * LONG] = a("fir_long_w").reshape(D, LONG)[:, ::-1]
    z["mlp1_aT"] = a("mlp1_w")[:, :D].T
    z["mlp1_sT"] = np.zeros((H, H * 16, D), np.float32)
    for h in range(H):
        z["mlp1_sT"][h, 16 * h:16 * h + 16] = a("mlp1_w")[:, D:].T
    z["mlp1_b"], z["mlp2_wT"], z["mlp2_b"] = cols(a("mlp1_b")), a("mlp2_w").T, a("mlp2_b")
    z["logit_temp"], z["conv_res"], z["norm_w"], z["o_wT"] = a("logit_temp"), a("conv_res_logit"), a("norm_w"), a("o_w").T
    z["gamma"], z["wq"] = p("gamma"), p("wq")
    z["keysT"] = p("keys").transpose(2, 0, 3, 1).reshape(2 * PH, P, NK)
    rows = lambda t: t[:NX].reshape(NK, YC, 2, D).transpose(1, 2, 0, 3).reshape(XC, P, D)
    z["downT"] = rows(p("table_down")).reshape(XC, P, KD, P).transpose(3, 0, 2, 1)
    z["up"] = rows(p("table_up")).transpose(1, 0, 2)
    z["W_inT"], z["b_in"], z["W_BT"], z["W_CT"] = q("W_in").T, cols(q("b_in")), q("W_B").T, q("W_C").T
    z["D"], z["W_outT"], z["b_out"] = cols(q("D")), q("W_out").T, q("b_out")
    z["gW"], z["gb"] = m("gW"), m("gb")
    w1 = np.concatenate([m("rW1"), m("sW1").reshape(D, 2, FF).transpose(1, 0, 2)])
    w2 = np.concatenate([m("rW2"), m("sW2").reshape(2, FF, D)])
    z["W1"] = w1.reshape(NU, KD, P, FF).transpose(0, 2, 1, 3)
    z["W2"] = w2.reshape(NU, FC, P, D).transpose(0, 2, 1, 3)
    z["b1"] = np.concatenate([m("rb1"), m("sb1").reshape(2, FF)]).reshape(NU, FC, P).transpose(2, 0, 1)
    z["b2"] = np.concatenate([m("rb2"), m("sb2")])
    z["c_ident"] = np.eye(P, dtype=np.float32)
    i, j = np.arange(P)[:, None], np.arange(P)[None, :]
    z["c_levels"] = np.stack([((i >> (lv + 1)) == (j >> (lv + 1))) & ((i >> lv) & 1 == 0) & ((j >> lv) & 1 == 1)
                              for lv in range(LEVELS)]).astype(np.float32)
    z["c_causal"] = (i <= j).astype(np.float32)
    z["c_flips"] = np.stack([i + j == P - 1, i + j == P // 2 - 1, i + j == P + P // 2 - 1], 1).astype(np.float32)
    z["c_iota"] = np.arange(P, dtype=np.float32)
    z["c_rows"] = np.stack([np.arange(TOPK), ROWAT, [0] + ROWLEN[:-1]]).astype(np.float32)
    return {n: np.ascontiguousarray(v) for n, v in z.items()}
```

```python
from contextlib import ExitStack

import numpy as np

import concourse.bass as bass
from concourse import mybir

F32 = mybir.dt.float32
BF16 = mybir.dt.bfloat16
I32 = mybir.dt.int32
U32 = mybir.dt.uint32
ALU = mybir.AluOpType
ACT = mybir.ActivationFunctionType
AX_X = mybir.AxisListType.X

P = 128
BATCH, T = 4, 512
NT = T // P
D = 256
KD = D // P
CUTOFFS = [0, 5000, 10000, 50000, 267735]
EMB = [D // 4**i for i in range(4)]
EMB_AT = [sum(EMB[:i]) for i in range(4)]
EMB_ALL = sum(EMB)
EMB_LOW = EMB_ALL - D
H, DH = 4, 64
TAPS, SHORT, LONG = 4, 5, 64
PH, NK, TOPK = 8, 64, 16
NX = NK * NK
XC = NX // P
YC = NK // 2
ROWLEN = [TOPK // (i + 1) for i in range(TOPK)]
ROWAT = [sum(ROWLEN[:i]) for i in range(TOPK)]
PAIRS = sum(ROWLEN)
TB = 16
DI, DS = 512, 16
NE, FF = 15, 512
FC = FF // P
TAKE = 3
N_TOK = BATCH * T
TILE = 256
HALF = TILE // P
TILES = (N_TOK * TAKE + NE * (TILE - 1)) // TILE
REGION = TILE + N_TOK
RING = 3
LEVELS = 7
LOWEST = -3.0e38
HEAD_ORDER = [0, 2, 1, 3]


class Chain:

    def __init__(self, eng, sem):
        self.eng, self.sem, self.n = eng, sem, 0

    def step(self, ins):
        ins.then_inc(self.sem, 1)
        self.n += 1

    def settle(self):
        self.eng.wait_ge(self.sem, self.n)

    def link(self, ins):
        self.step(ins)
        self.settle()


class Arena:

    def __init__(self, tensor, at, end):
        self.tensor, self.at, self.end = tensor, at, end

    def take(self, *shape, dtype=F32, parts=P):
        n = int(np.prod(shape))
        words = n if dtype != BF16 else n // 2
        view = self.tensor[0:parts, self.at:self.at + words]
        self.at += words
        assert self.at <= self.end, (self.at, self.end)
        if dtype != F32:
            view = view.bitcast(dtype)
        names = "abcde"[:len(shape)]
        if len(shape) > 1:
            sizes = {c: s for c, s in zip(names, shape)}
            view = view.rearrange(f"p ({' '.join(names)}) -> p {' '.join(names)}", **sizes)
        return view


def spread(ap, axis, n):
    shape = list(ap.shape)
    shape.insert(axis, n)
    return ap.unsqueeze(axis).broadcast_to(shape)


def build(nc, ins, out, stages="EAPSM"):
    ctx = ExitStack()
    with ctx:
        def sb(name, shape, dt=F32):
            return ctx.enter_context(nc.sbuf_tensor(name, shape, dt))

        def sem(name):
            return ctx.enter_context(nc.semaphore(name))

        B = [ctx.enter_context(nc.psum_tensor(f"bank{i}", [P, 512], F32)) for i in range(8)]

        w_qkv = sb("w_qkv", [P, 3, KD, D])
        w_beta = sb("w_beta", [P, KD, H])
        conv_w = sb("conv_w", [P, 3 * KD, TAPS])
        short_w = sb("short_w", [P, KD, SHORT])
        mlp1_a = sb("mlp1_a", [P, KD, D])
        mlp1_s = sb("mlp1_s", [H * 16, H, D])
        mlp1_b = sb("mlp1_b", [P, KD])
        mlp2_w = sb("mlp2_w", [P, KD, 4])
        mlp2_b = sb("mlp2_b", [P, 4])
        temp = sb("temp", [P, 4])
        res_gate = sb("res_gate", [P, H])
        norm_w = sb("norm_w", [P, DH])
        o_w = sb("o_w", [P, KD, D])
        proj = sb("proj", [EMB_LOW, D])
        gamma = sb("gamma", [P, D])
        w_sim = sb("w_sim", [P, KD, 2 * PH * NK])
        w_in = sb("w_in", [P, KD, 2 * DI])
        b_in = sb("b_in", [P, 2 * DI // P])
        w_B = sb("w_B", [P, DI // P, DS])
        w_C = sb("w_C", [DS, DI])
        skip_D = sb("skip_D", [P, DI // P])
        w_out = sb("w_out", [P, DI // P, D])
        b_out = sb("b_out", [P, D])
        gate_w = sb("gate_w", [P, KD, NE])
        gate_b = sb("gate_b", [P, NE])
        b1_shared = sb("b1_shared", [P, 2, FC])
        tile_no = sb("tile_no", [P, TILES])
        region_at = sb("region_at", [P, NE])
        strict = sb("strict", [P, P], BF16)
        ones_b = sb("ones_b", [P, P], BF16)
        restart = sb("restart", [P, NT, NE])
        all_hot = sb("all_hot", [P, BATCH * NT, TAKE, NE])
        all_rank = sb("all_rank", [P, BATCH * NT, TAKE])
        all_gate = sb("all_gate", [P, BATCH * NT, TAKE])
        count = sb("count", [P, NE])
        b2_all = sb("b2_all", [NE + 1, D])
        ident = sb("ident", [P, P])
        level_mask = sb("level_mask", [P, LEVELS, P])
        causal = sb("causal", [P, P])
        flips = sb("flips", [P, 3, P])
        iota_x = sb("iota_x", [P, P, TB], BF16)
        iota_y = sb("iota_y", [P, YC, TB], BF16)
        decay = sb("decay", [DS, T])

        hid = sb("hid", [P, NT, D])
        xn = sb("xn", [P, NT, D])
        xT = sb("xT", [P, KD, T])
        ids = sb("ids", [P, NT], I32)
        ids_f = sb("ids_f", [P, NT])
        id_low = sb("id_low", [P, 4, NT])
        id_ge = sb("id_ge", [P, 4, NT])
        id_mask = sb("id_mask", [P, 4, NT])
        id_row = sb("id_row", [P, 4, NT], U32)
        ln_part = sb("ln_part", [P, NT, 6])
        ln_mv = sb("ln_mv", [P, NT, 2])
        ln_ve = sb("ln_ve", [P, NT])
        ln_sd = sb("ln_sd", [P, NT])
        ln_r = sb("ln_r", [P, NT])

        base_d = nc.dram_tensor("base_d", (BATCH, P, NT, D), F32).ap()
        rows_d = nc.dram_tensor("rows_d", (NE * REGION, D), F32).ap()
        outs_d = nc.dram_tensor("outs_d", (TILES * TILE, D), F32).ap()

        ARENA = 35040
        arena_t = sb("arena", [P, ARENA])

        loads = sem("loads")
        made = sem("made")
        iter_done = sem("iter_done")
        go_on = sem("go_on")
        names = [
            "dve_step", "act_step", 
            "ids_in", "rows_ready", "low_ready", "low_ps", "lowT_ready", "proj_ps",
            "ln_var", "ln_std", "ln_out", "turn_ps", "turn_sb",
            "toep_in0", "toep_in1", "toep_in2", "toep_in3", 
            "qkv_ps", "pre_ready", "conv_ready", "silu_ready", "beta_ps", "beta_ready", "tok_ps", "tok_ready",
            "ss_ready", "ss_root", "unit_ready", "unitT_ps", "unitT_ready", "window_ps", "window_ready",
            "short_ready", "short_ps", "short_tok", "fir_ps", "fir_ready",
            "gram_ps", "gram_ready", "lm_ready", "u0_ready", "t0_ps", "t0_ready", "p_ps", "p_ready",
            "d_ps", "tu_ready", "w_ps", "w_ready", "attn_ps", "attn_ready", "ua_ps", "ua_ready",
            "do_ps", "do_ready", "ds_ps", "ds_ready",
            "l2_ready", "l2_root", "stat_ready", "stat_ps", "statT_ready", "h1_ps", "h1_ready", "h1_all_ps", "h1_all", "h1_sum", "logit_ps",
            "lg_ready", "lg_exp", "mix_ss", "mix_root", "mix_ready", "o_ps", 
            "xss_ready", "xss_root", "sim_ps", "sim_ready", "sim_used", "score_ready", "score_exp", "entry_ready",
            "entry_ps", "hot_ready", "cell_ps", "cell_ready",
            "tab_in0", "tab_in1", "up_in", "shared_in", "down_ps", "down_act", "up_ps", "hid_peer",
            "xz_ps", "xz_ready", "state_ps", "state_ready", "c_ps", "y_ready", "so_ps",
            "gl_ps", "gl_ready", "gl_exp", "gate_ready", "gate_ps", "gateT_ready", 
            "e1_ps", "e1_ready", "e2_ps", "e2_used", "bias_ps", "hid_out",
            "sel_ready", "rank_ps", "slot_ready",
        ]
        scattered = sem("scattered")
        routed = sem("routed")
        mix_step = sem("mix_step")
        padded = sem("padded")
        rw_in = [sem(f"rw_in{p}") for p in range(RING)]
        x_in = [sem(f"x_in{p}") for p in range(RING)]
        xt_ps, xt_ready, m1_ps, m1_ready, m2_ps, m2_ready = (
            sem(n) for n in ("xt_ps", "xt_ready", "m1_ps", "m1_ready", "m2_ps", "m2_ready"))
        y_stored = [sem(f"y_stored{p}") for p in range(RING)]
        base_in, mixed, final_out = (sem(n) for n in ("base_in", "mixed", "final_out"))
        gathered = [sem(f"gathered{b}") for b in range(BATCH)]
        S = {n: sem(n) for n in names + ["stored"]}
        attn_names = names[names.index("toep_in0"):names.index("xss_ready")]
        peer_names = [n for n in names[names.index("xss_ready"):names.index("xz_ps")] if n not in ("up_ps", "shared_in")]
        first_ids, first_step, first_rows = (sem(n) for n in ("first_ids", "first_step", "first_rows"))
        zeros_ready = sem("zeros_ready")
        rows_in = sem("rows_in")


        toep_in, tab_in = [S[f"toep_in{q}"] for q in range(4)], (S["tab_in0"], S["tab_in1"])

        block = ctx.enter_context(nc.Block())

        a = Arena(arena_t, 0, ARENA)
        feats = a.take(NT, 4, D)
        win = a.take(2 * NT, D)
        vpad = a.take(KD, T + SHORT - 1)
        qk_tok = a.take(2, NT, D)
        kb = a.take(NT, D)
        vb = a.take(NT, D)
        unitT = a.take(3, KD, T)
        beta = a.take(NT * H)
        ss = a.take(2 * NT * H)
        ss_sd = a.take(2 * NT * H)
        unit = a.take(2 * NT * H)
        early = a.at
        zeros = kb[:, 0:HALF]
        a = Arena(arena_t, early, ARENA)
        pre = a.take(3 * KD, T + TAPS - 1)
        conv = a.take(3 * KD, T)
        toep = [a.take(64, 64) for _ in range(3)] + [Arena(arena_t, early, ARENA).take(64, 64)]
        sq = a.take(2, NT, D)
        a = Arena(arena_t, early, ARENA)
        neg_wT = a.take(NT, KD, P)
        u_adj = a.take(D)
        state = a.take(KD, DH)
        stats = a.take(NT, H, 4, 4)
        st_sum, st_abs, st_css, st_mean2, st_l2 = (a.take(NT, 4, H) for _ in range(5))
        stats_mean = a.take(NT, 4, H)
        statT = a.take(T, parts=H * 16)
        lg, lg_e, lg_p = (a.take(NT, H, 4) for _ in range(3))
        lg_m, lg_s, lg_r = (a.take(NT, H) for _ in range(3))
        attn_m = a.take(2, H, P)
        cent = a.take(NT, 4 * H, DH)
        short_T = a.take(KD, T)
        scratch = a.at
        T_m = a.take(NT, H, P)
        U_m = a.take(NT, H, P)
        M_T = a.take(NT, H, P)
        L_T = a.take(NT, H, P)
        P_m = win[:, :, :].rearrange("p w c -> p (w c)").rearrange("p (t h c) -> p t h c", t=NT, h=H)
        a = Arena(arena_t, scratch, ARENA)
        h1 = a.take(2, KD, T)
        h1_all = a.take(KD, T)
        mix = cent[:, :, :, :].rearrange("p t (k h) d -> p t k h d", k=4)
        o_tok = h1[:, :, :, :].rearrange("p a b c -> p (a b c)")[:, 0:NT * D].rearrange("p (t c) -> p t c", t=NT)
        o_sq = h1[:, :, :, :].rearrange("p a b c -> p (a b c)")[:, NT * D:2 * NT * D].rearrange("p (t c) -> p t c", t=NT)
        oT = short_T

        embed = Arena(arena_t, early, ARENA)
        rows = embed.take(NT, EMB_ALL)
        low = embed.take(NT, EMB_LOW)
        lowT = embed.take(T, parts=EMB_LOW)

        a = Arena(arena_t, 0, ARENA)
        grid = a.take(XC, T)
        entT_x = a.take(T, dtype=BF16)
        entT_y = a.take(T, dtype=BF16)
        entT_w = a.take(3, T, dtype=BF16)
        hot_at = a.at
        hots = [(a.take(P, TB, dtype=BF16), a.take(YC, TB, dtype=BF16), a.take(3, YC, TB, dtype=BF16))
                for _ in range(2)]
        tab_u = a.take(XC, D)
        tab_end = a.at
        tab_d = Arena(arena_t, ARENA - 2 * 2 * D, ARENA).take(2, 2, KD, P)
        a = Arena(arena_t, hot_at, tab_end)
        sim = a.take(2, 2 * PH, NK)
        cand = a.take(NT * PH, PAIRS)
        look = Arena(arena_t, hot_at, tab_end).take(TOPK, TOPK * NT * PH, dtype=BF16)
        a.at = max(a.at, hot_at + TOPK * TOPK * NT * PH // 2)
        xx = Arena(arena_t, hot_at, ARENA).take(NT, D)
        w_rest = Arena(arena_t, hot_at, ARENA).take(T)
        w_rest2 = Arena(arena_t, hot_at + T, ARENA).take(T)
        val = a.take(2, NT, PH, TOPK)
        key = a.take(2, NT, PH, TOPK, dtype=U32)
        top = a.take(NT * PH, TOPK)
        pos = a.take(NT * PH, TOPK, dtype=U32)
        e_w = a.take(NT * PH, TOPK)
        e_x, e_y, e_far, e_gate = (a.take(NT, TOPK, PH) for _ in range(4))
        e_s = a.take(NT * PH)
        e_r = a.take(NT * PH)
        keyx, keyy, key_d, pos_b, col_b = (a.take(TOPK, NT * PH, dtype=BF16) for _ in range(5))
        x_sq, x_sd, x_r = a.take(NT), a.take(NT), a.take(NT)

        a = Arena(arena_t, 0, ARENA)
        xz = a.take(2 * DI // P, T)
        y = a.take(DI // P, T)
        drive = a.take(T, parts=DS)
        states = a.take(T, parts=DS)

        a = Arena(arena_t, 0, ARENA)
        gl = a.take(NT, NE)
        gm = a.take(NT)
        ge = a.take(NT, NE)
        gs, gr = a.take(NT), a.take(NT)
        garr = a.take(NT, NE + 5)
        gtop = a.take(NT, 8)
        gtake = a.take(NT, 8)
        gated = a.take(NT, NE + 1)
        gatedT = a.take(T, parts=NE + 1)
        moe_h = a.take(2, FC, T)
        assert a.at <= 8192
        a.at = 8192
        w1_shared = a.take(2, KD, FF)
        w2_shared = a.take(2, FC, D)
        sel, nth, rank, slot = (a.take(NT, NE) for _ in range(4))
        sel_b = a.take(NT, NE + 1, dtype=BF16)
        hot3 = a.take(NT, TAKE, NE)
        pick3 = a.take(NT, TAKE, NE)
        rank3, slot3, gate3 = (a.take(NT, TAKE) for _ in range(3))
        slot_u = a.take(NT, TAKE, dtype=U32)

        a = Arena(arena_t, 0, ARENA)
        r_w1 = a.take(RING, KD, FF)
        r_w2 = a.take(RING, FC, D)
        r_b1 = a.take(RING, FC)
        r_x = a.take(RING, HALF, D)
        r_xT = a.take(RING, KD, TILE)
        r_h = a.take(RING, FC, TILE)
        spent = a.at
        r_y = a.take(RING, HALF, D)
        n_tiles, t_start, t_sum, t_ahead, t_row0, t_jump = (a.take(NE) for _ in range(6))
        t_step = a.take(1)
        t_int = a.take(NE, dtype=I32)
        one_row = a.take(NE)
        t_ge = a.take(TILES, NE)
        t_gs = a.take(TILES, NE)
        t_exp, t_min, t_row = (a.take(TILES) for _ in range(3))
        tile_exp = a.take(TILES, dtype=I32)
        tile_row = a.take(TILES, dtype=I32)
        y_pick = a.take(BATCH * NT, TAKE, NE)
        y_slot = a.take(BATCH * NT, TAKE)
        y_slot_u = a.take(BATCH * NT, TAKE, dtype=U32)
        f_base = a.take(BATCH * NT, D)
        f_rows = Arena(arena_t, 0, spent).take(BATCH * NT, TAKE, D)

        n_loads = [0]

        def load(eng, dst, src):
            eng.dma_start(dst, src).then_inc(loads, 16)
            n_loads[0] += 16

        def setup_sync(sp):
            for i, n in enumerate(("q_wT", "k_wT", "v_wT")):
                load(sp, w_qkv[:, i], ins[n].rearrange("(k p) n -> p k n", p=P))
            load(sp, w_beta[:, :, :], ins["b_wT"].rearrange("(k p) n -> p k n", p=P))
            for i, n in enumerate(("q_cw", "k_cw", "v_cw")):
                load(sp, conv_w[:, KD * i:KD * (i + 1), :], ins[n].rearrange("(k p) n -> p k n", p=P))
            load(sp, short_w[:, :, :], ins["fir_short"].rearrange("(k p) n -> p k n", p=P))
            load(sp, mlp1_a[:, :, :], ins["mlp1_aT"].rearrange("(k p) n -> p k n", p=P))
            load(sp, mlp1_s[:, :, :], ins["mlp1_sT"].rearrange("h p n -> p h n"))
            load(sp, mlp1_b[:, :], ins["mlp1_b"])
            load(sp, mlp2_w[:, :, :], ins["mlp2_wT"].rearrange("(k p) n -> p k n", p=P))
            load(sp, mlp2_b[:, :], ins["mlp2_b"].partition_broadcast(P))
            load(sp, temp[:, 0:1], ins["logit_temp"].partition_broadcast(P))
            load(sp, res_gate[:, :], ins["conv_res"].partition_broadcast(P))
            load(sp, norm_w[:, :], ins["norm_w"].partition_broadcast(P))
            load(sp, o_w[:, :, :], ins["o_wT"].rearrange("(k p) n -> p k n", p=P))
            load(sp, proj[:, :], ins["proj"])
            load(sp, gamma[:, :], ins["gamma"].partition_broadcast(P))
            load(sp, w_in[:, :, :], ins["W_inT"].rearrange("(k p) n -> p k n", p=P))
            load(sp, b_in[:, :], ins["b_in"])
            load(sp, w_B[:, :, :], ins["W_BT"].rearrange("(k p) n -> p k n", p=P))
            load(sp, w_C[:, :], ins["W_CT"])
            load(sp, skip_D[:, :], ins["D"])
            load(sp, w_out[:, :, :], ins["W_outT"].rearrange("(k p) n -> p k n", p=P))
            load(sp, b_out[:, :], ins["b_out"].partition_broadcast(P))
            load(sp, gate_w[:, :, :], ins["gW"].rearrange("(k p) n -> p k n", p=P))
            load(sp, gate_b[:, :], ins["gb"].partition_broadcast(P))
            load(sp, b1_shared[:, :, :], ins["b1"][NE:NE + 2].rearrange("e p k -> p e k"))
            load(sp, tile_no[:, :], ins["c_iota"][0:TILES].partition_broadcast(P))
            load(sp, region_at[:, :], ins["c_region"].partition_broadcast(P))
            load(sp, restart[:, :, :].rearrange("p t e -> p (t e)"), ins["c_restart"].partition_broadcast(P))
            load(sp, b2_all[:, :], ins["b2"])
            load(sp, ident[:, :], ins["c_ident"])
            load(sp, level_mask[:, :, :], ins["c_levels"].rearrange("l p n -> p l n"))
            load(sp, causal[:, :], ins["c_causal"])
            load(sp, flips[:, :, :], ins["c_flips"])
            load(sp, iota, ins["c_iota"].partition_broadcast(P))
            load(sp, wq_sb, ins["wq"].rearrange("(c p) n -> p c n", p=P))
            load(sp, keys_sb, ins["keysT"].rearrange("c p n -> p c n"))
            sp.wait_ge(zeros_ready, 1)
            for e in range(NE):
                sp.dma_start(rows_d[e * REGION:e * REGION + TILE].rearrange("(h p) c -> p h c", p=P), zeros)\
                    .then_inc(padded, 16)

        a = Arena(arena_t, 0, ARENA)
        wq_sb = a.take(2 * PH, D)
        keys_sb = a.take(2 * PH, NK)
        iota = a.take(P)

        def setup_tensor(pe):
            pe.wait_ge(loads, n_loads[0])
            for c in range(2 * PH):
                for k in range(KD):
                    last = nc.tensor.matmul(B[2 * k + c // PH][:, (c % PH) * NK:(c % PH + 1) * NK],
                                            wq_sb[:, c, k * P:(k + 1) * P], keys_sb[:, c, :],
                                            start=True, stop=True)
            last.then_inc(made, 1)

        def setup_scalar(act):
            act.wait_ge(loads, n_loads[0])
            act.wait_ge(made, 1)
            for k in range(KD):
                for half in range(2):
                    nc.scalar.copy(w_sim[:, k, half * 512:(half + 1) * 512], B[2 * k + half][:, :]).then_inc(made, 1)
            nc.scalar.activation(temp[:, 1:2], temp[:, 0:1], ACT.Abs).then_inc(made, 1)
            act.wait_ge(made, 6)
            nc.scalar.activation(temp[:, 2:3], temp[:, 1:2], ACT.Exp, scale=-1.0).then_inc(made, 1)
            act.wait_ge(made, 7)
            nc.scalar.activation(temp[:, 3:4], temp[:, 2:3], ACT.Ln, bias=1.0).then_inc(made, 1)
            nc.scalar.activation(res_gate[:, :], res_gate[:, :], ACT.Sigmoid).then_inc(made, 1)

        def setup_vector(dve):
            dve.wait_ge(loads, n_loads[0])
            dve.wait_ge(made, 9)
            nc.vector.scalar_tensor_tensor(temp[:, 1:2], temp[:, 0:1], 0.0, temp[:, 3:4],
                                           ALU.max, ALU.add).then_inc(made, 1)
            dve.wait_ge(made, 10)
            nc.vector.reciprocal(temp[:, 0:1], temp[:, 1:2]).then_inc(made, 1)
            nc.vector.memset(decay[:, :], 0.9).then_inc(made, 1)
            nc.vector.tensor_copy(iota_x[:, :, :], spread(iota, 2, TB)).then_inc(made, 1)
            nc.vector.tensor_copy(iota_y[:, :, :], spread(iota[:, 0:YC], 2, TB)).then_inc(made, 1)

            nc.vector.tensor_tensor(strict[:, :], causal[:, :], ident[:, :], ALU.subtract).then_inc(made, 1)
            nc.vector.memset(ones_b[:, :], 1.0).then_inc(made, 1)
            nc.vector.memset(count[:, :], 0.0).then_inc(made, 1)

        MADE = 17
        inv_temp = temp[:, 0:1]

        def ids_sync(sp, b, ids_in):
            sp.dma_start(ids[:, :], ins["x"][bass.ds(b, 1)].rearrange("a p t -> p (a t)")).then_inc(ids_in, 16)

        def ids_vector(dve, v, ids_in, rows_ready):
            dve.wait_ge(ids_in, 16)
            v.link(nc.vector.tensor_copy(ids_f[:, :], ids[:, :]))
            for i in range(4):
                lo, hi = CUTOFFS[i], CUTOFFS[i + 1]
                v.step(nc.vector.tensor_scalar(id_low[:, i], ids_f[:, :], float(-lo), 0.0, ALU.add, ALU.max))
                v.step(nc.vector.tensor_scalar(id_ge[:, i], ids_f[:, :], float(lo), None, ALU.is_ge))
            v.settle()
            for i in range(4):
                lo, hi = CUTOFFS[i], CUTOFFS[i + 1]
                v.step(nc.vector.scalar_tensor_tensor(id_mask[:, i], ids_f[:, :], float(hi), id_ge[:, i],
                                                      ALU.is_lt, ALU.mult))
                nc.vector.tensor_scalar(id_row[:, i], id_low[:, i], float(hi - lo - 1), None,
                                        ALU.min).then_inc(rows_ready, 1)
            v.settle()

        def gather_rows(pool):
            for t in range(NT):
                for i in range(4):
                    nc.gpsimd.indirect_dma_start(
                        rows[:, t, EMB_AT[i]:EMB_AT[i] + EMB[i]], None, ins[f"emb{i}"],
                        bass.IndirectOffsetOnAxis(ap=id_row[:, i, t:t + 1], axis=0)).then_inc(rows_in, 16)

        def embed_vector(dve, v, b):
            dve.wait_ge(rows_in, (b + 1) * (16 * 4 * NT))
            for t in range(NT):
                for i in range(4):
                    dst = hid[:, t, :] if i == 0 else low[:, t, EMB_AT[i] - D:EMB_AT[i] - D + EMB[i]]
                    ins_ = nc.vector.tensor_scalar(dst, rows[:, t, EMB_AT[i]:EMB_AT[i] + EMB[i]],
                                                   id_mask[:, i, t:t + 1], 16.0, ALU.mult, ALU.mult)
                    if i < 3:
                        v.step(ins_)
                    else:
                        ins_.then_inc(S["low_ready"], 1)
            v.settle()
            for half in range(2):
                dve.wait_ge(S["proj_ps"], half + 1)
                t2 = slice(2 * half, 2 * half + 2)
                v.step(nc.vector.tensor_tensor(hid[:, t2, :], hid[:, t2, :],
                                               B[1 + half][:, :].rearrange("p (t c) -> p t c", t=2), ALU.add))
            v.settle()

        def embed_tensor(pe):
            for t in range(NT):
                pe.wait_ge(S["low_ready"], t + 1)
                nc.tensor.transpose(B[0][0:EMB_LOW, t * P:(t + 1) * P], low[:, t, :], ident[:, :]).then_inc(S["low_ps"], 1)
            pe.wait_ge(S["lowT_ready"], 1)
            for t in range(NT):
                nc_i = nc.tensor.matmul(B[1 + t // 2][:, (t % 2) * D:(t % 2 + 1) * D], lowT[:, t * P:(t + 1) * P],
                                        proj[:, :], start=True, stop=True)
                if t % 2:
                    nc_i.then_inc(S["proj_ps"], 1)

        def embed_scalar(act):
            act.wait_ge(S["low_ps"], NT)
            nc.scalar.copy(lowT, B[0][0:EMB_LOW, :]).then_inc(S["lowT_ready"], 1)

        def norm_vector(dve, v, use):
            for t in range(NT):
                v.step(nc.vector.bn_stats(ln_part[:, t, :], hid[:, t, :]))
            v.settle()
            for t in range(NT):
                v.step(nc.vector.bn_aggr(ln_mv[:, t, :], ln_part[:, t, :]))
            v.settle()
            nc.vector.tensor_scalar(ln_ve[:, :], ln_mv[:, :, 1], 1e-5, None, ALU.add).then_inc(S["ln_var"], 1)
            dve.wait_ge(S["ln_std"], use + 1)
            v.link(nc.vector.reciprocal(ln_r[:, :], ln_sd[:, :]))
            for t in range(NT):
                nc.vector.tensor_scalar(xn[:, t, :], hid[:, t, :], ln_mv[:, t, 0:1], ln_r[:, t:t + 1],
                                        ALU.subtract, ALU.mult).then_inc(S["ln_out"], 1)

        def norm_scalar(act, use):
            act.wait_ge(S["ln_var"], use + 1)
            nc.scalar.activation(ln_sd[:, :], ln_ve[:, :], ACT.Sqrt).then_inc(S["ln_std"], 1)

        def turn_tensor(pe, src, turn, first, second):
            for k in range(KD):
                bank = (first, second)[k]
                for t in range(NT):
                    last = nc.tensor.transpose(B[bank][:, t * P:(t + 1) * P], src[:, t, k * P:(k + 1) * P], ident[:, :])
                last.then_inc(S["turn_ps"], 1)

        def turn_scalar(act, dst, turn, first, second):
            for k in range(KD):
                act.wait_ge(S["turn_ps"], KD * turn + k + 1)
                nc.scalar.copy(dst[:, k, :], B[(first, second)[k]][:, :]).then_inc(S["turn_sb"], 1)

        def turned(eng, turn):
            eng.wait_ge(S["turn_sb"], KD * (turn + 1))

        SHORT_AT = (4, 2)

        def attn_sync(sp, b):
            for q in range(4):
                if q == 3:
                    sp.wait_ge(S["low_ready"], NT)
                    ids_sync(sp, b + 1, S["ids_in"])
                    sp.wait_ge(S["tok_ps"], 6)
                f = ins["fir_long"]
                src = bass.AP(tensor=f.tensor, offset=64 * q * 192 + 1, ap=[[1, P], [192, 64], [1, 64]])
                sp.dma_start(toep[q], src).then_inc(toep_in[q], 16)

        def attn_tensor(pe):
            turned(pe, 0)
            for i in range(3):
                for c in range(KD):
                    for k in range(KD):
                        last = nc.tensor.matmul(B[2 * i + c][:, :], w_qkv[:, i, k, c * P:(c + 1) * P], xT[:, k, :],
                                                start=(k == 0), stop=(k == KD - 1))
                    last.then_inc(S["qkv_ps"], 1)
            for t in range(NT):
                for k in range(KD):
                    last = nc.tensor.matmul(B[6][:, t * H:(t + 1) * H], xT[:, k, t * P:(t + 1) * P], w_beta[:, k, :],
                                            start=(k == 0), stop=(k == KD - 1))
            last.then_inc(S["beta_ps"], 1)
            pe.wait_ge(S["pre_ready"], 6)
            for i in range(3):
                pe.wait_ge(S["silu_ready"], KD * (i + 1))
                for half in range(2):
                    for t in range(2 * half, 2 * half + 2):
                        for c in range(KD):
                            src = (conv[:, 2 * i + c, t * P:(t + 1) * P] if i < 2 else
                                   vpad[:, c, SHORT - 1 + t * P:SHORT - 1 + (t + 1) * P])
                            last = nc.tensor.transpose(B[2 * i + half][:, (t % 2) * D + c * P:(t % 2) * D + (c + 1) * P],
                                                       src, ident[:, :])
                    last.then_inc(S["tok_ps"], 1)
            pe.wait_ge(S["tok_ready"], 6)
            v_tok = lambda t: feats[:, t:t + 2, 3, :]
            for n in range(2):
                nc.tensor.matmul(B[n][:, :], flips[:, 0, :], v_tok(2 * n), start=True, stop=True).then_inc(S["window_ps"], 1)
            nc.tensor.matmul(B[2][:, 0:D], flips[:, 1, :], feats[:, 0, 3, :], start=True, stop=True)
            nc.tensor.matmul(B[2][:, D:2 * D], flips[:, 1, :], feats[:, 1, 3, :], start=True, stop=False)
            nc.tensor.matmul(B[2][:, D:2 * D], flips[:, 2, :], feats[:, 0, 3, :], start=False, stop=True)\
                .then_inc(S["window_ps"], 1)
            nc.tensor.matmul(B[3][:, :], flips[:, 1, :], v_tok(2), start=True, stop=False)
            nc.tensor.matmul(B[3][:, :], flips[:, 2, :], v_tok(1), start=False, stop=True).then_inc(S["window_ps"], 1)
            def long_fir(q):
                pe.wait_ge(toep_in[q], 16)
                if q >= 2:
                    pe.wait_ge(S["fir_ready"], 2 * (q - 1))
                for c in range(64):
                    last = nc.tensor.matmul(B[6 + q % 2][0:64, c * 8:(c + 1) * 8], toep[q][:, c, :],
                                            win[:, :, 64 * q + c], start=True, stop=True)
                last.then_inc(S["fir_ps"], 1)

            pe.wait_ge(S["window_ready"], 4)
            pe.wait_ge(S["beta_ready"], 1)
            long_fir(0)
            long_fir(1)
            pe.wait_ge(S["unit_ready"], 1)
            for i in range(3):
                for c in range(KD):
                    for t in range(NT):
                        src = qk_tok[:, i, t, c * P:(c + 1) * P] if i < 2 else kb[:, t, c * P:(c + 1) * P]
                        last = nc.tensor.transpose(B[2 * i + c][:, t * P:(t + 1) * P], src, ident[:, :])
                    last.then_inc(S["unitT_ps"], 1)
            long_fir(2)
            long_fir(3)
            pe.wait_ge(S["unitT_ready"], 6)
            for n in range(4):
                odd = n % 2
                r = slice(64 * odd, 64 * odd + 64)
                for t in range(2 * (n // 2), 2 * (n // 2) + 2):
                    tt = slice(t * P, (t + 1) * P)
                    for c in range(KD):
                        at = (KD * (t % 2) + c) * P
                        last = nc.tensor.matmul(B[n][:, at:at + P], unitT[r, 1, c, tt], unitT[r, 2, c, tt],
                                                start=True, stop=True)
                last.then_inc(S["gram_ps"], 1)
            for t in range(NT):
                pe.wait_ge(S["u0_ready"], t + 1)
                if t >= 2:
                    pe.wait_ge(S["t0_ready"], t - 1)
                for h in range(H):
                    last = nc.tensor.transpose(B[4 + t % 2][:, h * P:(h + 1) * P], U_m[:, t, h, :], ident[:, :])
                last.then_inc(S["t0_ps"], 1)
            for lv in range(1, LEVELS):
                n = (lv - 1) * NT
                for t in range(NT):
                    pe.wait_ge(S["lm_ready"], n + t + 1)
                    if lv == 1:
                        pe.wait_ge(S["t0_ready"], NT)
                    else:
                        pe.wait_ge(S["tu_ready"], n - NT + t + 1)
                    if n + t >= 2:
                        pe.wait_ge(S["p_ready"], n + t - 1)
                    for h in range(H):
                        last = nc.tensor.matmul(B[4 + t % 2][:, h * P:(h + 1) * P], L_T[:, t, h, :], T_m[:, t, h, :],
                                                start=True, stop=True)
                    last.then_inc(S["p_ps"], 1)
                    if t >= 1:
                        delta_products(pe, lv, t - 1)
                    if (lv, t) == SHORT_AT:
                        pe.wait_ge(S["short_ready"], KD)
                        pe.wait_ge(S["fir_ready"], 8)
                        for half in range(2):
                            for u in range(2 * half, 2 * half + 2):
                                for c in range(KD):
                                    at = (u % 2) * D + c * P
                                    last = nc.tensor.transpose(B[6 + half][:, at:at + P],
                                                               short_T[:, c, u * P:(u + 1) * P], ident[:, :])
                            last.then_inc(S["short_ps"], 1)
                delta_products(pe, lv, NT - 1)
            for t in range(NT):
                pe.wait_ge(S["tu_ready"], (LEVELS - 2) * NT + t + 1)
                for h in range(H):
                    r = slice(64 * (h % 2), 64 * (h % 2) + 64)
                    last = nc.tensor.matmul(B[4 + t // 2][r, (t % 2) * D + (h // 2) * P:(t % 2) * D + (h // 2 + 1) * P],
                                            kb[:, t, h * DH:(h + 1) * DH], U_m[:, t, h, :], start=True, stop=True)
                last.then_inc(S["w_ps"], 1)
            for t in range(NT):
                tt = slice(t * P, (t + 1) * P)
                if t == 0:
                    pe.wait_ge(S["w_ready"], NT)
                else:
                    pe.wait_ge(S["ds_ready"], t)
                    pe.wait_ge(S["attn_ready"], 2 * t)
                for h in HEAD_ORDER:
                    r = slice(64 * (h % 2), 64 * (h % 2) + 64)
                    c = h // 2
                    last = nc.tensor.matmul(B[(3, 6)[h % 2]][:, c * P:(c + 1) * P], unitT[r, 1, c, tt],
                                            unitT[r, 0, c, tt], start=True, stop=True)
                last.then_inc(S["attn_ps"], 1)
                for h in HEAD_ORDER:
                    r = slice(64 * (h % 2), 64 * (h % 2) + 64)
                    c = slice((h // 2) * DH, (h // 2 + 1) * DH)
                    last = nc.tensor.matmul(B[(0, 4)[h % 2]][:, c], U_m[:, t, h, :], vb[:, t, h * DH:(h + 1) * DH],
                                            start=True, stop=(t == 0))
                    if t:
                        last = nc.tensor.matmul(B[(0, 4)[h % 2]][:, c], neg_wT[r, t, h // 2, :], state[r, h // 2, :],
                                                start=False, stop=True)
                last.then_inc(S["ua_ps"], 1)
                pe.wait_ge(S["ua_ready"], 2 * (t + 1))
                if t:
                    pe.wait_ge(S["do_ready"], 2 * t)
                if t < NT - 1:
                    for h in HEAD_ORDER:
                        r = slice(64 * (h % 2), 64 * (h % 2) + 64)
                        hh = slice(h * DH, (h + 1) * DH)
                        last = nc.tensor.matmul(B[2][r, (h // 2) * DH:(h // 2 + 1) * DH], qk_tok[:, 1, t, hh],
                                                u_adj[:, hh], start=True, stop=True)
                    last.then_inc(S["ds_ps"], 1)
                pe.wait_ge(S["attn_ready"], 2 * (t + 1))
                for h in HEAD_ORDER:
                    r = slice(64 * (h % 2), 64 * (h % 2) + 64)
                    c = slice((h // 2) * DH, (h // 2 + 1) * DH)
                    last = nc.tensor.matmul(B[(1, 5)[h % 2]][:, c], attn_m[:, t % 2, h, :], u_adj[:, h * DH:(h + 1) * DH],
                                            start=True, stop=(t == 0))
                    if t:
                        last = nc.tensor.matmul(B[(1, 5)[h % 2]][:, c], unitT[r, 0, h // 2, tt], state[r, h // 2, :],
                                                start=False, stop=True)
                last.then_inc(S["do_ps"], 1)
            pe.wait_ge(S["do_ready"], 2 * NT)
            for c in range(KD):
                for k in range(KD):
                    last = nc.tensor.matmul(B[4 + c][:, :], mlp1_a[:, k, c * P:(c + 1) * P], xT[:, k, :],
                                            start=(k == 0), stop=(k == KD - 1))
                last.then_inc(S["h1_all_ps"], 1)
            pe.wait_ge(S["stat_ready"], 1)
            for t in range(NT):
                last = nc.tensor.transpose(B[6][0:H * 16, t * P:(t + 1) * P],
                                           stats[:, t].rearrange("p h k s -> p (h k s)"), ident[:, :])
            last.then_inc(S["stat_ps"], 1)
            pe.wait_ge(S["statT_ready"], 1)
            pe.wait_ge(S["do_ready"], 2 * NT)

            def logits(h):
                pe.wait_ge(S["h1_ready"], KD * (h + 1))
                for t in range(NT):
                    for k in range(KD):
                        last = nc.tensor.matmul(B[7][:, (t * H + h) * 4:(t * H + h + 1) * 4],
                                                h1[:, h % 2, k, t * P:(t + 1) * P], mlp2_w[:, k, :],
                                                start=(k == 0), stop=(k == KD - 1))
                last.then_inc(S["logit_ps"], 1)

            for h in range(H):
                for c in range(KD):
                    n = KD * h + c
                    if n >= 4:
                        pe.wait_ge(S["h1_sum"], n - 3)
                    nc.tensor.matmul(B[n % 4][:, :], mlp1_s[:, h, c * P:(c + 1) * P], statT,
                                     start=True, stop=True).then_inc(S["h1_ps"], 1)
                if h:
                    logits(h - 1)
            logits(H - 1)
            pe.wait_ge(S["mix_ready"], 1)
            turn_tensor(pe, o_tok, 1, 0, 1)
            turned(pe, 1)
            for t in range(NT):
                for k in range(KD):
                    last = nc.tensor.matmul(B[2 + t // 2][:, (t % 2) * D:(t % 2 + 1) * D], oT[:, k, t * P:(t + 1) * P],
                                            o_w[:, k, :], start=(k == 0), stop=(k == KD - 1))
                if t % 2:
                    last.then_inc(S["o_ps"], 1)

        def delta_products(pe, lv, t):
            n = (lv - 1) * NT + t
            pe.wait_ge(S["p_ready"], n + 1)
            if n >= 2:
                pe.wait_ge(S["tu_ready"], n - 1)
            if lv < LEVELS - 1:
                for h in range(H):
                    nc.tensor.matmul(B[t % 2][:, h * P:(h + 1) * P], U_m[:, t, h, :], P_m[:, t, h, :],
                                     start=True, stop=True)
            for h in range(H):
                last = nc.tensor.matmul(B[2 + t % 2][:, h * P:(h + 1) * P], P_m[:, t, h, :], U_m[:, t, h, :],
                                        start=True, stop=True)
            last.then_inc(S["d_ps"], 1)

        def attn_scalar(act, c):
            for i in range(6):
                act.wait_ge(S["qkv_ps"], i + 1)
                nc.scalar.copy(pre[:, i, TAPS - 1:], B[i][:, :]).then_inc(S["pre_ready"], 1)
            for i in range(6):
                act.wait_ge(S["conv_ready"], i + 1)
                dst = conv[:, i, :] if i < 4 else vpad[:, i - 4, SHORT - 1:]
                nc.scalar.activation(dst, conv[:, i, :], ACT.Silu).then_inc(S["silu_ready"], 1)
            act.wait_ge(S["beta_ps"], 1)
            nc.scalar.activation(beta, B[6][:, 0:NT * H], ACT.Sigmoid).then_inc(S["beta_ready"], 1)
            for i in range(6):
                act.wait_ge(S["tok_ps"], i + 1)
                half = i % 2
                src = B[i][:, :].rearrange("p (t c) -> p t c", t=2)
                dst = qk_tok[:, i // 2, 2 * half:2 * half + 2, :] if i < 4 else feats[:, 2 * half:2 * half + 2, 3, :]
                nc.scalar.copy(dst, src).then_inc(S["tok_ready"], 1)
            for n in range(4):
                act.wait_ge(S["window_ps"], n + 1)
                first = (1, 5, 0, 4)[n]
                nc.scalar.copy(win[:, first:first + 3:2, :], B[n][:, :].rearrange("p (w c) -> p w c", w=2))\
                    .then_inc(S["window_ready"], 1)
            act.wait_ge(S["ss_ready"], 1)
            nc.scalar.activation(ss_sd, ss, ACT.Sqrt).then_inc(S["ss_root"], 1)
            def fir_windows(q):
                act.wait_ge(S["fir_ps"], q + 1)
                for half in range(2):
                    src = B[6 + q % 2][0:64, :].rearrange("p (c t w) -> p w t c", t=NT, w=2)[:, half]
                    nc.scalar.copy(feats[64 * half:64 * half + 64, :, 1, 64 * q:64 * (q + 1)], src)\
                        .then_inc(S["fir_ready"], 1)

            fir_windows(0)
            fir_windows(1)
            for i in range(6):
                act.wait_ge(S["unitT_ps"], i + 1)
                nc.scalar.copy(unitT[:, i // 2, i % 2, :], B[i][:, :]).then_inc(S["unitT_ready"], 1)
            fir_windows(2)
            fir_windows(3)
            act.wait_ge(S["fir_ps"], 4)
            for n in range(4):
                act.wait_ge(S["gram_ps"], n + 1)
                t = 2 * (n // 2)
                nc.scalar.copy(M_T[:, t:t + 2, n % 2:H:2],
                               B[n][:, :].rearrange("p (t h c) -> p t h c", t=2, h=KD)).then_inc(S["gram_ready"], 1)
            for t in range(NT):
                act.wait_ge(S["t0_ps"], t + 1)
                nc.scalar.copy(T_m[:, t], B[4 + t % 2][:, :].rearrange("p (h c) -> p h c", h=H)).then_inc(S["t0_ready"], 1)
            for lv in range(1, LEVELS):
                for t in range(NT):
                    n = (lv - 1) * NT + t
                    act.wait_ge(S["p_ps"], n + 1)
                    if n >= NT:
                        act.wait_ge(S["d_ps"], n - NT + 1)
                    nc.scalar.copy(P_m[:, t], B[4 + t % 2][:, :].rearrange("p (h c) -> p h c", h=H))\
                        .then_inc(S["p_ready"], 1)
                    if (lv, t) == SHORT_AT:
                        for half in range(2):
                            act.wait_ge(S["short_ps"], half + 1)
                            nc.scalar.copy(feats[:, 2 * half:2 * half + 2, 0, :],
                                           B[6 + half][:, :].rearrange("p (t c) -> p t c", t=2))\
                                .then_inc(S["short_tok"], 1)
            for t in range(NT):
                act.wait_ge(S["w_ps"], 2 * (t // 2) + 2)
                nc.scalar.mul(neg_wT[:, t], B[4 + t // 2][:, (t % 2) * D:(t % 2 + 1) * D]
                              .rearrange("p (k c) -> p k c", k=KD), -1.0).then_inc(S["w_ready"], 1)
            for t in range(NT):
                act.wait_ge(S["ua_ps"], t + 1)
                if t:
                    act.wait_ge(S["do_ps"], t)
                by_head = lambda x: x.rearrange("p (h d) -> p h d", d=DH)
                for odd in range(2):
                    nc.scalar.copy(by_head(u_adj)[:, odd:H:2], by_head(B[(0, 4)[odd]][:, 0:P])).then_inc(S["ua_ready"], 1)
                act.wait_ge(S["do_ps"], t + 1)
                for odd in range(2):
                    nc.scalar.copy(by_head(feats[:, t, 2, :])[:, odd:H:2], by_head(B[(1, 5)[odd]][:, 0:P]))\
                        .then_inc(S["do_ready"], 1)
            for c in range(KD):
                act.wait_ge(S["h1_all_ps"], c + 1)
                nc.scalar.activation(h1_all[:, c, :], B[4 + c][:, :], ACT.Identity, bias=mlp1_b[:, c:c + 1])\
                    .then_inc(S["h1_all"], 1)
            act.wait_ge(S["l2_ready"], 1)
            nc.scalar.activation(st_l2, st_mean2, ACT.Sqrt).then_inc(S["l2_root"], 1)
            act.wait_ge(S["stat_ps"], 1)
            nc.scalar.copy(statT, B[6][0:H * 16, :]).then_inc(S["statT_ready"], 1)
            for h in range(H):
                for k in range(KD):
                    n = KD * h + k
                    act.wait_ge(S["h1_sum"], n + 1)
                    nc.scalar.activation(h1[:, h % 2, k, :], h1[:, h % 2, k, :], ACT.Gelu_apprx_tanh)\
                        .then_inc(S["h1_ready"], 1)
            act.wait_ge(S["lg_ready"], 1)
            nc.scalar.activation(lg_e, lg_p, ACT.Exp, scale=inv_temp).then_inc(S["lg_exp"], 1)
            act.wait_ge(S["mix_ss"], 1)
            nc.scalar.activation(ss_sd[:, 0:NT * H], ss[:, 0:NT * H], ACT.Sqrt).then_inc(S["mix_root"], 1)
            turn_scalar(act, oT, 1, 0, 1)

        def attn_vector(dve, v):
            V = nc.vector
            v.step(V.memset(pre[:, :, 0:TAPS - 1], 0.0))
            v.step(V.memset(vpad[:, :, 0:SHORT - 1], 0.0))
            v.settle()
            for i in range(0, 6, 2):
                dve.wait_ge(S["pre_ready"], i + 2)
                for tap in range(TAPS):
                    for j in (i, i + 1):
                        x = pre[:, j, tap:tap + T]
                        w = conv_w[:, j, tap:tap + 1]
                        if tap == 0:
                            v.step(V.tensor_scalar(conv[:, j, :], x, w, None, ALU.mult))
                        elif tap < TAPS - 1:
                            v.step(V.scalar_tensor_tensor(conv[:, j, :], x, w, conv[:, j, :], ALU.mult, ALU.add))
                        else:
                            V.scalar_tensor_tensor(conv[:, j, :], x, w, conv[:, j, :], ALU.mult, ALU.add)\
                                .then_inc(S["conv_ready"], 1)
                    v.settle()
            dve.wait_ge(S["beta_ready"], 1)
            v.step(V.tensor_scalar(beta, beta, 1e-6, None, ALU.max))
            dve.wait_ge(S["tok_ready"], 4)
            v.link(V.tensor_tensor(sq, qk_tok, qk_tok, ALU.mult))
            v.link(V.tensor_reduce(ss, sq.rearrange("p i t (h d) -> p (i t h) d", h=H), AX_X, ALU.add))
            V.tensor_scalar(ss, ss, 1e-6, None, ALU.add).then_inc(S["ss_ready"], 1)
            dve.wait_ge(S["ss_root"], 1)
            v.link(V.reciprocal(unit, ss_sd))
            heads = qk_tok.rearrange("p i t (h d) -> p (i t h) d", h=H)
            v.link(V.tensor_tensor(heads, heads, spread(unit, 2, DH), ALU.mult))
            k_heads = qk_tok[:, 1].rearrange("p t (h d) -> p (t h) d", h=H)
            dve.wait_ge(S["tok_ready"], 6)
            dve.wait_ge(padded, 16 * NE)
            v_heads = feats[:, :, 3, :].rearrange("p t (h d) -> p t h d", h=H)
            v.step(V.tensor_tensor(vb.rearrange("p t (h d) -> p t h d", h=H), v_heads,
                                   spread(beta.rearrange("p (t h) -> p t h", t=NT), 3, DH), ALU.mult))
            V.tensor_tensor(kb.rearrange("p t (h d) -> p (t h) d", h=H), k_heads, spread(beta, 2, DH), ALU.mult)\
                .then_inc(S["unit_ready"], 1)
            ids_vector(dve, v, S["ids_in"], S["rows_ready"])
            for t in range(NT):
                dve.wait_ge(S["gram_ready"], 2 * (t // 2) + 2)
                v.link(V.tensor_tensor(U_m[:, t], M_T[:, t], spread(level_mask[:, 0, :], 1, H), ALU.mult))
                V.tensor_tensor(U_m[:, t], spread(ident[:, :], 1, H), U_m[:, t], ALU.subtract).then_inc(S["u0_ready"], 1)
            def short_tap(tap):
                v.settle()
                for c in range(KD):
                    x = vpad[:, c, tap:tap + T]
                    w = short_w[:, c, tap:tap + 1]
                    if tap == 0:
                        v.step(V.tensor_scalar(short_T[:, c, :], x, w, None, ALU.mult))
                    elif tap < SHORT - 1:
                        v.step(V.scalar_tensor_tensor(short_T[:, c, :], x, w, short_T[:, c, :], ALU.mult, ALU.add))
                    else:
                        V.scalar_tensor_tensor(short_T[:, c, :], x, w, short_T[:, c, :], ALU.mult, ALU.add)\
                            .then_inc(S["short_ready"], 1)

            def statistics(k, part):
                f = feats[:, :, k, :].rearrange("p t (h d) -> p t h d", h=H)
                cc = cent[:, :, k * H:(k + 1) * H, :]
                v.settle()
                if part == 0:
                    v.step(V.tensor_reduce(st_sum[:, :, k], f, AX_X, ALU.add))
                elif part == 1:
                    v.step(V.tensor_scalar(stats_mean[:, :, k], st_sum[:, :, k], 1.0 / DH, None, ALU.mult))
                    v.step(V.tensor_reduce(st_abs[:, :, k], f, AX_X, ALU.add, apply_absolute_value=True))
                elif part == 2:
                    v.step(V.tensor_tensor(cc, f, spread(stats_mean[:, :, k], 3, DH), ALU.subtract))
                    v.step(V.tensor_tensor(st_mean2[:, :, k], st_sum[:, :, k], stats_mean[:, :, k], ALU.mult))
                elif part == 3:
                    v.step(V.tensor_tensor(cc, cc, cc, ALU.mult))
                else:
                    v.step(V.tensor_reduce(st_css[:, :, k], cc, AX_X, ALU.add))

            dve.wait_ge(S["fir_ready"], 8)
            for lv in range(1, LEVELS):
                for t in range(NT):
                    n = (lv - 1) * NT + t
                    dve.wait_ge(S["d_ps"], n + 1)
                    if lv == 1:
                        dve.wait_ge(S["u0_ready"], NT)
                        dve.wait_ge(S["t0_ready"], NT)
                    else:
                        dve.wait_ge(S["tu_ready"], n - NT + 1)
                    if lv < LEVELS - 1:
                        v.step(V.tensor_tensor(T_m[:, t], T_m[:, t], B[t % 2][:, :].rearrange("p (h c) -> p h c", h=H),
                                               ALU.subtract))
                    V.tensor_tensor(U_m[:, t], U_m[:, t], B[2 + t % 2][:, :].rearrange("p (h c) -> p h c", h=H),
                                    ALU.subtract).then_inc(S["tu_ready"], 1)
                    if n < SHORT:
                        short_tap(n)
                    elif n < SHORT + 10:
                        statistics((3, 1)[(n - SHORT) // 5], (n - SHORT) % 5)
                    elif n >= NT * (LEVELS - 1) - 5:
                        dve.wait_ge(S["short_tok"], 2)
                        statistics(0, n - (NT * (LEVELS - 1) - 5))
            for t in range(NT):
                dve.wait_ge(S["attn_ps"], t + 1)
                if t >= 2:
                    dve.wait_ge(S["do_ps"], t - 1)
                for odd in range(2):
                    V.tensor_tensor(attn_m[:, t % 2, odd:H:2], B[(3, 6)[odd]][:, 0:D].rearrange("p (h c) -> p h c", h=KD),
                                    spread(causal[:, :], 1, KD), ALU.mult).then_inc(S["attn_ready"], 1)
                if t < NT - 1:
                    dve.wait_ge(S["ds_ps"], t + 1)
                    if t:
                        dve.wait_ge(S["do_ps"], t + 1)
                        dve.wait_ge(S["ds_ready"], t)
                        V.tensor_tensor(state, state, B[2][:, 0:P].rearrange("p (k c) -> p k c", k=KD), ALU.add)\
                            .then_inc(S["ds_ready"], 1)
                    else:
                        V.tensor_copy(state, B[2][:, 0:P].rearrange("p (k c) -> p k c", k=KD)).then_inc(S["ds_ready"], 1)
            dve.wait_ge(S["do_ready"], 2 * NT)
            for part in range(5):
                statistics(2, part)
            v.settle()
            flat = lambda x: x.rearrange("p t k h -> p (t k h)")
            V.tensor_tensor(flat(st_mean2), flat(st_mean2), flat(st_css), ALU.add).then_inc(S["l2_ready"], 1)
            dve.wait_ge(S["l2_root"], 1)
            for t in range(NT):
                for n, (src, mul) in enumerate(((stats_mean, 1.0), (st_css, 1.0 / DH), (st_abs, 1.0 / DH), (st_l2, 1.0))):
                    ins_ = V.tensor_scalar(stats[:, t, :, :, n].rearrange("p h k -> p k h"), src[:, t], mul, None, ALU.mult)
                    if t == NT - 1 and n == 3:
                        ins_.then_inc(S["stat_ready"], 1)
                    else:
                        v.step(ins_)
            for n in range(H * KD):
                dve.wait_ge(S["h1_ps"], n + 1)
                if n == 0:
                    dve.wait_ge(S["h1_all"], KD)
                if n >= 4:
                    dve.wait_ge(S["logit_ps"], n // KD - 1)
                V.tensor_tensor(h1[:, (n // KD) % 2, n % KD, :], B[n % 4][:, :], h1_all[:, n % KD, :], ALU.add)\
                    .then_inc(S["h1_sum"], 1)
            dve.wait_ge(S["logit_ps"], H)
            L = B[7][:, 0:NT * H * 4].rearrange("p (t h k) -> p (t h) k", t=NT, h=H)
            g = lambda x: x.rearrange("p t h k -> p (t h) k")
            m = lambda x: x.rearrange("p t h -> p (t h)")
            v.link(V.tensor_tensor(g(lg), L, spread(mlp2_b[:, :], 1, NT * H), ALU.add))
            v.link(V.tensor_reduce(m(lg_m), g(lg), AX_X, ALU.max))
            V.tensor_tensor(g(lg_p), g(lg), spread(m(lg_m), 2, 4), ALU.subtract).then_inc(S["lg_ready"], 1)
            dve.wait_ge(S["lg_exp"], 1)
            v.link(V.tensor_reduce(m(lg_s), g(lg_e), AX_X, ALU.add))
            v.link(V.reciprocal(m(lg_r), m(lg_s)))
            v.link(V.tensor_tensor(g(lg_p), g(lg_e), spread(m(lg_r), 2, 4), ALU.mult))
            v.link(V.tensor_scalar(g(lg_p), g(lg_p), 0.02, None, ALU.max))
            v.link(V.tensor_reduce(m(lg_s), g(lg_p), AX_X, ALU.add))
            v.link(V.reciprocal(m(lg_r), m(lg_s)))
            v.link(V.tensor_tensor(g(lg_p), g(lg_p), spread(m(lg_r), 2, 4), ALU.mult))
            v.link(V.tensor_tensor(lg_p[:, :, :, 0], lg_p[:, :, :, 0], spread(res_gate[:, :], 1, NT), ALU.add))
            for t in range(NT):
                for k in range(4):
                    v.step(V.tensor_tensor(mix[:, t, k], feats[:, t, k, :].rearrange("p (h d) -> p h d", h=H),
                                           spread(lg_p[:, t, :, k], 2, DH), ALU.mult))
            v.settle()
            mk = lambda k: mix[:, :, k].rearrange("p t h d -> p t (h d)")
            v.step(V.tensor_tensor(mk(0), mk(0), mk(1), ALU.add))
            v.step(V.tensor_tensor(mk(2), mk(2), mk(3), ALU.add))
            v.settle()
            v.link(V.tensor_tensor(o_tok, mk(0), mk(2), ALU.add))
            v.link(V.tensor_tensor(o_sq, o_tok, o_tok, ALU.mult))
            oh = o_tok.rearrange("p t (h d) -> p (t h) d", h=H)
            v.link(V.tensor_reduce(ss[:, 0:NT * H], o_sq.rearrange("p t (h d) -> p (t h) d", h=H), AX_X, ALU.add))
            V.tensor_scalar(ss[:, 0:NT * H], ss[:, 0:NT * H], 1.0 / DH, 1e-5, ALU.mult, ALU.add).then_inc(S["mix_ss"], 1)
            dve.wait_ge(S["mix_root"], 1)
            v.link(V.reciprocal(unit[:, 0:NT * H], ss_sd[:, 0:NT * H]))
            v.link(V.tensor_tensor(oh, oh, spread(unit[:, 0:NT * H], 2, DH), ALU.mult))
            V.tensor_tensor(oh, oh, spread(norm_w[:, :], 1, NT * H), ALU.mult).then_inc(S["mix_ready"], 1)
            add_hidden(dve, v, S["o_ps"], 2, 3)

        def add_hidden(dve, v, ready, first, second):
            for half in range(2):
                dve.wait_ge(ready, half + 1)
                t2 = slice(2 * half, 2 * half + 2)
                v.step(nc.vector.tensor_tensor(hid[:, t2, :], hid[:, t2, :],
                                               B[(first, second)[half]][:, :].rearrange("p (t c) -> p t c", t=2), ALU.add))
            v.settle()

        def attn_gpsimd(pool):
            for lv in range(1, LEVELS):
                for t in range(NT):
                    n = (lv - 1) * NT + t
                    pool.wait_ge(S["gram_ready"], 2 * (t // 2) + 2)
                    if lv > 1:
                        pool.wait_ge(S["p_ps"], n - NT + 1)
                    nc.gpsimd.tensor_tensor(L_T[:, t], M_T[:, t], spread(level_mask[:, lv, :], 1, H), ALU.mult)\
                        .then_inc(S["lm_ready"], 1)

        BLOCKS_OF_TILE = P // TB
        SIM_AND_DOWN = [("sim", n) for n in range(4)]
        SIM_AND_DOWN += [("down", n) for n in range(6)] + [("sim", 4), ("sim", 5)]
        SIM_AND_DOWN += [("down", n) for n in range(6, 12)] + [("sim", 6), ("sim", 7)]
        SIM_AND_DOWN += [("down", n) for n in range(12, XC)]

        def peer_vector(dve, v):
            V = nc.vector
            dve.wait_ge(S["ln_out"], 2 * NT)
            v.link(V.tensor_tensor(xx, xn[:, :, :], xn[:, :, :], ALU.mult))
            v.link(V.tensor_reduce(x_sq, xx, AX_X, ALU.add))
            v.link(V.tensor_copy(x_r, x_sq))
            V.tensor_copy(x_sq, x_r).then_inc(S["xss_ready"], 1)
            dve.wait_ge(S["xss_root"], 1)
            v.link(V.tensor_scalar(x_sd, x_sd, 1e-12, None, ALU.max))
            v.link(V.reciprocal(x_r, x_sd))
            for t in range(NT):
                v.step(V.tensor_scalar(xn[:, t, :], xn[:, t, :], x_r[:, t:t + 1], 16.0, ALU.mult, ALU.mult))
            v.settle()
            V.tensor_tensor(xn[:, :, :], xn[:, :, :], spread(gamma[:, :], 1, NT), ALU.mult).then_inc(S["ln_out"], 1)
            for t in range(NT):
                dve.wait_ge(S["sim_ready"], 2 * t + 2)
                segs = [(c // PH, c % PH, sim[:, t % 2, c, :]) for c in range(2 * PH)]
                for p, h, x in segs:
                    v.step(V.max(val[:, p, t, h, 0:8], x))
                v.settle()
                for p, h, x in segs:
                    v.step(V.max_index(key[:, p, t, h, 0:8], val[:, p, t, h, 0:8], x))
                v.settle()
                for p, h, x in segs:
                    v.step(V.match_replace(x, val[:, p, t, h, 0:8], x, LOWEST))
                v.settle()
                for p, h, x in segs:
                    v.step(V.max(val[:, p, t, h, 8:16], x))
                v.settle()
                for p, h, x in segs[:-1]:
                    v.step(V.max_index(key[:, p, t, h, 8:16], val[:, p, t, h, 8:16], x))
                p, h, x = segs[-1]
                V.max_index(key[:, p, t, h, 8:16], val[:, p, t, h, 8:16], x).then_inc(S["sim_used"], 1)
            dve.wait_ge(S["sim_used"], NT)
            G = NT * PH
            vx, vy = (val[:, p].rearrange("p t h k -> p (t h) k") for p in range(2))
            for i in range(8):
                n = ROWLEN[i]
                v.step(V.tensor_tensor(cand[:, :, ROWAT[i]:ROWAT[i] + n], vy[:, :, 0:n],
                                       vx[:, :, i:i + 1].broadcast_to([P, G, n]), ALU.add))
            v.step(V.tensor_tensor(cand[:, :, ROWAT[8]:PAIRS], vx[:, :, 8:16],
                                   vy[:, :, 0:1].broadcast_to([P, G, 8]), ALU.add))
            v.step(V.tensor_copy(keyx, key[:, 0].rearrange("p t h k -> p k (t h)")))
            v.step(V.tensor_copy(keyy, key[:, 1].rearrange("p t h k -> p k (t h)")))
            v.settle()
            v.step(V.tensor_copy(key_d[:, 0:1, :], keyx[:, 0:1, :]))
            v.step(V.tensor_tensor(key_d[:, 1:TOPK, :], keyx[:, 1:TOPK, :], keyx[:, 0:TOPK - 1, :], ALU.subtract))
            for g in range(G):
                v.step(V.max(top[:, g, 0:8], cand[:, g, :]))
            v.settle()
            for g in range(G):
                v.step(V.max_index(pos[:, g, 0:8], top[:, g, 0:8], cand[:, g, :]))
            v.settle()
            for g in range(G):
                v.step(V.match_replace(cand[:, g, :], top[:, g, 0:8], cand[:, g, :], LOWEST))
            v.settle()
            for g in range(G):
                v.step(V.max(top[:, g, 8:16], cand[:, g, :]))
            v.settle()
            for g in range(G):
                v.step(V.max_index(pos[:, g, 8:16], top[:, g, 8:16], cand[:, g, :]))
            v.settle()
            v.step(V.tensor_copy(pos_b, pos.rearrange("p g k -> p k g")))
            V.tensor_tensor(e_w, top, top[:, :, 0:1].broadcast_to([P, G, TOPK]), ALU.subtract).then_inc(S["score_ready"], 1)
            v.settle()

            def look_up(out, at, op, consts, factors, table):
                flat = at.rearrange("p k g -> p (k g)")
                for m in range(TOPK):
                    v.step(V.tensor_scalar(look[:, m], flat, float(consts[m]), float(factors[m]), op, ALU.mult))
                v.settle()
                if table is not None:
                    look4 = look.rearrange("p m (k g) -> p m k g", g=G)
                    v.link(V.tensor_tensor(look4, look4, spread(table, 2, TOPK), ALU.mult))
                n = TOPK
                while n > 1:
                    n //= 2
                    pairs = look[:, 0:2 * n].rearrange("p (m two) x -> p m two x", two=2)
                    if n > 1:
                        v.link(V.tensor_tensor(look[:, 0:n], pairs[:, :, 0], pairs[:, :, 1], ALU.add))
                    else:
                        a, b = (look[:, i].rearrange("p (k t h) -> p k t h", k=TOPK, t=NT) for i in range(2))
                        v.link(V.tensor_tensor(out, a, b, ALU.add))

            look_up(col_b.rearrange("p k (t h) -> p k t h", t=NT), pos_b, ALU.is_ge, ROWAT, [0] + ROWLEN[:-1], None)
            v.link(V.tensor_tensor(col_b, pos_b, col_b, ALU.subtract))
            look_up(e_x.rearrange("p t k h -> p k t h"), pos_b, ALU.is_ge, ROWAT, [1] * TOPK, key_d)
            look_up(e_y.rearrange("p t k h -> p k t h"), col_b, ALU.is_equal, range(TOPK), [1] * TOPK, keyy)
            v.link(V.tensor_scalar(e_far, e_y, float(YC), None, ALU.is_ge))
            v.step(V.scalar_tensor_tensor(e_x, e_far, float(NK), e_x, ALU.mult, ALU.add))
            v.step(V.scalar_tensor_tensor(e_y, e_far, -float(YC), e_y, ALU.mult, ALU.add))
            dve.wait_ge(S["score_exp"], 1)
            v.link(V.tensor_reduce(e_s, e_w, AX_X, ALU.add))
            v.link(V.reciprocal(e_r, e_s))
            V.tensor_tensor(e_gate.rearrange("p t k h -> p t h k"), e_w.rearrange("p (t h) k -> p t h k", t=NT),
                            spread(e_r, 2, TOPK).rearrange("p (t h) k -> p t h k", t=NT), ALU.mult)\
                .then_inc(S["entry_ready"], 1)
            dve.wait_ge(S["entry_ps"], 3)
            v.step(V.tensor_copy(entT_x, B[4][:, :]))
            v.step(V.tensor_copy(entT_y, B[5][:, :]))
            v.link(V.tensor_copy(entT_w[:, 0, :], B[6][:, :]))
            v.link(V.tensor_tensor(w_rest, B[6][:, :], entT_w[:, 0, :], ALU.subtract))
            v.link(V.tensor_copy(entT_w[:, 1, :], w_rest))
            v.link(V.tensor_tensor(w_rest2, w_rest, entT_w[:, 1, :], ALU.subtract))
            v.link(V.tensor_copy(entT_w[:, 2, :], w_rest2))
            def gate(n):
                dve.wait_ge(S["cell_ps"], n + 1)
                part = grid[:, :, n * TB:(n + 1) * TB].rearrange("p j t -> p t j")
                V.tensor_tensor(part, B[n % 4][:, :].rearrange("p (t j) -> p t j", t=TB), part, ALU.mult)\
                    .then_inc(S["cell_ready"], 1)

            def add_tile(t):
                dve.wait_ge(S["up_ps"], t + 1)
                V.tensor_tensor(hid[:, t, :], hid[:, t, :], B[6 + t % 2][:, 0:D], ALU.add).then_inc(S["hid_peer"], 1)

            for n in range(T // TB):
                hx, hy, hw = hots[n % 2]
                tt = slice(n * TB, (n + 1) * TB)
                if n >= 2:
                    dve.wait_ge(S["cell_ps"], n - 1)
                v.step(V.tensor_tensor(hy, spread(entT_y[:, tt], 1, YC), iota_y[:, :, :], ALU.is_equal))
                v.step(V.tensor_tensor(hx, spread(entT_x[:, tt], 1, P), iota_x[:, :, :], ALU.is_equal))
                v.settle()
                for i in range(3):
                    ins_ = V.tensor_tensor(hw[:, i], hy, spread(entT_w[:, i, tt], 1, YC), ALU.mult)
                    if i < 2:
                        v.step(ins_)
                    else:
                        ins_.then_inc(S["hot_ready"], 1)
                if n == 0:
                    dve.wait_ge(S["down_act"], XC)
                else:
                    gate(n - 1)
                if n in (BLOCKS_OF_TILE * 2 + 3, BLOCKS_OF_TILE * 3 + 3):
                    add_tile(n // BLOCKS_OF_TILE - 2)
            gate(T // TB - 1)
            add_tile(2)
            add_tile(3)
            dve.wait_ge(S["hid_peer"], NT)

        def peer_scalar(act, c):
            act.wait_ge(S["xss_ready"], 1)
            nc.scalar.activation(x_sd, x_sq, ACT.Sqrt).then_inc(S["xss_root"], 1)
            turn_scalar(act, xT, 2, 0, 1)
            for kind, n in SIM_AND_DOWN:
                if kind == "sim":
                    act.wait_ge(S["sim_ps"], n + 1)
                    if n >= 4:
                        act.wait_ge(S["sim_used"], n // 2 - 1)
                    nc.scalar.copy(sim[:, (n // 2) % 2, (n % 2) * PH:(n % 2 + 1) * PH, :],
                                   B[2 + n % 2][:, :].rearrange("p (h k) -> p h k", h=PH)).then_inc(S["sim_ready"], 1)
                else:
                    act.wait_ge(S["down_ps"], n + 1)
                    nc.scalar.activation(grid[:, n, :], B[n % 2][:, :], ACT.Gelu).then_inc(S["down_act"], 1)
            act.wait_ge(S["score_ready"], 1)
            nc.scalar.activation(e_w, e_w, ACT.Exp).then_inc(S["score_exp"], 1)

        def peer_tensor(pe):
            pe.wait_ge(S["ln_out"], 2 * NT + 1)
            turn_tensor(pe, xn, 2, 0, 1)
            turned(pe, 2)
            for kind, n in SIM_AND_DOWN:
                if kind == "sim":
                    t, half = n // 2, n % 2
                    if n >= 2:
                        pe.wait_ge(S["sim_ready"], n - 1)
                    for k in range(KD):
                        last = nc.tensor.matmul(B[2 + n % 2][:, :], xT[:, k, t * P:(t + 1) * P],
                                                w_sim[:, k, half * 512:(half + 1) * 512],
                                                start=(k == 0), stop=(k == KD - 1))
                    last.then_inc(S["sim_ps"], 1)
                else:
                    pe.wait_ge(tab_in[(n // 2) % 2], 16 * (n // 4 + 1))
                    if n >= 2:
                        pe.wait_ge(S["down_act"], n - 1)
                    for k in range(KD):
                        last = nc.tensor.matmul(B[n % 2][:, :], tab_d[:, (n // 2) % 2, n % 2, k, :], xT[:, k, :],
                                                start=(k == 0), stop=(k == KD - 1))
                    last.then_inc(S["down_ps"], 1)
            pe.wait_ge(S["entry_ready"], 1)
            for i, e in enumerate((e_x, e_y, e_gate)):
                for t in range(NT):
                    last = nc.tensor.transpose(B[4 + i][:, t * P:(t + 1) * P], e[:, t].rearrange("p k h -> p (k h)"), ident[:, :])
                last.then_inc(S["entry_ps"], 1)
            pe.wait_ge(S["sim_ready"], 2 * NT)
            pe.wait_ge(S["down_act"], XC)

            def up(s):
                t, j0 = s // BLOCKS_OF_TILE, (s % BLOCKS_OF_TILE) * 4
                if j0 == 0:
                    pe.wait_ge(S["cell_ready"], BLOCKS_OF_TILE * (t + 1))
                    if t == 0:
                        pe.wait_ge(S["up_in"], 16 * 4)
                    if t >= 2:
                        pe.wait_ge(S["hid_peer"], t - 1)
                for j in range(j0, j0 + 4):
                    last = nc.tensor.matmul(B[6 + t % 2][:, 0:D], grid[:, j, t * P:(t + 1) * P], tab_u[:, j, :],
                                            start=(j == 0), stop=(j == XC - 1))
                if j0 + 4 == XC:
                    last.then_inc(S["up_ps"], 1)

            delay = BLOCKS_OF_TILE + 1
            for n in range(T // TB):
                hx, hy, hw = hots[n % 2]
                pe.wait_ge(S["hot_ready"], n + 1)
                if n >= 4:
                    pe.wait_ge(S["cell_ready"], n - 3)
                for t in range(TB):
                    for i in range(3):
                        last = nc.tensor.matmul(B[n % 4][:, t * YC:(t + 1) * YC], hx[:, :, t], hw[:, i, :, t],
                                                start=(i == 0), stop=(i == 2))
                last.then_inc(S["cell_ps"], 1)
                if n >= delay:
                    up(n - delay)
            for s in range(T // TB - delay, T // TB):
                up(s)

        def peer_sync(sp):
            sp.wait_ge(S["unit_ready"], 1)
            for j in range(XC // 2):
                if j >= 2:
                    sp.wait_ge(S["down_ps"], 2 * (j - 1))
                sp.dma_start(tab_d[:, j % 2], ins["downT"][:, 2 * j:2 * j + 2]).then_inc(tab_in[j % 2], 16)
            sp.wait_ge(S["entry_ps"], 3)
            for q in range(4):
                part = slice(q * XC // 4, (q + 1) * XC // 4)
                sp.dma_start(tab_u[:, part], ins["up"][:, part]).then_inc(S["up_in"], 16)

        def moe_sync(sp):
            for n in attn_names:
                sp.sem_clear(S[n])
            sp.wait_ge(S["up_ps"], NT)
            sp.dma_start(w1_shared, ins["W1"][NE:NE + 2].rearrange("e p k n -> p e k n")).then_inc(S["shared_in"], 16)
            sp.dma_start(w2_shared, ins["W2"][NE:NE + 2].rearrange("e p k n -> p e k n")).then_inc(S["shared_in"], 16)
            sp.wait_ge(S["sel_ready"], 1)
            for n in peer_names:
                sp.sem_clear(S[n])

        def ssm_tensor(pe):
            pe.wait_ge(S["ln_out"], 3 * NT + 1)
            turn_tensor(pe, xn, 3, 0, 1)
            turned(pe, 3)
            for e in range(2 * DI // P):
                if e >= 4:
                    pe.wait_ge(S["xz_ready"], e - 3)
                for k in range(KD):
                    last = nc.tensor.matmul(B[2 + e % 4][:, :], w_in[:, k, e * P:(e + 1) * P], xT[:, k, :],
                                            start=(k == 0), stop=(k == KD - 1))
                last.then_inc(S["xz_ps"], 1)
            pe.wait_ge(S["xz_ready"], 4)
            for k in range(DI // P):
                last = nc.tensor.matmul(B[6][0:DS, :], w_B[:, k, :], xz[:, k, :], start=(k == 0), stop=(k == DI // P - 1))
            last.then_inc(S["state_ps"], 1)
            pe.wait_ge(S["state_ready"], 1)
            pe.wait_ge(S["xz_ready"], 8)
            for e in range(DI // P):
                nc.tensor.matmul(B[2 + e][:, :], w_C[:, e * P:(e + 1) * P], states, start=True, stop=True)\
                    .then_inc(S["c_ps"], 1)
            pe.wait_ge(S["y_ready"], DI // P)
            for t in range(NT):
                for k in range(DI // P):
                    last = nc.tensor.matmul(B[t // 2][:, (t % 2) * D:(t % 2 + 1) * D], y[:, k, t * P:(t + 1) * P],
                                            w_out[:, k, :], start=(k == 0), stop=(k == DI // P - 1))
                if t % 2:
                    last.then_inc(S["so_ps"], 1)

        def ssm_scalar(act, c):
            turn_scalar(act, xT, 3, 0, 1)
            for e in range(2 * DI // P):
                act.wait_ge(S["xz_ps"], e + 1)
                nc.scalar.activation(xz[:, e, :], B[2 + e % 4][:, :], ACT.Silu, bias=b_in[:, e:e + 1])\
                    .then_inc(S["xz_ready"], 1)

        def ssm_vector(dve, v):
            V = nc.vector
            dve.wait_ge(S["ln_out"], 3 * NT + 1)
            v.step(V.tensor_tensor(hid[:, :, :], hid[:, :, :], spread(b_out[:, :], 1, NT), ALU.add))
            dve.wait_ge(S["state_ps"], 1)
            v.link(V.tensor_scalar(drive, B[6][0:DS, :], 0.1, None, ALU.mult))
            V.tensor_tensor_scan(states, decay[:, :], drive, 0.0, ALU.mult, ALU.add).then_inc(S["state_ready"], 1)
            dve.wait_ge(S["xz_ready"], 8)
            for e in range(DI // P):
                dve.wait_ge(S["c_ps"], e + 1)
                v.link(V.scalar_tensor_tensor(y[:, e, :], xz[:, e, :], skip_D[:, e:e + 1], B[2 + e][:, :],
                                              ALU.mult, ALU.add))
                V.tensor_tensor(y[:, e, :], y[:, e, :], xz[:, DI // P + e, :], ALU.mult).then_inc(S["y_ready"], 1)
            add_hidden(dve, v, S["so_ps"], 0, 1)

        def moe_tensor(pe):
            pe.wait_ge(S["ln_out"], 4 * NT + 1)
            turn_tensor(pe, xn, 4, 2, 3)
            turned(pe, 4)
            for t in range(NT):
                for k in range(KD):
                    last = nc.tensor.matmul(B[6][:, t * NE:(t + 1) * NE], xT[:, k, t * P:(t + 1) * P], gate_w[:, k, :],
                                            start=(k == 0), stop=(k == KD - 1))
            last.then_inc(S["gl_ps"], 1)

            def first(e):
                for c in range(FC):
                    for k in range(KD):
                        last = nc.tensor.matmul(B[c][:, :], w1_shared[:, e, k, c * P:(c + 1) * P], xT[:, k, :],
                                                start=(k == 0), stop=(k == KD - 1))
                    last.then_inc(S["e1_ps"], 1)

            def second(e):
                pe.wait_ge(S["e1_ready"], FC * (e + 1))
                for t in range(NT):
                    if NT * e + t >= 2:
                        pe.wait_ge(S["e2_used"], NT * e + t - 1)
                    for k in range(FC):
                        last = nc.tensor.matmul(B[4 + t % 2][:, 0:D], moe_h[:, e % 2, k, t * P:(t + 1) * P],
                                                w2_shared[:, e, k, :], start=(k == 0), stop=(k == FC - 1))
                    last.then_inc(S["e2_ps"], 1)

            pe.wait_ge(S["shared_in"], 32)
            first(0)
            pe.wait_ge(S["sel_ready"], 1)
            for t in range(NT):
                cols = slice(t * NE, (t + 1) * NE)
                last = nc.tensor.matmul(B[7][:, cols], strict[:, :], sel_b[:, t, 0:NE], start=True, stop=(t == 0))
                for u in range(t):
                    last = nc.tensor.matmul(B[7][:, cols], ones_b[:, :], sel_b[:, u, 0:NE], start=False, stop=(u == t - 1))
            for t in range(NT):
                last = nc.tensor.matmul(B[7][:, NT * NE:(NT + 1) * NE], ones_b[:, :], sel_b[:, t, 0:NE],
                                        start=(t == 0), stop=(t == NT - 1))
            last.then_inc(S["rank_ps"], 1)
            pe.wait_ge(S["gate_ready"], 1)
            for t in range(NT):
                last = nc.tensor.transpose(B[6][0:NE + 1, t * P:(t + 1) * P], gated[:, t, :], ident[:, :])
            last.then_inc(S["gate_ps"], 1)
            pe.wait_ge(S["gateT_ready"], 1)
            for t in range(NT):
                last = nc.tensor.matmul(B[4 + t // 2][:, (t % 2) * D:(t % 2 + 1) * D], gatedT[:, t * P:(t + 1) * P],
                                        b2_all[:, :], start=True, stop=True)
                if t % 2:
                    last.then_inc(S["bias_ps"], 1)
            pe.wait_ge(S["e1_ready"], FC)
            first(1)
            pe.wait_ge(S["hid_out"], 2)
            second(0)
            second(1)

        def moe_scalar(act, c):
            turn_scalar(act, xT, 4, 2, 3)
            act.wait_ge(S["gl_ready"], 1)
            nc.scalar.activation(ge, gl, ACT.Exp).then_inc(S["gl_exp"], 1)
            for e in range(2):
                for k in range(FC):
                    act.wait_ge(S["e1_ps"], FC * e + k + 1)
                    nc.scalar.activation(moe_h[:, e % 2, k, :], B[k][:, :], ACT.Gelu,
                                         bias=b1_shared[:, e, k:k + 1]).then_inc(S["e1_ready"], 1)
                if e == 0:
                    act.wait_ge(S["gate_ps"], 1)
                    nc.scalar.copy(gatedT, B[6][0:NE + 1, :]).then_inc(S["gateT_ready"], 1)

        def moe_vector(dve, v, b):
            V = nc.vector
            dve.wait_ge(S["ln_out"], 4 * NT + 1)
            v.step(V.tensor_tensor(hid[:, :, :], hid[:, :, :], xn[:, :, :], ALU.add))
            v.step(V.memset(garr, -1.0))
            v.step(V.memset(gtake, -1.0))
            v.step(V.memset(gated, 1.0))
            dve.wait_ge(S["gl_ps"], 1)
            v.link(V.tensor_tensor(gl, B[6][:, 0:NT * NE].rearrange("p (t e) -> p t e", t=NT),
                                   spread(gate_b[:, :], 1, NT), ALU.add))
            v.link(V.tensor_reduce(gm, gl, AX_X, ALU.max))
            V.tensor_tensor(gl, gl, spread(gm, 2, NE), ALU.subtract).then_inc(S["gl_ready"], 1)
            dve.wait_ge(S["gl_exp"], 1)
            v.link(V.tensor_reduce(gs, ge, AX_X, ALU.add))
            v.link(V.reciprocal(gr, gs))
            v.link(V.tensor_tensor(garr[:, :, 0:NE], ge, spread(gr, 2, NE), ALU.mult))
            v.link(V.tensor_copy(ge, garr[:, :, 0:NE]))
            for t in range(NT):
                v.step(V.max(gtop[:, t, :], garr[:, t, :]))
            v.settle()
            v.link(V.tensor_copy(gtake[:, :, 0:TAKE], gtop[:, :, 0:TAKE]))
            for t in range(NT):
                v.step(V.match_replace(garr[:, t, :], gtake[:, t, :], garr[:, t, :], -2.0))
            v.settle()
            v.step(V.tensor_scalar(sel, garr[:, :, 0:NE], -2.0, None, ALU.is_equal))
            V.tensor_scalar(sel_b[:, :, 0:NE], garr[:, :, 0:NE], -2.0, None, ALU.is_equal).then_inc(S["sel_ready"], 1)
            V.scalar_tensor_tensor(gated[:, :, 0:NE], garr[:, :, 0:NE], -2.0, ge, ALU.is_equal, ALU.mult)\
                .then_inc(S["gate_ready"], 1)
            v.settle()
            v.link(V.tensor_tensor_scan(nth.rearrange("p t e -> p (t e)"), restart[:, :, :].rearrange("p t e -> p (t e)"),
                                        sel.rearrange("p t e -> p (t e)"), 0.0, ALU.mult, ALU.add))
            for k in range(TAKE):
                v.step(V.scalar_tensor_tensor(hot3[:, :, k, :], nth, float(k + 1), sel, ALU.is_equal, ALU.mult))
            dve.wait_ge(S["rank_ps"], 1)
            v.link(V.tensor_tensor(rank, B[7][:, 0:NT * NE].rearrange("p (t e) -> p t e", t=NT),
                                   spread(count[:, :], 1, NT), ALU.add))
            v.step(V.tensor_tensor(count[:, :], count[:, :], B[7][:, NT * NE:(NT + 1) * NE], ALU.add))
            v.step(V.tensor_tensor(slot, rank, spread(region_at[:, :], 1, NT), ALU.add))
            v.settle()
            dve.wait_ge(S["gate_ready"], 1)
            for what, to in ((slot, slot3), (rank, rank3), (gated[:, :, 0:NE], gate3)):
                v.link(V.tensor_tensor(pick3, hot3, spread(what, 2, TAKE), ALU.mult))
                v.link(V.tensor_reduce(to, pick3, AX_X, ALU.add))
                if what is slot:
                    V.tensor_copy(slot_u, slot3).then_inc(S["slot_ready"], 1)
            tiles = bass.ds(b * NT, NT)
            v.step(V.tensor_copy(all_hot[:, tiles], hot3))
            v.step(V.tensor_copy(all_rank[:, tiles], rank3))
            v.step(V.tensor_copy(all_gate[:, tiles], gate3))
            for half in range(2):
                dve.wait_ge(S["bias_ps"], half + 1)
                t2 = slice(2 * half, 2 * half + 2)
                V.tensor_tensor(hid[:, t2, :], hid[:, t2, :], B[4 + half][:, :].rearrange("p (t c) -> p t c", t=2),
                                ALU.add).then_inc(S["hid_out"], 1)
            dve.wait_ge(S["hid_out"], 2)
            for e in range(2):
                for t in range(NT):
                    n = NT * e + t
                    dve.wait_ge(S["e2_ps"], n + 1)
                    if e:
                        dve.wait_ge(S["e2_used"], n - NT + 1)
                    V.tensor_tensor(hid[:, t, :], B[4 + t % 2][:, 0:D], hid[:, t, :], ALU.add)\
                        .then_inc(S["e2_used"], 1)
            dve.wait_ge(S["e2_used"], 2 * NT)

        def moe_gpsimd(pool, b):
            pool.wait_ge(S["slot_ready"], 1)
            for t in range(NT):
                for k in range(TAKE):
                    nc.gpsimd.indirect_dma_start(rows_d, bass.IndirectOffsetOnAxis(ap=slot_u[:, t, k:k + 1], axis=0),
                                                 xn[:, t, :], None).then_inc(scattered, 16)
            pool.wait_ge(scattered, (b + 1) * (16 * NT * TAKE))

        LEAD = RING + 1
        LOOPS = (TILES - RING - LEAD) // RING
        TAIL = LEAD + LOOPS * RING

        def routed_vector_tables(dve, v):
            V = nc.vector
            v.step(V.memset(one_row, 1.0))
            v.link(V.tensor_scalar(n_tiles, count[:, :], float(TILE - 1), None, ALU.add))
            v.link(V.tensor_copy(t_int, n_tiles))
            v.link(V.tensor_scalar(t_int, t_int, TILE.bit_length() - 1, None, ALU.arith_shift_right))
            v.link(V.tensor_copy(n_tiles, t_int))
            v.link(V.tensor_tensor_scan(t_sum, one_row, n_tiles, 0.0, ALU.mult, ALU.add))
            v.step(V.tensor_tensor(t_start, t_sum, n_tiles, ALU.subtract))
            v.step(V.scalar_tensor_tensor(t_ahead, n_tiles, float(TILE), count[:, :], ALU.mult, ALU.subtract))
            v.step(V.tensor_scalar(t_step, t_sum[:, NE - 1:NE], -1.0, None, ALU.add))
            v.settle()
            v.step(V.tensor_scalar(t_min, tile_no[:, :], t_step, None, ALU.min))
            v.link(V.tensor_tensor(t_row0, region_at[:, :], t_ahead, ALU.subtract))
            v.link(V.scalar_tensor_tensor(t_row0, t_start, -float(TILE), t_row0, ALU.mult, ALU.add))
            v.step(V.tensor_copy(t_jump[:, 0:1], t_row0[:, 0:1]))
            v.step(V.tensor_tensor(t_jump[:, 1:NE], t_row0[:, 1:NE], t_row0[:, 0:NE - 1], ALU.subtract))
            v.step(V.tensor_tensor(t_ge, spread(t_min, 2, NE), spread(t_start, 1, TILES), ALU.is_ge))
            v.settle()
            v.step(V.tensor_reduce(t_exp, t_ge, AX_X, ALU.add))
            v.link(V.tensor_tensor(t_gs, t_ge, spread(t_jump, 1, TILES), ALU.mult))
            v.step(V.tensor_scalar(t_exp, t_exp, -1.0, None, ALU.add))
            v.link(V.tensor_reduce(t_row, t_gs, AX_X, ALU.add))
            v.step(V.tensor_copy(tile_exp, t_exp))
            v.link(V.scalar_tensor_tensor(t_row, t_min, float(TILE), t_row, ALU.mult, ALU.add))
            V.tensor_copy(tile_row, t_row).then_inc(routed, 1)
            v.link(V.scalar_tensor_tensor(t_sum, t_start, float(TILE), t_ahead, ALU.mult, ALU.add))
            v.link(V.tensor_tensor(y_pick.rearrange("p t k e -> p (t k) e"), all_hot[:, :, :, :].rearrange("p t k e -> p (t k) e"),
                                   spread(t_sum, 1, BATCH * NT * TAKE), ALU.mult))
            v.link(V.tensor_reduce(y_slot, y_pick, AX_X, ALU.add))
            v.link(V.tensor_tensor(y_slot, y_slot, all_rank[:, :, :], ALU.add))
            V.tensor_copy(y_slot_u, y_slot).then_inc(routed, 1)

        def load_rows(act, n, p):
            row = act.value_load(tile_row[0:1, bass.ds(n, 1)] if not isinstance(n, int) else tile_row[0:1, n:n + 1],
                                 min_val=0, max_val=NE * REGION - TILE)
            act.dma_start(r_x[:, p], rows_d[bass.ds(row, TILE)].rearrange("(h p) c -> p h c", p=P)).then_inc(x_in[p], 16)

        def load_expert(act, n, p):
            e = act.value_load(tile_exp[0:1, bass.ds(n, 1)] if not isinstance(n, int) else tile_exp[0:1, n:n + 1],
                               min_val=0, max_val=NE - 1)
            act.dma_start(r_w1[:, p], ins["W1"][bass.ds(e, 1)].rearrange("a p k n -> p (a k) n")).then_inc(rw_in[p], 16)
            act.dma_start(r_w2[:, p], ins["W2"][bass.ds(e, 1)].rearrange("a p k n -> p (a k) n")).then_inc(rw_in[p], 16)
            act.dma_start(r_b1[:, p], ins["b1"][bass.ds(e, 1)].rearrange("a p k -> p (a k)")).then_inc(rw_in[p], 16)

        def expert_tensor(pe, n, p, r):
            if not isinstance(n, int) or n + 1 < TILES:
                turn_rows(pe, n + 1, (p + 1) % RING, r + (p + 1) // RING)
            pe.wait_ge(rw_in[p], 48 * r)
            pe.wait_ge(xt_ready, n + 1)
            for c in range(FC):
                bank = B[1 + 2 * p + c // 2]
                for k in range(KD):
                    last = nc.tensor.matmul(bank[:, (c % 2) * TILE:(c % 2 + 1) * TILE], r_w1[:, p, k, c * P:(c + 1) * P],
                                            r_xT[:, p, k, :], start=(k == 0), stop=(k == KD - 1))
                if c % 2:
                    last.then_inc(m1_ps, 1)

        def turn_rows(pe, n, p, r):
            pe.wait_ge(x_in[p], 16 * r)
            if not isinstance(n, int) or n > 0:
                pe.wait_ge(xt_ready, n)
            for k in range(KD):
                for h in range(HALF):
                    last = nc.tensor.transpose(B[0][:, k * TILE + h * P:k * TILE + (h + 1) * P],
                                               r_x[:, p, h, k * P:(k + 1) * P], ident[:, :])
            last.then_inc(xt_ps, 1)

        def second_product(pe, n, p):
            pe.wait_ge(m1_ready, FC * (n + 1))
            if not isinstance(n, int) or n > 0:
                pe.wait_ge(m2_ready, n)
            for h in range(HALF):
                for k in range(FC):
                    last = nc.tensor.matmul(B[7][:, h * D:(h + 1) * D], r_h[:, p, k, h * P:(h + 1) * P], r_w2[:, p, k, :],
                                            start=(k == 0), stop=(k == FC - 1))
            last.then_inc(m2_ps, 1)

        def routed_tensor(pe):
            turn_rows(pe, 0, 0, 1)
            for n in range(LEAD):
                expert_tensor(pe, n, n % RING, n // RING + 1)
                if n:
                    second_product(pe, n - 1, (n - 1) % RING)
            with pe.Fori(0, LOOPS) as i:
                for q in range(RING):
                    p = (LEAD + q) % RING
                    expert_tensor(pe, i * RING + LEAD + q, p, i + 1 + (LEAD + q) // RING)
                    second_product(pe, i * RING + LEAD + q - 1, (p - 1) % RING)
            for n in range(TAIL, TILES):
                expert_tensor(pe, n, n % RING, n // RING + 1)
                second_product(pe, n - 1, (n - 1) % RING)
            second_product(pe, TILES - 1, (TILES - 1) % RING)

        def activate(act, n, p, rows_ahead=True, expert_ahead=True):
            for c in range(FC):
                act.wait_ge(m1_ps, 2 * n + c // 2 + 1)
                nc.scalar.activation(r_h[:, p, c, :], B[1 + 2 * p + c // 2][:, (c % 2) * TILE:(c % 2 + 1) * TILE], ACT.Gelu,
                                     bias=r_b1[:, p, c:c + 1]).then_inc(m1_ready, 1)
            if rows_ahead:
                act.wait_ge(xt_ps, n + 1)
                load_rows(act, n + 3, p)
            if expert_ahead:
                act.wait_ge(m2_ps, n)
                load_expert(act, n + 2, (p + 2) % RING)

        def routed_scalar(act):
            act.wait_ge(routed, 1)
            for n in range(RING):
                load_rows(act, n, n)
                load_expert(act, n, n)
            for n in range(LEAD):
                activate(act, n, n % RING, expert_ahead=n > 0)
            with act.Fori(0, LOOPS) as i:
                for q in range(RING):
                    activate(act, i * RING + LEAD + q, (LEAD + q) % RING)
            for n in range(TAIL, TILES):
                activate(act, n, n % RING, n + RING < TILES, n + 2 < TILES)

        def expert_vector(dve, n, p):
            dve.wait_ge(xt_ps, n + 1)
            nc.vector.tensor_copy(r_xT[:, p].rearrange("p k n -> p (k n)"), B[0][:, :]).then_inc(xt_ready, 1)

        def output_vector(dve, n, p, r):
            dve.wait_ge(m2_ps, n + 1)
            if not isinstance(n, int) or n >= RING:
                dve.wait_ge(y_stored[p], 16 * (r - 1))
            nc.vector.tensor_copy(r_y[:, p].rearrange("p h c -> p (h c)"), B[7][:, :]).then_inc(m2_ready, 1)

        def routed_vector(dve, v):
            routed_vector_tables(dve, v)
            expert_vector(dve, 0, 0)
            for n in range(LEAD):
                expert_vector(dve, n + 1, (n + 1) % RING)
                if n:
                    output_vector(dve, n - 1, (n - 1) % RING, (n - 1) // RING + 1)
            with dve.Fori(0, LOOPS) as i:
                for q in range(RING):
                    n = i * RING + LEAD + q
                    expert_vector(dve, n + 1, (LEAD + q + 1) % RING)
                    output_vector(dve, n - 1, (LEAD + q - 1) % RING, i + (LEAD + q - 1) // RING + 1)
            for n in range(TAIL, TILES):
                if n + 1 < TILES:
                    expert_vector(dve, n + 1, (n + 1) % RING)
                output_vector(dve, n - 1, (n - 1) % RING, (n - 1) // RING + 1)
            output_vector(dve, TILES - 1, (TILES - 1) % RING, (TILES - 1) // RING + 1)
            dve.wait_ge(base_in, 16 * BATCH)
            for b in range(BATCH):
                dve.wait_ge(gathered[b], 16 * NT * TAKE)
                for k in range(TAKE):
                    for t in range(b * NT, (b + 1) * NT):
                        ins_ = nc.vector.scalar_tensor_tensor(f_base[:, t], f_rows[:, t, k], all_gate[:, t, k:k + 1],
                                                              f_base[:, t], ALU.mult, ALU.add)
                        if k == TAKE - 1:
                            ins_.then_inc(mixed, 1)
                        else:
                            v.step(ins_)
                    if k < TAKE - 1:
                        v.settle()

        def routed_sync(sp):
            sp.wait_ge(routed, 2)
            full = TILES // RING
            with sp.Fori(0, full) as i:
                for p in range(RING):
                    store_tile(sp, i * RING + p, p)
            for n in range(full * RING, TILES):
                store_tile(sp, n, n % RING)
            for b in range(BATCH):
                sp.dma_start(f_base[:, b * NT:(b + 1) * NT], base_d[b]).then_inc(base_in, 16)
            for b in range(BATCH):
                sp.wait_ge(mixed, (b + 1) * NT)
                sp.dma_start(out[b].rearrange("(t p) c -> p t c", p=P), f_base[:, b * NT:(b + 1) * NT]).then_inc(final_out, 16)
            sp.wait_ge(final_out, 16 * BATCH)

        def store_tile(sp, n, p):
            sp.wait_ge(m2_ready, n + 1)
            sp.dma_start(outs_d[bass.ds(n * TILE, TILE)].rearrange("(h p) c -> p h c", p=P), r_y[:, p]).then_inc(y_stored[p], 16)

        def routed_gpsimd(pool):
            pool.wait_ge(routed, 2)
            for p in range(RING):
                pool.wait_ge(y_stored[p], 16 * ((TILES - 1 - p) // RING + 1))
            for t in range(BATCH * NT):
                for k in range(TAKE):
                    nc.gpsimd.indirect_dma_start(f_rows[:, t, k], None, outs_d,
                                                 bass.IndirectOffsetOnAxis(ap=y_slot_u[:, t, k:k + 1], axis=0))\
                        .then_inc(gathered[t // NT], 16)

        def finish_sequence(eng, b):
            eng.sem_inc(iter_done, 1)
            eng.wait_ge(go_on, b + 1)

        E, A_, PE_, S_, M_ = (c in stages for c in "EAPSM")

        @block.sync
        def _(sp):
            ids_sync(sp, 0, first_ids)
            setup_sync(sp)
            with sp.Fori(0, BATCH) as b:
                if A_:
                    attn_sync(sp, b)
                if PE_:
                    peer_sync(sp)
                if M_:
                    moe_sync(sp)
                sp.wait_ge(iter_done, 1)
                if M_:
                    sp.dma_start(base_d[bass.ds(b, 1)].rearrange("a p t c -> p (a t) c"), hid[:, :, :])\
                        .then_inc(S["stored"], 16)
                else:
                    sp.dma_start(out[bass.ds(b, 1)].rearrange("a (t p) c -> p (a t) c", p=P), hid[:, :, :])\
                        .then_inc(S["stored"], 16)
                sp.wait_ge(iter_done, 4)
                for n in names:
                    if not (A_ and M_ and n in attn_names + peer_names):
                        sp.sem_clear(S[n])
                sp.sem_clear(iter_done)
                sp.wait_ge(S["stored"], 16)
                sp.sem_clear(S["stored"])
                sp.sem_inc(go_on, 1)
            if M_:
                routed_sync(sp)

        @block.gpsimd
        def _(pool):
            pool.wait_ge(first_rows, 4)
            gather_rows(pool)
            with pool.Fori(0, BATCH) as b:
                if A_:
                    attn_gpsimd(pool)
                if PE_:
                    pool.wait_ge(S["rows_ready"], 4)
                    pool.wait_ge(S["up_ps"], NT)
                    gather_rows(pool)
                if M_:
                    moe_gpsimd(pool, b)
                if PE_:
                    pool.wait_ge(rows_in, (b + 2) * (16 * 4 * NT))
                pool.wait_ge(iter_done, 1)
                finish_sequence(pool, b)
            if M_:
                routed_gpsimd(pool)

        @block.tensor
        def _(pe):
            setup_tensor(pe)
            pe.wait_ge(made, MADE)
            with pe.Fori(0, BATCH) as b:
                if E:
                    embed_tensor(pe)
                if A_:
                    pe.wait_ge(S["ln_out"], NT)
                    turn_tensor(pe, xn, 0, 0, 1)
                    attn_tensor(pe)
                if PE_:
                    peer_tensor(pe)
                if S_:
                    ssm_tensor(pe)
                if M_:
                    moe_tensor(pe)
                pe.wait_ge(iter_done, 1)
                finish_sequence(pe, b)
            if M_:
                routed_tensor(pe)

        @block.scalar
        def _(act):
            setup_scalar(act)
            act.wait_ge(made, MADE)
            with act.Fori(0, BATCH) as b:
                c = Chain(act, S["act_step"])
                if E:
                    embed_scalar(act)
                if A_:
                    norm_scalar(act, 0)
                    turn_scalar(act, xT, 0, 0, 1)
                    attn_scalar(act, c)
                if PE_:
                    norm_scalar(act, 1)
                    peer_scalar(act, c)
                if S_:
                    norm_scalar(act, 2)
                    ssm_scalar(act, c)
                if M_:
                    norm_scalar(act, 3)
                    moe_scalar(act, c)
                act.wait_ge(iter_done, 1)
                finish_sequence(act, b)
            if M_:
                routed_scalar(act)

        @block.vector
        def _(dve):
            nc.vector.memset(zeros, 0.0).then_inc(zeros_ready, 1)
            ids_vector(dve, Chain(dve, first_step), first_ids, first_rows)
            setup_vector(dve)
            dve.wait_ge(made, MADE)
            with dve.Fori(0, BATCH) as b:
                v = Chain(dve, S["dve_step"])
                if E:
                    embed_vector(dve, v, b)
                if A_:
                    norm_vector(dve, v, 0)
                    attn_vector(dve, v)
                if PE_:
                    norm_vector(dve, v, 1)
                    peer_vector(dve, v)
                if S_:
                    norm_vector(dve, v, 2)
                    ssm_vector(dve, v)
                if M_:
                    norm_vector(dve, v, 3)
                    moe_vector(dve, v, b)
                finish_sequence(dve, b)
            if M_:
                routed_vector(dve, Chain(dve, mix_step))


def kernel(**inputs):
    import concourse.bacc as _bacc
    from concourse.bass_utils import run_bass_kernel_spmd as _run

    nc = _bacc.Bacc("TRN2", target_bir_lowering=False, num_devices=1)
    arrays = arrange(inputs)
    ins = {n: nc.dram_tensor(f"in_{n}", a.shape, mybir.dt.from_np(a.dtype), kind="ExternalInput").ap()
           for n, a in arrays.items()}
    out = nc.dram_tensor("out_0", (BATCH, T, D), F32, kind="ExternalOutput").ap()
    build(nc, ins, out)
    r = _run(nc, [{f"in_{n}": a for n, a in arrays.items()}], core_ids=[0])
    return r.results[0]["out_0"]


def arrange(inputs):
    g = {n: np.asarray(a) for n, a in inputs.items()}
    a, p, q, m = (lambda n, pre=pre: g[pre + n] for pre in ("L0_attn_", "L0_ffn_", "L1_attn_", "L1_ffn_"))
    cols = lambda v: v.reshape(-1, P).T
    tokens = g["x"].reshape(BATCH, NT, P).transpose(0, 2, 1)
    z = {"x": np.concatenate([tokens, tokens[:1]])}
    for i in range(4):
        z[f"emb{i}"] = g[f"L0_tok_emb{i}"]
    z["proj"] = np.concatenate([g["L0_tok_proj1"], g["L0_tok_proj2"], g["L0_tok_proj3"]])
    for n in "qkv":
        z[f"{n}_wT"] = a(f"{n}_w").T
        z[f"{n}_cw"] = a(f"{n}_cw")
    z["b_wT"] = a("b_w").T
    z["fir_short"] = a("fir_short_w").reshape(D, SHORT)
    z["fir_long"] = np.zeros((D, 3 * LONG), np.float32)
    z["fir_long"][:, LONG:2 * LONG] = a("fir_long_w").reshape(D, LONG)[:, ::-1]
    z["mlp1_aT"] = a("mlp1_w")[:, :D].T
    z["mlp1_sT"] = np.zeros((H, H * 16, D), np.float32)
    for h in range(H):
        z["mlp1_sT"][h, 16 * h:16 * h + 16] = a("mlp1_w")[:, D:].T
    z["mlp1_b"], z["mlp2_wT"], z["mlp2_b"] = cols(a("mlp1_b")), a("mlp2_w").T, a("mlp2_b")
    z["logit_temp"], z["conv_res"], z["norm_w"], z["o_wT"] = a("logit_temp"), a("conv_res_logit"), a("norm_w"), a("o_w").T
    z["gamma"], z["wq"] = p("gamma"), p("wq")
    z["keysT"] = p("keys").transpose(2, 0, 3, 1).reshape(2 * PH, P, NK)
    rows = lambda t: t[:NX].reshape(NK, 2, YC, D).transpose(2, 1, 0, 3).reshape(XC, P, D)
    z["downT"] = rows(p("table_down")).reshape(XC, P, KD, P).transpose(3, 0, 2, 1)
    z["up"] = rows(p("table_up")).transpose(1, 0, 2)
    z["W_inT"], z["b_in"], z["W_BT"], z["W_CT"] = q("W_in").T, cols(q("b_in")), q("W_B").T, q("W_C").T
    z["D"], z["W_outT"], z["b_out"] = cols(q("D")), q("W_out").T, q("b_out")
    z["gW"], z["gb"] = m("gW"), m("gb")
    w1 = np.concatenate([m("rW1"), m("sW1").reshape(D, 2, FF).transpose(1, 0, 2)])
    w2 = np.concatenate([m("rW2"), m("sW2").reshape(2, FF, D)])
    z["W1"] = w1.reshape(NE + 2, KD, P, FF).transpose(0, 2, 1, 3)
    z["W2"] = w2.reshape(NE + 2, FC, P, D).transpose(0, 2, 1, 3)
    z["b1"] = np.concatenate([m("rb1"), m("sb1").reshape(2, FF)]).reshape(NE + 2, FC, P).transpose(0, 2, 1)
    z["b2"] = np.concatenate([m("rb2"), m("sb2")])
    z["c_ident"] = np.eye(P, dtype=np.float32)
    i, j = np.arange(P)[:, None], np.arange(P)[None, :]
    z["c_levels"] = np.stack([((i >> (lv + 1)) == (j >> (lv + 1))) & ((i >> lv) & 1 == 0) & ((j >> lv) & 1 == 1)
                              for lv in range(LEVELS)]).astype(np.float32)
    z["c_causal"] = (i <= j).astype(np.float32)
    z["c_flips"] = np.stack([i + j == P - 1, i + j == P // 2 - 1, i + j == P + P // 2 - 1], 1).astype(np.float32)
    z["c_iota"] = np.arange(P, dtype=np.float32)
    z["c_region"] = (np.arange(NE) * REGION + TILE).astype(np.float32)
    z["c_restart"] = np.tile(np.arange(NE) > 0, NT).astype(np.float32)
    return {n: np.ascontiguousarray(v) for n, v in z.items()}
```

```python
from contextlib import ExitStack

import numpy as np

import concourse.bass as bass
from concourse import mybir

F32 = mybir.dt.float32
BF16 = mybir.dt.bfloat16
I32 = mybir.dt.int32
U32 = mybir.dt.uint32
ALU = mybir.AluOpType
ACT = mybir.ActivationFunctionType
AX_X = mybir.AxisListType.X

P = 128
BATCH, T = 4, 512
NT = T // P
D = 256
KD = D // P
CUTOFFS = [0, 5000, 10000, 50000, 267735]
EMB = [D // 4**i for i in range(4)]
EMB_AT = [sum(EMB[:i]) for i in range(4)]
EMB_ALL = sum(EMB)
EMB_LOW = EMB_ALL - D
H, DH = 4, 64
TAPS, SHORT, LONG = 4, 5, 64
PH, NK, TOPK = 8, 64, 16
NX = NK * NK
XC = NX // P
YC = NK // 2
ROWLEN = [TOPK // (i + 1) for i in range(TOPK)]
ROWAT = [sum(ROWLEN[:i]) for i in range(TOPK)]
PAIRS = sum(ROWLEN)
TB = 16
DI, DS = 512, 16
NE, FF = 15, 512
FC = FF // P
TAKE = 3
N_TOK = BATCH * T
TILE = 256
HALF = TILE // P
TILES = (N_TOK * TAKE + NE * (TILE - 1)) // TILE
REGION = TILE + N_TOK
RING = 3
LEVELS = 7
LOWEST = -3.0e38
HEAD_ORDER = [0, 2, 1, 3]


class Chain:

    def __init__(self, eng, sem):
        self.eng, self.sem, self.n = eng, sem, 0

    def step(self, ins):
        ins.then_inc(self.sem, 1)
        self.n += 1

    def settle(self):
        if self.n:
            self.eng.wait_ge(self.sem, self.n)

    def settle_but(self, n):
        self.eng.wait_ge(self.sem, self.n - n)

    def link(self, ins):
        self.step(ins)
        self.settle()


class Arena:

    def __init__(self, tensor, at, end):
        self.tensor, self.at, self.end = tensor, at, end

    def take(self, *shape, dtype=F32, parts=P):
        n = int(np.prod(shape))
        words = n if dtype != BF16 else n // 2
        view = self.tensor[0:parts, self.at:self.at + words]
        self.at += words
        assert self.at <= self.end, (self.at, self.end)
        if dtype != F32:
            view = view.bitcast(dtype)
        names = "abcde"[:len(shape)]
        if len(shape) > 1:
            sizes = {c: s for c, s in zip(names, shape)}
            view = view.rearrange(f"p ({' '.join(names)}) -> p {' '.join(names)}", **sizes)
        return view


def spread(ap, axis, n):
    shape = list(ap.shape)
    shape.insert(axis, n)
    return ap.unsqueeze(axis).broadcast_to(shape)


def build(nc, ins, out, stages="EAPSM"):
    ctx = ExitStack()
    with ctx:
        def sb(name, shape, dt=F32):
            return ctx.enter_context(nc.sbuf_tensor(name, shape, dt))

        def sem(name):
            return ctx.enter_context(nc.semaphore(name))

        B = [ctx.enter_context(nc.psum_tensor(f"bank{i}", [P, 512], F32)) for i in range(8)]

        w_qkv = sb("w_qkv", [P, 3, KD, D])
        w_beta = sb("w_beta", [P, KD, H])
        conv_w = sb("conv_w", [P, 3 * KD, TAPS])
        short_w = sb("short_w", [P, KD, SHORT])
        long_w = sb("long_w", [P, LONG])
        mlp1_a = sb("mlp1_a", [P, KD, D])
        mlp1_s = sb("mlp1_s", [H * 16, H, D])
        mlp1_b = sb("mlp1_b", [P, KD])
        mlp2_w = sb("mlp2_w", [P, H, KD, H * 4])
        mlp2_b = sb("mlp2_b", [P, 4])
        temp = sb("temp", [P, 4])
        res_gate = sb("res_gate", [P, H])
        norm_w = sb("norm_w", [P, 1])
        o_w = sb("o_w", [P, KD, D])
        proj = sb("proj", [EMB_LOW, D])
        gamma = sb("gamma", [P, D])
        w_sim = sb("w_sim", [P, KD, 2 * PH * NK])
        w_in = sb("w_in", [P, KD, 2 * DI])
        b_in = sb("b_in", [P, 2 * DI // P])
        w_B = sb("w_B", [P, DI // P, DS])
        w_C = sb("w_C", [DS, DI])
        skip_D = sb("skip_D", [P, DI // P])
        w_out = sb("w_out", [P, DI // P, D])
        b_out = sb("b_out", [P, D])
        gate_w = sb("gate_w", [P, KD, NE])
        gate_b = sb("gate_b", [P, NE])
        b1_shared = sb("b1_shared", [P, 2, FC])
        tile_no = sb("tile_no", [P, TILES])
        region_at = sb("region_at", [P, NE])
        strict = sb("strict", [P, P], BF16)
        ones_b = sb("ones_b", [P, P], BF16)
        restart = sb("restart", [P, NT, NE])
        all_hot = sb("all_hot", [P, BATCH * NT, TAKE, NE])
        all_rank = sb("all_rank", [P, BATCH * NT, TAKE])
        all_gate = sb("all_gate", [P, BATCH * NT, TAKE])
        count = sb("count", [P, NE])
        b2_all = sb("b2_all", [NE + 1, D])
        ident = sb("ident", [P, P])
        level_mask = sb("level_mask", [P, LEVELS, P])
        causal = sb("causal", [P, P])
        flips = sb("flips", [P, 3, P])
        iota_x = sb("iota_x", [P, P, TB], BF16)
        iota_y = sb("iota_y", [P, YC, TB], BF16)
        decay = sb("decay", [DS, T])

        hid = sb("hid", [P, NT, D])
        xn = sb("xn", [P, NT, D])
        xT = sb("xT", [P, KD, T])
        ids = sb("ids", [P, NT], I32)
        ids_f = sb("ids_f", [P, NT])
        id_low = sb("id_low", [P, 4, NT])
        id_ge = sb("id_ge", [P, 4, NT])
        id_mask = sb("id_mask", [P, 4, NT])
        id_row = sb("id_row", [P, 4, NT], U32)
        ln_part = sb("ln_part", [P, NT, 6])
        ln_mv = sb("ln_mv", [P, NT, 2])
        ln_ve = sb("ln_ve", [P, 2, NT])
        ln_sd = sb("ln_sd", [P, 2, NT])
        ln_r = sb("ln_r", [P, NT])
        ln_len = sb("ln_len", [P, NT])

        base_d = nc.dram_tensor("base_d", (BATCH, P, NT, D), F32).ap()
        rows_d = nc.dram_tensor("rows_d", (NE * REGION, D), F32).ap()
        outs_d = nc.dram_tensor("outs_d", (TILES * TILE, D), F32).ap()

        ARENA = 34880
        arena_t = sb("arena", [P, ARENA])

        keys_in = sem("keys_in")
        loads = sem("loads")
        late_loads = sem("late_loads")
        made = sem("made")
        iter_done = sem("iter_done")
        go_on = sem("go_on")
        names = [
            "dve_step",
            "ids_in", "rows_ready", "embedded",
            "ln_var", "ln_std", "ln_out", "turn_ps", "turn_sb",
            "toep_in0", "toep_in1", "long_ready", "long_ps", "long_tok",
            "qkv_ps", "pre_ready", "conv_ready", "silu_ready", "beta_ps", "beta_ready", "tok_ps", "tok_ready",
            "ss_ready", "ss_root", "unit_ready", "unitT_ps", "unitT_ready", "window_ps", "window_ready",
            "short_ready", "short_ps", "short_tok", "fir_ps", "fir_ready",
            "gram_ps", "gram_ready", "lm_ready", "u0_ready", "t0_ps", "t0_ready", "p_ps", "p_ready",
            "d_ps", "tu_ready", "w_ps", "w_ready", "attn_ps", "attn_ready", "ua_ps", "ua_ready",
            "do_ps", "do_ready", "ds_ps", "ds_ready",
            "l2_ready", "l2_root", "stat_ready", "stat_ps", "statT_ready", "h1_ps", "h1_ready", "h1_all_ps", "h1_all", "h1_sum", "logit_ps", "lgT_ready", "lg_ps",
            "lg_ready", "lg_exp", "mix_ss", "mix_root", "mix_ready", "o_ps", 
            "sim_ps", "sim_ready", "sim_used", "score_ready", "score_exp", "entry_ready", "entT_ready",
            "entry_ps", "hot_ready", "cell_ps", "cell_ready",
            "tab_in0", "tab_in1", "up_in", "shared_in", "down_ps", "down_act", "up_ps", "hid_peer",
            "xz_ps", "xz_ready", "state_ps", "state_ready", "c_ps", "y_ready", "so_ps",
            "gl_ps", "gl_ready", "gl_exp", "gate_ready", "gate_ps", "gateT_ready", 
            "e1_ps", "e1_ready", "e2_ps", "e2_used", "bias_ps", "hid_out",
            "sel_ready", "rank_ps", "slot_ready",
        ]
        scattered = sem("scattered")
        routed = sem("routed")
        mix_step = sem("mix_step")
        padded = sem("padded")
        rw_in = [sem(f"rw_in{p}") for p in range(RING)]
        x_in = [sem(f"x_in{p}") for p in range(RING)]
        xt_ps, xt_ready, m1_ps, m1_ready, m2_ps, m2_ready = (
            sem(n) for n in ("xt_ps", "xt_ready", "m1_ps", "m1_ready", "m2_ps", "m2_ready"))
        y_stored = [sem(f"y_stored{p}") for p in range(RING)]
        base_in, mixed, final_out = (sem(n) for n in ("base_in", "mixed", "final_out"))
        gathered = [sem(f"gathered{b}") for b in range(BATCH)]
        S = {n: sem(n) for n in names}
        stored = sem("stored")
        attn_names = names[names.index("toep_in0"):names.index("sim_ps")]
        peer_names = [n for n in names[names.index("sim_ps"):names.index("xz_ps")] if n not in ("up_ps", "shared_in")]
        first_ids, first_step, first_rows, first_embedded = (
            sem(n) for n in ("first_ids", "first_step", "first_rows", "first_embedded"))
        zeros_ready = sem("zeros_ready")
        rows_in = sem("rows_in")


        toep_in, tab_in = (S["toep_in0"], S["toep_in1"]), (S["tab_in0"], S["tab_in1"])

        block = ctx.enter_context(nc.Block())

        a = Arena(arena_t, 0, ARENA)
        feats = a.take(NT, 4, D)
        win = a.take(2 * NT, D)
        vpad = a.take(KD, T + LONG - 1)
        qk_tok = a.take(2, NT, D)
        kb = a.take(NT, D)
        vb = a.take(NT, D)
        unitT = a.take(3, KD, T)
        beta = a.take(NT * H)
        ss = a.take(2 * NT * H)
        ss_sd = a.take(2 * NT * H)
        unit = a.take(2 * NT * H)
        early = a.at
        zeros = kb[:, 0:HALF]
        a = Arena(arena_t, early, ARENA)
        pre = a.take(3 * KD, T + TAPS - 1)
        conv = a.take(3 * KD, T)
        toep = [a.take(64, 64) for _ in range(2)]
        sq = a.take(2, NT, D)
        a = Arena(arena_t, early, ARENA)
        neg_wT = a.take(NT, KD, P)
        u_adj = a.take(D)
        state = a.take(KD, DH)
        stats = a.take(NT, H, 4, 4)
        st_sum, st_abs, st_css, st_mean2, st_l2 = (a.take(NT, 4, H) for _ in range(5))
        stats_mean = a.take(NT, 4, H)
        statT = a.take(T, parts=H * 16)
        lgT = statT[0:H * 4, :]
        lg, lg_e, lg_p = (a.take(NT, H, 4) for _ in range(3))
        lg_m, lg_s, lg_r = (a.take(NT, H) for _ in range(3))
        attn_m = a.take(2, H, P)
        cent = a.take(NT, 4 * H, DH)
        short_T = a.take(KD, T)
        scratch = a.at
        T_m = a.take(NT, H, P)
        U_m = a.take(NT, H, P)
        M_T = a.take(NT, H, P)
        L_T = a.take(NT, H, P)
        long_T = a.take(2, T)
        emb = a.take(NT, D)
        P_m = win[:, :, :].rearrange("p w c -> p (w c)").rearrange("p (t h c) -> p t h c", t=NT, h=H)
        a = Arena(arena_t, scratch, ARENA)
        h1 = a.take(2, KD, T)
        h1_all = a.take(KD, T)
        mix = cent[:, :, :, :].rearrange("p t (k h) d -> p t k h d", k=4)
        o_tok = h1[:, :, :, :].rearrange("p a b c -> p (a b c)")[:, 0:NT * D].rearrange("p (t c) -> p t c", t=NT)
        o_sq = h1[:, :, :, :].rearrange("p a b c -> p (a b c)")[:, NT * D:2 * NT * D].rearrange("p (t c) -> p t c", t=NT)
        oT = short_T

        embed = Arena(arena_t, early, ARENA)
        rows = embed.take(NT, EMB_ALL)
        low = embed.take(NT, EMB_LOW)
        lowT = embed.take(T, parts=EMB_LOW)

        a = Arena(arena_t, 0, ARENA)
        grid = a.take(XC, T)
        entT_x = a.take(T, dtype=BF16)
        entT_y = a.take(T, dtype=BF16)
        entT_w = a.take(3, T, dtype=BF16)
        hot_at = a.at
        hots = [(a.take(P, TB, dtype=BF16), a.take(YC, TB, dtype=BF16), a.take(3, YC, TB, dtype=BF16))
                for _ in range(2)]
        tab_u = a.take(XC, D)
        tab_end = a.at
        tab_d = Arena(arena_t, ARENA - 2 * 2 * D, ARENA).take(2, 2, KD, P)
        a = Arena(arena_t, hot_at, tab_end)
        sim = a.take(2, 2 * PH, NK)
        cand = a.take(NT * PH, PAIRS)
        look = Arena(arena_t, hot_at, tab_end).take(TOPK, TOPK * NT * PH, dtype=BF16)
        a.at = max(a.at, hot_at + TOPK * TOPK * NT * PH // 2)
        w_rest = Arena(arena_t, hot_at, ARENA).take(T)
        val = a.take(2, NT, PH, TOPK)
        key = a.take(2, NT, PH, TOPK, dtype=U32)
        top = a.take(NT * PH, TOPK)
        pos = a.take(NT * PH, TOPK, dtype=U32)
        e_w = a.take(NT * PH, TOPK)
        e_x, e_y, e_far, e_gate = (a.take(NT, TOPK, PH) for _ in range(4))
        e_s = a.take(NT * PH)
        e_r = a.take(NT * PH)
        keyx, keyy, key_d, pos_b, col_b = (a.take(TOPK, NT * PH, dtype=BF16) for _ in range(5))

        a = Arena(arena_t, 0, ARENA)
        xz = a.take(2 * DI // P, T)
        y = a.take(DI // P, T)
        drive = a.take(T, parts=DS)
        states = a.take(T, parts=DS)

        a = Arena(arena_t, 0, ARENA)
        gl = a.take(NT, NE)
        gm = a.take(NT)
        ge = a.take(NT, NE)
        gs, gr = a.take(NT), a.take(NT)
        garr = a.take(NT, NE + 5)
        gtop = a.take(NT, 8)
        gtake = a.take(NT, 8)
        gated = a.take(NT, NE + 1)
        gatedT = a.take(T, parts=NE + 1)
        moe_h = a.take(2, FC, T)
        assert a.at <= 8192
        a.at = 8192
        w1_shared = a.take(2, KD, FF)
        w2_shared = a.take(2, FC, D)
        sel, nth, rank, slot = (a.take(NT, NE) for _ in range(4))
        sel_b = a.take(NT, NE + 1, dtype=BF16)
        hot3 = a.take(NT, TAKE, NE)
        pick3 = a.take(NT, TAKE, NE)
        rank3, slot3, gate3 = (a.take(NT, TAKE) for _ in range(3))
        slot_u = a.take(NT, TAKE, dtype=U32)

        a = Arena(arena_t, 0, ARENA)
        r_w1 = a.take(RING, KD, FF)
        r_w2 = a.take(RING, FC, D)
        r_b1 = a.take(RING, FC)
        r_x = a.take(RING, HALF, D)
        r_xT = a.take(RING, KD, TILE)
        r_h = a.take(RING, FC, TILE)
        spent = a.at
        r_y = a.take(RING, HALF, D)
        n_tiles, t_start, t_sum, t_ahead, t_row0, t_jump = (a.take(NE) for _ in range(6))
        t_step = a.take(1)
        t_int = a.take(NE, dtype=I32)
        one_row = a.take(NE)
        t_ge = a.take(TILES, NE)
        t_gs = a.take(TILES, NE)
        t_exp, t_min, t_row = (a.take(TILES) for _ in range(3))
        tile_exp = a.take(TILES, dtype=I32)
        tile_row = a.take(TILES, dtype=I32)
        y_pick = a.take(BATCH * NT, TAKE, NE)
        y_slot = a.take(BATCH * NT, TAKE)
        y_slot_u = a.take(BATCH * NT, TAKE, dtype=U32)
        f_base = a.take(BATCH * NT, D)
        f_rows = Arena(arena_t, 0, spent).take(BATCH * NT, TAKE, D)

        n_loads, n_late = [0], [0]

        def load(eng, dst, src):
            eng.dma_start(dst, src).then_inc(loads, 16)
            n_loads[0] += 16

        def load_late(eng, dst, src):
            eng.dma_start(dst, src).then_inc(late_loads, 16)
            n_late[0] += 16

        def setup_sync(sp):
            sp.dma_start(wq_sb, ins["wq"].rearrange("(c p) n -> p c n", p=P)).then_inc(keys_in, 16)
            sp.dma_start(keys_sb, ins["keysT"].rearrange("c p n -> p c n")).then_inc(keys_in, 16)
            for i, n in enumerate(("q_wT", "k_wT", "v_wT")):
                load(sp, w_qkv[:, i], ins[n].rearrange("(k p) n -> p k n", p=P))
            load(sp, w_beta[:, :, :], ins["b_wT"].rearrange("(k p) n -> p k n", p=P))
            for i, n in enumerate(("q_cw", "k_cw", "v_cw")):
                load(sp, conv_w[:, KD * i:KD * (i + 1), :], ins[n].rearrange("(k p) n -> p k n", p=P))
            load(sp, short_w[:, :, :], ins["fir_short"].rearrange("(k p) n -> p k n", p=P))
            load(sp, long_w[:, :], ins["long_w"])
            load(sp, mlp1_a[:, :, :], ins["mlp1_aT"].rearrange("(k p) n -> p k n", p=P))
            load(sp, mlp1_s[:, :, :], ins["mlp1_sT"].rearrange("h p n -> p h n"))
            load(sp, mlp1_b[:, :], ins["mlp1_b"])
            load(sp, mlp2_w[:, :, :, :], ins["mlp2_wT"].rearrange("h (k p) n -> p h k n", p=P))
            load(sp, mlp2_b[:, :], ins["mlp2_b"].partition_broadcast(P))
            load(sp, temp[:, 0:1], ins["logit_temp"].partition_broadcast(P))
            load(sp, res_gate[:, :], ins["conv_res"].partition_broadcast(P))
            load(sp, norm_w[:, :], ins["norm_w"])
            load(sp, o_w[:, :, :], ins["o_wT"].rearrange("(k p) n -> p k n", p=P))
            load(sp, proj[:, :], ins["proj"])
            load(sp, gamma[:, :], ins["gamma"].partition_broadcast(P))
            load(sp, ident[:, :], ins["c_ident"])
            load(sp, level_mask[:, :, :], ins["c_levels"].rearrange("l p n -> p l n"))
            load(sp, causal[:, :], ins["c_causal"])
            load(sp, flips[:, :, :], ins["c_flips"])
            load(sp, iota, ins["c_iota"].partition_broadcast(P))
            load_late(sp, w_in[:, :, :], ins["W_inT"].rearrange("(k p) n -> p k n", p=P))
            load_late(sp, b_in[:, :], ins["b_in"])
            load_late(sp, w_B[:, :, :], ins["W_BT"].rearrange("(k p) n -> p k n", p=P))
            load_late(sp, w_C[:, :], ins["W_CT"])
            load_late(sp, skip_D[:, :], ins["D"])
            load_late(sp, w_out[:, :, :], ins["W_outT"].rearrange("(k p) n -> p k n", p=P))
            load_late(sp, b_out[:, :], ins["b_out"].partition_broadcast(P))
            load_late(sp, gate_w[:, :, :], ins["gW"].rearrange("(k p) n -> p k n", p=P))
            load_late(sp, gate_b[:, :], ins["gb"].partition_broadcast(P))
            load_late(sp, b1_shared[:, :, :], ins["b1"][NE:NE + 2].rearrange("e p k -> p e k"))
            load_late(sp, tile_no[:, :], ins["c_iota"][0:TILES].partition_broadcast(P))
            load_late(sp, region_at[:, :], ins["c_region"].partition_broadcast(P))
            load_late(sp, restart[:, :, :].rearrange("p t e -> p (t e)"), ins["c_restart"].partition_broadcast(P))
            load_late(sp, b2_all[:, :], ins["b2"])
            sp.wait_ge(zeros_ready, 1)
            for e in range(NE):
                sp.dma_start(rows_d[e * REGION:e * REGION + TILE].rearrange("(h p) c -> p h c", p=P), zeros)\
                    .then_inc(padded, 16)

        a = Arena(arena_t, 0, ARENA)
        wq_sb = a.take(2 * PH, D)
        keys_sb = a.take(2 * PH, NK)
        iota = a.take(P)

        def setup_tensor(pe):
            pe.wait_ge(keys_in, 32)
            for c in range(2 * PH):
                for k in range(KD):
                    last = nc.tensor.matmul(B[2 * k + c // PH][:, (c % PH) * NK:(c % PH + 1) * NK],
                                            wq_sb[:, c, k * P:(k + 1) * P], keys_sb[:, c, :],
                                            start=True, stop=True)
            last.then_inc(made, 1)

        def setup_scalar(act):
            act.wait_ge(loads, n_loads[0])
            act.wait_ge(made, 1)
            for k in range(KD):
                for half in range(2):
                    nc.scalar.copy(w_sim[:, k, half * 512:(half + 1) * 512], B[2 * k + half][:, :]).then_inc(made, 1)
            nc.scalar.activation(temp[:, 1:2], temp[:, 0:1], ACT.Abs).then_inc(made, 1)
            act.wait_ge(made, 6)
            nc.scalar.activation(temp[:, 2:3], temp[:, 1:2], ACT.Exp, scale=-1.0).then_inc(made, 1)
            act.wait_ge(made, 7)
            nc.scalar.activation(temp[:, 3:4], temp[:, 2:3], ACT.Ln, bias=1.0).then_inc(made, 1)
            nc.scalar.activation(res_gate[:, :], res_gate[:, :], ACT.Sigmoid).then_inc(made, 1)

        def setup_vector(dve):
            dve.wait_ge(loads, n_loads[0])
            dve.wait_ge(made, 9)
            nc.vector.scalar_tensor_tensor(temp[:, 1:2], temp[:, 0:1], 0.0, temp[:, 3:4],
                                           ALU.max, ALU.add).then_inc(made, 1)
            dve.wait_ge(made, 10)
            nc.vector.reciprocal(temp[:, 0:1], temp[:, 1:2]).then_inc(made, 1)
            nc.vector.memset(decay[:, :], 0.9).then_inc(made, 1)
            nc.vector.tensor_scalar(o_w[:, :, :], o_w[:, :, :], norm_w[:, 0:1], None, ALU.mult).then_inc(made, 1)
            nc.vector.tensor_copy(iota_x[:, :, :], spread(iota, 2, TB)).then_inc(made, 1)
            nc.vector.tensor_copy(iota_y[:, :, :], spread(iota[:, 0:YC], 2, TB)).then_inc(made, 1)

            nc.vector.tensor_tensor(strict[:, :], causal[:, :], ident[:, :], ALU.subtract).then_inc(made, 1)
            nc.vector.memset(ones_b[:, :], 1.0).then_inc(made, 1)
            nc.vector.memset(count[:, :], 0.0).then_inc(made, 1)

        MADE = 18
        inv_temp = temp[:, 0:1]

        def ids_sync(sp, b, ids_in):
            sp.dma_start(ids[:, :], ins["x"][bass.ds(b, 1)].rearrange("a p t -> p (a t)")).then_inc(ids_in, 16)

        def ids_vector(dve, v, ids_in, rows_ready):
            dve.wait_ge(ids_in, 16)
            v.link(nc.vector.tensor_copy(ids_f[:, :], ids[:, :]))
            for i in range(4):
                lo, hi = CUTOFFS[i], CUTOFFS[i + 1]
                v.step(nc.vector.tensor_scalar(id_low[:, i], ids_f[:, :], float(-lo), 0.0, ALU.add, ALU.max))
                v.step(nc.vector.tensor_scalar(id_ge[:, i], ids_f[:, :], float(lo), None, ALU.is_ge))
            v.settle()
            for i in range(4):
                lo, hi = CUTOFFS[i], CUTOFFS[i + 1]
                v.step(nc.vector.scalar_tensor_tensor(id_mask[:, i], ids_f[:, :], float(hi), id_ge[:, i],
                                                      ALU.is_lt, ALU.mult))
                nc.vector.tensor_scalar(id_row[:, i], id_low[:, i], float(hi - lo - 1), None,
                                        ALU.min).then_inc(rows_ready, 1)
            v.settle()

        def gather_rows(pool):
            for t in range(NT):
                for i in range(4):
                    nc.gpsimd.indirect_dma_start(
                        rows[:, t, EMB_AT[i]:EMB_AT[i] + EMB[i]], None, ins[f"emb{i}"],
                        bass.IndirectOffsetOnAxis(ap=id_row[:, i, t:t + 1], axis=0)).then_inc(rows_in, 16)

        def embed_rows_vector(dve, v, gathered_rows, done):
            dve.wait_ge(rows_in, gathered_rows)
            for t in range(NT):
                for i in range(4):
                    dst = emb[:, t, :] if i == 0 else low[:, t, EMB_AT[i] - D:EMB_AT[i] - D + EMB[i]]
                    ins_ = nc.vector.tensor_scalar(dst, rows[:, t, EMB_AT[i]:EMB_AT[i] + EMB[i]],
                                                   id_mask[:, i, t:t + 1], 16.0, ALU.mult, ALU.mult)
                    if t == NT - 1 and i == 3:
                        ins_.then_inc(done, 1)
                    else:
                        v.step(ins_)

        def embed_turn_tensor(pe, done, at):
            pe.wait_ge(done, at + 1)
            for t in range(NT):
                last = nc.tensor.transpose(B[6][0:EMB_LOW, t * P:(t + 1) * P], low[:, t, :], ident[:, :])
            last.then_inc(done, 1)

        def embed_scalar(act, done, at):
            act.wait_ge(done, at + 2)
            nc.scalar.copy(lowT, B[6][0:EMB_LOW, :]).then_inc(done, 1)

        def embed_tensor(pe, done, at):
            pe.wait_ge(done, at + 3)
            for t in range(NT):
                last = nc.tensor.matmul(B[6 + t // 2][:, (t % 2) * D:(t % 2 + 1) * D], lowT[:, t * P:(t + 1) * P],
                                        proj[:, :], start=True, stop=True)
            last.then_inc(done, 1)

        def embed_vector(dve, v, done, at):
            dve.wait_ge(done, at + 4)
            for half in range(2):
                t2 = slice(2 * half, 2 * half + 2)
                v.step(nc.vector.tensor_tensor(emb[:, t2, :], emb[:, t2, :],
                                               B[6 + half][:, :].rearrange("p (t c) -> p t c", t=2), ALU.add))
            moments(v, emb, range(NT))
            v.settle()

        def moments(v, src, tiles):
            v.settle()
            for t in tiles:
                v.step(nc.vector.bn_stats(ln_part[:, t, :], src[:, t, :]))

        def norm_vector(dve, v, use, src, rms=False):
            v.settle()
            for t in range(NT):
                v.step(nc.vector.bn_aggr(ln_mv[:, t, :], ln_part[:, t, :]))
            v.settle()
            v.step(nc.vector.tensor_scalar(ln_ve[:, 1, :], ln_mv[:, :, 1], float(D), None, ALU.mult))
            nc.vector.tensor_scalar(ln_ve[:, 0, :], ln_mv[:, :, 1], 1e-5, None, ALU.add).then_inc(S["ln_var"], 1)
            dve.wait_ge(S["ln_std"], use + 1)
            v.link(nc.vector.reciprocal(ln_r[:, :], ln_sd[:, 0, :]))
            if rms:
                v.link(nc.vector.tensor_tensor(ln_len[:, :], ln_sd[:, 1, :], ln_r[:, :], ALU.mult))
                v.link(nc.vector.tensor_scalar(ln_len[:, :], ln_len[:, :], 1e-12, None, ALU.max))
                v.link(nc.vector.reciprocal(ln_len[:, :], ln_len[:, :]))
                v.link(nc.vector.tensor_tensor(ln_r[:, :], ln_r[:, :], ln_len[:, :], ALU.mult))
            for t in range(NT):
                nc.vector.tensor_scalar(xn[:, t, :], src[:, t, :], ln_mv[:, t, 0:1], ln_r[:, t:t + 1],
                                        ALU.subtract, ALU.mult).then_inc(S["ln_out"], 1)

        def norm_scalar(act, use):
            act.wait_ge(S["ln_var"], use + 1)
            nc.scalar.activation(ln_sd[:, :, :], ln_ve[:, :, :], ACT.Sqrt).then_inc(S["ln_std"], 1)

        def turn_tensor(pe, src, turn, first, second):
            for k in range(KD):
                bank = (first, second)[k]
                for t in range(NT):
                    last = nc.tensor.transpose(B[bank][:, t * P:(t + 1) * P], src[:, t, k * P:(k + 1) * P], ident[:, :])
                last.then_inc(S["turn_ps"], 1)

        def turn_scalar(act, dst, turn, first, second):
            for k in range(KD):
                act.wait_ge(S["turn_ps"], KD * turn + k + 1)
                nc.scalar.copy(dst[:, k, :], B[(first, second)[k]][:, :]).then_inc(S["turn_sb"], 1)

        def turned(eng, turn):
            eng.wait_ge(S["turn_sb"], KD * (turn + 1))

        SHORT_AT, LONG_AT = (3, 2), (6, 1)
        TAPS_AHEAD = 36

        def attn_sync(sp, b):
            for q in range(2):
                f = ins["fir_long"]
                src = bass.AP(tensor=f.tensor, offset=64 * q * 192 + 1, ap=[[1, P], [192, 64], [1, 64]])
                sp.dma_start(toep[q], src).then_inc(toep_in[q], 16)
            ids_sync(sp, b + 1, S["ids_in"])

        def attn_tensor(pe):
            turned(pe, 0)
            for i in range(3):
                for c in range(KD):
                    for k in range(KD):
                        last = nc.tensor.matmul(B[2 * i + c][:, :], w_qkv[:, i, k, c * P:(c + 1) * P], xT[:, k, :],
                                                start=(k == 0), stop=(k == KD - 1))
                    last.then_inc(S["qkv_ps"], 1)
            for t in range(NT):
                for k in range(KD):
                    last = nc.tensor.matmul(B[6][:, t * H:(t + 1) * H], xT[:, k, t * P:(t + 1) * P], w_beta[:, k, :],
                                            start=(k == 0), stop=(k == KD - 1))
            last.then_inc(S["beta_ps"], 1)
            pe.wait_ge(S["pre_ready"], 6)
            for i in range(3):
                pe.wait_ge(S["silu_ready"], KD * (i + 1))
                for half in range(2):
                    for t in range(2 * half, 2 * half + 2):
                        for c in range(KD):
                            src = (conv[:, 2 * i + c, t * P:(t + 1) * P] if i < 2 else
                                   vpad[:, c, LONG - 1 + t * P:LONG - 1 + (t + 1) * P])
                            last = nc.tensor.transpose(B[2 * i + half][:, (t % 2) * D + c * P:(t % 2) * D + (c + 1) * P],
                                                       src, ident[:, :])
                    last.then_inc(S["tok_ps"], 1)
            pe.wait_ge(S["tok_ready"], 6)
            v_tok = lambda t: feats[:, t:t + 2, 3, :]
            for n in range(2):
                nc.tensor.matmul(B[n][:, :], flips[:, 0, :], v_tok(2 * n), start=True, stop=True).then_inc(S["window_ps"], 1)
            nc.tensor.matmul(B[2][:, 0:D], flips[:, 1, :], feats[:, 0, 3, :], start=True, stop=True)
            nc.tensor.matmul(B[2][:, D:2 * D], flips[:, 1, :], feats[:, 1, 3, :], start=True, stop=False)
            nc.tensor.matmul(B[2][:, D:2 * D], flips[:, 2, :], feats[:, 0, 3, :], start=False, stop=True)\
                .then_inc(S["window_ps"], 1)
            nc.tensor.matmul(B[3][:, :], flips[:, 1, :], v_tok(2), start=True, stop=False)
            nc.tensor.matmul(B[3][:, :], flips[:, 2, :], v_tok(1), start=False, stop=True).then_inc(S["window_ps"], 1)
            def long_fir(q):
                pe.wait_ge(toep_in[q], 16)
                for c in range(64):
                    last = nc.tensor.matmul(B[6 + q % 2][0:64, c * 8:(c + 1) * 8], toep[q][:, c, :],
                                            win[:, :, 64 * q + c], start=True, stop=True)
                last.then_inc(S["fir_ps"], 1)

            pe.wait_ge(S["window_ready"], 4)
            pe.wait_ge(S["beta_ready"], 1)
            long_fir(0)
            long_fir(1)
            pe.wait_ge(S["unit_ready"], 1)
            for i in range(3):
                for c in range(KD):
                    for t in range(NT):
                        src = qk_tok[:, i, t, c * P:(c + 1) * P] if i < 2 else kb[:, t, c * P:(c + 1) * P]
                        last = nc.tensor.transpose(B[2 * i + c][:, t * P:(t + 1) * P], src, ident[:, :])
                    last.then_inc(S["unitT_ps"], 1)
            pe.wait_ge(S["unitT_ready"], 6)
            for n in range(4):
                odd = n % 2
                r = slice(64 * odd, 64 * odd + 64)
                for t in range(2 * (n // 2), 2 * (n // 2) + 2):
                    tt = slice(t * P, (t + 1) * P)
                    for c in range(KD):
                        at = (KD * (t % 2) + c) * P
                        last = nc.tensor.matmul(B[n][:, at:at + P], unitT[r, 1, c, tt], unitT[r, 2, c, tt],
                                                start=True, stop=True)
                last.then_inc(S["gram_ps"], 1)
            for t in range(NT):
                pe.wait_ge(S["u0_ready"], t + 1)
                if t >= 2:
                    pe.wait_ge(S["t0_ready"], t - 1)
                for h in range(H):
                    last = nc.tensor.transpose(B[4 + t % 2][:, h * P:(h + 1) * P], U_m[:, t, h, :], ident[:, :])
                last.then_inc(S["t0_ps"], 1)
            for lv in range(1, LEVELS):
                n = (lv - 1) * NT
                for t in range(NT):
                    pe.wait_ge(S["lm_ready"], n + t + 1)
                    if lv == 1:
                        pe.wait_ge(S["t0_ready"], NT)
                    else:
                        pe.wait_ge(S["tu_ready"], n - NT + t + 1)
                    if n + t >= 2:
                        pe.wait_ge(S["p_ready"], n + t - 1)
                    for h in range(H):
                        last = nc.tensor.matmul(B[4 + t % 2][:, h * P:(h + 1) * P], L_T[:, t, h, :], T_m[:, t, h, :],
                                                start=True, stop=True)
                    last.then_inc(S["p_ps"], 1)
                    if t >= 1:
                        delta_products(pe, lv, t - 1)
                    if (lv, t) == LONG_AT:
                        pe.wait_ge(S["long_ready"], 1)
                        pe.wait_ge(S["short_tok"], 1)
                        for u in range(NT):
                            last = nc.tensor.transpose(B[6][:, u * P:(u + 1) * P], long_T[:, 0, u * P:(u + 1) * P], ident[:, :])
                        last.then_inc(S["long_ps"], 1)
                    if (lv, t) == SHORT_AT:
                        pe.wait_ge(S["short_ready"], KD)
                        pe.wait_ge(S["fir_ready"], 4)
                        for half in range(2):
                            for u in range(2 * half, 2 * half + 2):
                                for c in range(KD):
                                    at = (u % 2) * D + c * P
                                    last = nc.tensor.transpose(B[6 + half][:, at:at + P],
                                                               short_T[:, c, u * P:(u + 1) * P], ident[:, :])
                            last.then_inc(S["short_ps"], 1)
                delta_products(pe, lv, NT - 1)
            for t in range(NT):
                pe.wait_ge(S["tu_ready"], (LEVELS - 2) * NT + t + 1)
                for h in range(H):
                    r = slice(64 * (h % 2), 64 * (h % 2) + 64)
                    last = nc.tensor.matmul(B[4 + t // 2][r, (t % 2) * D + (h // 2) * P:(t % 2) * D + (h // 2 + 1) * P],
                                            kb[:, t, h * DH:(h + 1) * DH], U_m[:, t, h, :], start=True, stop=True)
                last.then_inc(S["w_ps"], 1)
            pe.wait_ge(S["w_ready"], NT)
            for t in range(NT):
                tt = slice(t * P, (t + 1) * P)
                rows_of = lambda h: slice(64 * (h % 2), 64 * (h % 2) + 64)
                cols_of = lambda h: slice((h // 2) * DH, (h // 2 + 1) * DH)
                if t:
                    pe.wait_ge(S["attn_ready"], 2 * t)
                for h in HEAD_ORDER:
                    r, c = rows_of(h), h // 2
                    last = nc.tensor.matmul(B[(3, 6)[h % 2]][:, c * P:(c + 1) * P], unitT[r, 1, c, tt],
                                            unitT[r, 0, c, tt], start=True, stop=True)
                last.then_inc(S["attn_ps"], 1)
                if t:
                    pe.wait_ge(S["ua_ready"], 2 * t)
                banks = (0, 4)
                for odd in range(2):
                    for i, h in enumerate((odd, odd + 2)):
                        last = nc.tensor.matmul(B[banks[odd]][:, cols_of(h)], U_m[:, t, h, :],
                                                vb[:, t, h * DH:(h + 1) * DH],
                                                start=(i == 0), stop=(t == 0), skip_group_check=True)
                if t:
                    pe.wait_ge(S["ds_ready"], t)
                    for h in HEAD_ORDER:
                        last = nc.tensor.matmul(B[banks[h % 2]][:, cols_of(h)], neg_wT[rows_of(h), t, h // 2, :],
                                                state[rows_of(h), h // 2, :], start=False, stop=True, skip_group_check=True)
                last.then_inc(S["ua_ps"], 1)
                if t:
                    pe.wait_ge(S["do_ready"], 2 * t)
                    for odd in range(2):
                        for i, h in enumerate((odd, odd + 2)):
                            nc.tensor.matmul(B[(1, 5)[odd]][:, cols_of(h)], unitT[rows_of(h), 0, h // 2, tt],
                                             state[rows_of(h), h // 2, :], start=(i == 0), stop=False,
                                             skip_group_check=True)
                c, k = t // KD, t % KD
                if t == KD:
                    pe.wait_ge(S["h1_all"], 1)
                last = nc.tensor.matmul(B[7][:, :], mlp1_a[:, k, c * P:(c + 1) * P], xT[:, k, :],
                                        start=(k == 0), stop=(k == KD - 1))
                if k == KD - 1:
                    last.then_inc(S["h1_all_ps"], 1)
                pe.wait_ge(S["ua_ready"], 2 * (t + 1))
                if t < NT - 1:
                    for h in HEAD_ORDER:
                        hh = slice(h * DH, (h + 1) * DH)
                        last = nc.tensor.matmul(B[2][rows_of(h), cols_of(h)], qk_tok[:, 1, t, hh],
                                                u_adj[:, hh], start=True, stop=True)
                    last.then_inc(S["ds_ps"], 1)
                pe.wait_ge(S["attn_ready"], 2 * (t + 1))
                for odd in range(2):
                    for i, h in enumerate((odd, odd + 2)):
                        last = nc.tensor.matmul(B[(1, 5)[odd]][:, cols_of(h)], attn_m[:, t % 2, h, :],
                                                u_adj[:, h * DH:(h + 1) * DH], start=(t == 0 and i == 0), stop=True,
                                                skip_group_check=True)
                last.then_inc(S["do_ps"], 1)
            pe.wait_ge(S["stat_ready"], 1)
            for t in range(NT):
                last = nc.tensor.transpose(B[6][0:H * 16, t * P:(t + 1) * P],
                                           stats[:, t].rearrange("p h k s -> p (h k s)"), ident[:, :])
            last.then_inc(S["stat_ps"], 1)
            pe.wait_ge(S["statT_ready"], 1)
            pe.wait_ge(S["do_ready"], 2 * NT)

            def logits(h):
                pe.wait_ge(S["h1_ready"], KD * (h + 1))
                for k in range(KD):
                    last = nc.tensor.matmul(B[7][0:H * 4, :], mlp2_w[:, h, k, :], h1[:, h % 2, k, :],
                                            start=(h == 0 and k == 0), stop=(h == H - 1 and k == KD - 1))
                last.then_inc(S["logit_ps"], 1)

            for h in range(H):
                for c in range(KD):
                    n = KD * h + c
                    if n >= 4:
                        pe.wait_ge(S["h1_sum"], n - 3)
                    nc.tensor.matmul(B[n % 4][:, :], mlp1_s[:, h, c * P:(c + 1) * P], statT,
                                     start=True, stop=True).then_inc(S["h1_ps"], 1)
                if h:
                    logits(h - 1)
            logits(H - 1)
            pe.wait_ge(S["lgT_ready"], 1)
            for t in range(NT):
                last = nc.tensor.transpose(B[6][:, t * H * 4:(t + 1) * H * 4], lgT[:, t * P:(t + 1) * P],
                                           ident[0:H * 4, 0:H * 4])
            last.then_inc(S["lg_ps"], 1)
            pe.wait_ge(S["mix_ready"], 1)
            turn_tensor(pe, o_tok, 1, 0, 1)
            turned(pe, 1)
            for t in range(NT):
                for k in range(KD):
                    last = nc.tensor.matmul(B[2 + t // 2][:, (t % 2) * D:(t % 2 + 1) * D], oT[:, k, t * P:(t + 1) * P],
                                            o_w[:, k, :], start=(k == 0), stop=(k == KD - 1))
                if t % 2:
                    last.then_inc(S["o_ps"], 1)

        def delta_products(pe, lv, t):
            n = (lv - 1) * NT + t
            pe.wait_ge(S["p_ready"], n + 1)
            if n >= 2:
                pe.wait_ge(S["tu_ready"], n - 1)
            if lv < LEVELS - 1:
                for h in range(H):
                    nc.tensor.matmul(B[t % 2][:, h * P:(h + 1) * P], U_m[:, t, h, :], P_m[:, t, h, :],
                                     start=True, stop=True)
            for h in range(H):
                last = nc.tensor.matmul(B[2 + t % 2][:, h * P:(h + 1) * P], P_m[:, t, h, :], U_m[:, t, h, :],
                                        start=True, stop=True)
            last.then_inc(S["d_ps"], 1)

        def attn_scalar(act):
            for i in range(6):
                act.wait_ge(S["qkv_ps"], i + 1)
                nc.scalar.copy(pre[:, i, TAPS - 1:], B[i][:, :]).then_inc(S["pre_ready"], 1)
            for i in range(6):
                act.wait_ge(S["conv_ready"], i + 1)
                dst = conv[:, i, :] if i < 4 else vpad[:, i - 4, LONG - 1:]
                nc.scalar.activation(dst, conv[:, i, :], ACT.Silu).then_inc(S["silu_ready"], 1)
            act.wait_ge(S["beta_ps"], 1)
            nc.scalar.activation(beta, B[6][:, 0:NT * H], ACT.Sigmoid).then_inc(S["beta_ready"], 1)
            for i in range(6):
                act.wait_ge(S["tok_ps"], i + 1)
                half = i % 2
                src = B[i][:, :].rearrange("p (t c) -> p t c", t=2)
                dst = qk_tok[:, i // 2, 2 * half:2 * half + 2, :] if i < 4 else feats[:, 2 * half:2 * half + 2, 3, :]
                nc.scalar.copy(dst, src).then_inc(S["tok_ready"], 1)
            for n in range(4):
                act.wait_ge(S["window_ps"], n + 1)
                first = (1, 5, 0, 4)[n]
                nc.scalar.copy(win[:, first:first + 3:2, :], B[n][:, :].rearrange("p (w c) -> p w c", w=2))\
                    .then_inc(S["window_ready"], 1)
            act.wait_ge(S["ss_ready"], 1)
            nc.scalar.activation(ss_sd, ss, ACT.Sqrt).then_inc(S["ss_root"], 1)
            def fir_windows(q):
                act.wait_ge(S["fir_ps"], q + 1)
                for half in range(2):
                    src = B[6 + q % 2][0:64, :].rearrange("p (c t w) -> p w t c", t=NT, w=2)[:, half]
                    nc.scalar.copy(feats[64 * half:64 * half + 64, :, 1, 64 * q:64 * (q + 1)], src)\
                        .then_inc(S["fir_ready"], 1)

            fir_windows(0)
            fir_windows(1)
            for i in range(6):
                act.wait_ge(S["unitT_ps"], i + 1)
                nc.scalar.copy(unitT[:, i // 2, i % 2, :], B[i][:, :]).then_inc(S["unitT_ready"], 1)
            act.wait_ge(S["fir_ps"], 2)
            for n in range(4):
                act.wait_ge(S["gram_ps"], n + 1)
                t = 2 * (n // 2)
                nc.scalar.copy(M_T[:, t:t + 2, n % 2:H:2],
                               B[n][:, :].rearrange("p (t h c) -> p t h c", t=2, h=KD)).then_inc(S["gram_ready"], 1)
            for t in range(NT):
                act.wait_ge(S["t0_ps"], t + 1)
                nc.scalar.copy(T_m[:, t], B[4 + t % 2][:, :].rearrange("p (h c) -> p h c", h=H)).then_inc(S["t0_ready"], 1)
            for lv in range(1, LEVELS):
                for t in range(NT):
                    n = (lv - 1) * NT + t
                    act.wait_ge(S["p_ps"], n + 1)
                    if n >= NT:
                        act.wait_ge(S["d_ps"], n - NT + 1)
                    nc.scalar.copy(P_m[:, t], B[4 + t % 2][:, :].rearrange("p (h c) -> p h c", h=H))\
                        .then_inc(S["p_ready"], 1)
                    if (lv, t) == LONG_AT:
                        act.wait_ge(S["long_ps"], 1)
                        nc.scalar.copy(feats[:, :, 1, P:D], B[6][:, :].rearrange("p (t c) -> p t c", t=NT))\
                            .then_inc(S["long_tok"], 1)
                    if (lv, t) == SHORT_AT:
                        for half in range(2):
                            act.wait_ge(S["short_ps"], half + 1)
                            nc.scalar.copy(feats[:, 2 * half:2 * half + 2, 0, :],
                                           B[6 + half][:, :].rearrange("p (t c) -> p t c", t=2))\
                                .then_inc(S["short_tok"], 1)
            for t in range(NT):
                act.wait_ge(S["w_ps"], 2 * (t // 2) + 2)
                nc.scalar.mul(neg_wT[:, t], B[4 + t // 2][:, (t % 2) * D:(t % 2 + 1) * D]
                              .rearrange("p (k c) -> p k c", k=KD), -1.0).then_inc(S["w_ready"], 1)
            for t in range(NT):
                act.wait_ge(S["ua_ps"], t + 1)
                if t:
                    act.wait_ge(S["do_ps"], t)
                by_head = lambda x: x.rearrange("p (h d) -> p h d", d=DH)
                for odd in range(2):
                    nc.scalar.copy(by_head(u_adj)[:, odd:H:2], by_head(B[(0, 4)[odd]][:, 0:P])).then_inc(S["ua_ready"], 1)
                act.wait_ge(S["do_ps"], t + 1)
                for odd in range(2):
                    nc.scalar.copy(by_head(feats[:, t, 2, :])[:, odd:H:2], by_head(B[(1, 5)[odd]][:, 0:P]))\
                        .then_inc(S["do_ready"], 1)
                if t % KD == KD - 1:
                    c = t // KD
                    act.wait_ge(S["h1_all_ps"], c + 1)
                    nc.scalar.activation(h1_all[:, c, :], B[7][:, :], ACT.Identity, bias=mlp1_b[:, c:c + 1])\
                        .then_inc(S["h1_all"], 1)
            act.wait_ge(S["l2_ready"], 1)
            nc.scalar.activation(st_l2, st_mean2, ACT.Sqrt).then_inc(S["l2_root"], 1)
            act.wait_ge(S["stat_ps"], 1)
            nc.scalar.copy(statT, B[6][0:H * 16, :]).then_inc(S["statT_ready"], 1)
            for h in range(H):
                for k in range(KD):
                    n = KD * h + k
                    act.wait_ge(S["h1_sum"], n + 1)
                    nc.scalar.activation(h1[:, h % 2, k, :], h1[:, h % 2, k, :], ACT.Gelu_apprx_tanh)\
                        .then_inc(S["h1_ready"], 1)
            act.wait_ge(S["logit_ps"], H)
            nc.scalar.copy(lgT, B[7][0:H * 4, :]).then_inc(S["lgT_ready"], 1)
            act.wait_ge(S["lg_ready"], 1)
            nc.scalar.activation(lg_e, lg_p, ACT.Exp, scale=inv_temp).then_inc(S["lg_exp"], 1)
            act.wait_ge(S["mix_ss"], 1)
            nc.scalar.activation(ss_sd[:, 0:NT * H], ss[:, 0:NT * H], ACT.Sqrt).then_inc(S["mix_root"], 1)
            turn_scalar(act, oT, 1, 0, 1)

        def attn_vector(dve, v, b):
            V = nc.vector
            v.step(V.memset(pre[:, :, 0:TAPS - 1], 0.0))
            v.step(V.memset(vpad[:, :, 0:LONG - 1], 0.0))
            v.settle()
            for i in range(0, 6, 2):
                dve.wait_ge(S["pre_ready"], i + 2)
                for tap in range(TAPS):
                    for j in (i, i + 1):
                        x = pre[:, j, tap:tap + T]
                        w = conv_w[:, j, tap:tap + 1]
                        if tap == 0:
                            v.step(V.tensor_scalar(conv[:, j, :], x, w, None, ALU.mult))
                        elif tap < TAPS - 1:
                            v.step(V.scalar_tensor_tensor(conv[:, j, :], x, w, conv[:, j, :], ALU.mult, ALU.add))
                        else:
                            V.scalar_tensor_tensor(conv[:, j, :], x, w, conv[:, j, :], ALU.mult, ALU.add)\
                                .then_inc(S["conv_ready"], 1)
                    v.settle()
            dve.wait_ge(S["beta_ready"], 1)
            v.step(V.tensor_scalar(beta, beta, 1e-6, None, ALU.max))
            dve.wait_ge(S["tok_ready"], 4)
            v.link(V.tensor_tensor(sq, qk_tok, qk_tok, ALU.mult))
            v.link(V.tensor_reduce(ss, sq.rearrange("p i t (h d) -> p (i t h) d", h=H), AX_X, ALU.add))
            V.tensor_scalar(ss, ss, 1e-6, None, ALU.add).then_inc(S["ss_ready"], 1)
            dve.wait_ge(S["ss_root"], 1)
            v.link(V.reciprocal(unit, ss_sd))
            heads = qk_tok.rearrange("p i t (h d) -> p (i t h) d", h=H)
            v.link(V.tensor_tensor(heads, heads, spread(unit, 2, DH), ALU.mult))
            k_heads = qk_tok[:, 1].rearrange("p t (h d) -> p (t h) d", h=H)
            dve.wait_ge(S["tok_ready"], 6)
            dve.wait_ge(padded, 16 * NE)
            v_heads = feats[:, :, 3, :].rearrange("p t (h d) -> p t h d", h=H)
            v.step(V.tensor_tensor(vb.rearrange("p t (h d) -> p t h d", h=H), v_heads,
                                   spread(beta.rearrange("p (t h) -> p t h", t=NT), 3, DH), ALU.mult))
            V.tensor_tensor(kb.rearrange("p t (h d) -> p (t h) d", h=H), k_heads, spread(beta, 2, DH), ALU.mult)\
                .then_inc(S["unit_ready"], 1)
            ids_vector(dve, v, S["ids_in"], S["rows_ready"])
            def long_tap(tap):
                x = vpad[:, 1, tap:tap + T]
                acc, w = long_T[:, tap % 2, :], long_w[:, tap:tap + 1]
                if tap < 2:
                    v.step(V.tensor_scalar(acc, x, w, None, ALU.mult))
                else:
                    v.settle_but(1)
                    v.step(V.scalar_tensor_tensor(acc, x, w, acc, ALU.mult, ALU.add))

            for tap in range(TAPS_AHEAD):
                long_tap(tap)
            for t in range(NT):
                dve.wait_ge(S["gram_ready"], 2 * (t // 2) + 2)
                v.link(V.tensor_tensor(U_m[:, t], M_T[:, t], spread(level_mask[:, 0, :], 1, H), ALU.mult))
                V.tensor_tensor(U_m[:, t], spread(ident[:, :], 1, H), U_m[:, t], ALU.subtract).then_inc(S["u0_ready"], 1)
            def short_tap(tap):
                v.settle()
                for c in range(KD):
                    x = vpad[:, c, LONG - SHORT + tap:LONG - SHORT + tap + T]
                    w = short_w[:, c, tap:tap + 1]
                    if tap == 0:
                        v.step(V.tensor_scalar(short_T[:, c, :], x, w, None, ALU.mult))
                    elif tap < SHORT - 1:
                        v.step(V.scalar_tensor_tensor(short_T[:, c, :], x, w, short_T[:, c, :], ALU.mult, ALU.add))
                    else:
                        V.scalar_tensor_tensor(short_T[:, c, :], x, w, short_T[:, c, :], ALU.mult, ALU.add)\
                            .then_inc(S["short_ready"], 1)

            def statistics(k, part):
                f = feats[:, :, k, :].rearrange("p t (h d) -> p t h d", h=H)
                cc = cent[:, :, k * H:(k + 1) * H, :]
                v.settle()
                if part == 0:
                    v.step(V.tensor_reduce(st_sum[:, :, k], f, AX_X, ALU.add))
                elif part == 1:
                    v.step(V.tensor_scalar(stats_mean[:, :, k], st_sum[:, :, k], 1.0 / DH, None, ALU.mult))
                    v.step(V.tensor_reduce(st_abs[:, :, k], f, AX_X, ALU.add, apply_absolute_value=True))
                elif part == 2:
                    v.step(V.tensor_tensor(cc, f, spread(stats_mean[:, :, k], 3, DH), ALU.subtract))
                    v.step(V.tensor_tensor(st_mean2[:, :, k], st_sum[:, :, k], stats_mean[:, :, k], ALU.mult))
                elif part == 3:
                    v.step(V.tensor_tensor(cc, cc, cc, ALU.mult))
                else:
                    v.step(V.tensor_reduce(st_css[:, :, k], cc, AX_X, ALU.add))

            def in_pause(n):
                long_at = SHORT
                sum_at = long_at + (LONG - TAPS_AHEAD) // 2
                if n < long_at:
                    short_tap(n)
                elif n < sum_at:
                    tap = TAPS_AHEAD + 2 * (n - long_at)
                    v.settle()
                    long_tap(tap)
                    long_tap(tap + 1)
                elif n == sum_at:
                    v.settle()
                    V.tensor_tensor(long_T[:, 0, :], long_T[:, 0, :], long_T[:, 1, :], ALU.add)\
                        .then_inc(S["long_ready"], 1)
                elif n < sum_at + 16:
                    k, part = (3, 0, 1)[(n - sum_at - 1) // 5], (n - sum_at - 1) % 5
                    if k == 0:
                        dve.wait_ge(S["short_tok"], 2)
                    if k == 1:
                        dve.wait_ge(S["long_tok"], 1)
                    statistics(k, part)

            dve.wait_ge(S["fir_ready"], 4)
            for lv in range(1, LEVELS):
                for t in range(NT):
                    n = (lv - 1) * NT + t
                    dve.wait_ge(S["d_ps"], n + 1)
                    if lv == 1:
                        dve.wait_ge(S["u0_ready"], NT)
                        dve.wait_ge(S["t0_ready"], NT)
                    else:
                        dve.wait_ge(S["tu_ready"], n - NT + 1)
                    if lv < LEVELS - 1:
                        v.step(V.tensor_tensor(T_m[:, t], T_m[:, t], B[t % 2][:, :].rearrange("p (h c) -> p h c", h=H),
                                               ALU.subtract))
                    V.tensor_tensor(U_m[:, t], U_m[:, t], B[2 + t % 2][:, :].rearrange("p (h c) -> p h c", h=H),
                                    ALU.subtract).then_inc(S["tu_ready"], 1)
                    in_pause(n)
            for t in range(NT):
                pause = (LEVELS - 1) * NT + 4 * t
                dve.wait_ge(S["attn_ps"], t + 1)
                if t >= 2:
                    dve.wait_ge(S["do_ps"], t - 1)
                for odd in range(2):
                    V.tensor_tensor(attn_m[:, t % 2, odd:H:2], B[(3, 6)[odd]][:, 0:D].rearrange("p (h c) -> p h c", h=KD),
                                    spread(causal[:, :], 1, KD), ALU.mult).then_inc(S["attn_ready"], 1)
                if t < NT - 1:
                    in_pause(pause)
                    in_pause(pause + 1)
                    dve.wait_ge(S["ds_ps"], t + 1)
                    if t:
                        dve.wait_ge(S["ds_ready"], t)
                        V.tensor_tensor(state, state, B[2][:, 0:P].rearrange("p (k c) -> p k c", k=KD), ALU.add)\
                            .then_inc(S["ds_ready"], 1)
                    else:
                        V.tensor_copy(state, B[2][:, 0:P].rearrange("p (k c) -> p k c", k=KD)).then_inc(S["ds_ready"], 1)
                in_pause(pause + 2)
                in_pause(pause + 3)
            dve.wait_ge(S["do_ready"], 2 * NT)
            for part in range(5):
                statistics(2, part)
            v.settle()
            flat = lambda x: x.rearrange("p t k h -> p (t k h)")
            V.tensor_tensor(flat(st_mean2), flat(st_mean2), flat(st_css), ALU.add).then_inc(S["l2_ready"], 1)
            dve.wait_ge(S["l2_root"], 1)
            for n, (src, mul) in enumerate(((stats_mean, 1.0), (st_css, 1.0 / DH), (st_abs, 1.0 / DH), (st_l2, 1.0))):
                ins_ = V.tensor_scalar(stats[:, :, :, :, n].rearrange("p t h k -> p t k h"), src, mul, None, ALU.mult)
                if n == 3:
                    ins_.then_inc(S["stat_ready"], 1)
                else:
                    v.step(ins_)
            for n in range(H * KD):
                dve.wait_ge(S["h1_ps"], n + 1)
                if n == 0:
                    dve.wait_ge(S["h1_all"], KD)
                if n >= 4:
                    dve.wait_ge(S["logit_ps"], n // KD - 1)
                V.tensor_tensor(h1[:, (n // KD) % 2, n % KD, :], B[n % 4][:, :], h1_all[:, n % KD, :], ALU.add)\
                    .then_inc(S["h1_sum"], 1)
            dve.wait_ge(S["lg_ps"], 1)
            L = B[6][:, 0:NT * H * 4].rearrange("p (t h k) -> p (t h) k", t=NT, h=H)
            g = lambda x: x.rearrange("p t h k -> p (t h) k")
            m = lambda x: x.rearrange("p t h -> p (t h)")
            v.link(V.tensor_tensor(g(lg), L, spread(mlp2_b[:, :], 1, NT * H), ALU.add))
            v.link(V.tensor_reduce(m(lg_m), g(lg), AX_X, ALU.max))
            V.tensor_tensor(g(lg_p), g(lg), spread(m(lg_m), 2, 4), ALU.subtract).then_inc(S["lg_ready"], 1)
            dve.wait_ge(S["lg_exp"], 1)
            v.link(V.tensor_reduce(m(lg_s), g(lg_e), AX_X, ALU.add))
            v.link(V.reciprocal(m(lg_r), m(lg_s)))
            v.link(V.tensor_tensor(g(lg_p), g(lg_e), spread(m(lg_r), 2, 4), ALU.mult))
            v.link(V.tensor_scalar(g(lg_p), g(lg_p), 0.02, None, ALU.max))
            v.link(V.tensor_reduce(m(lg_s), g(lg_p), AX_X, ALU.add))
            v.link(V.reciprocal(m(lg_r), m(lg_s)))
            v.link(V.tensor_tensor(g(lg_p), g(lg_p), spread(m(lg_r), 2, 4), ALU.mult))
            v.link(V.tensor_tensor(lg_p[:, :, :, 0], lg_p[:, :, :, 0], spread(res_gate[:, :], 1, NT), ALU.add))
            for t in range(NT):
                v.step(V.tensor_tensor(mix[:, t], feats[:, t].rearrange("p k (h d) -> p k h d", h=H),
                                       spread(lg_p[:, t].rearrange("p h k -> p k h"), 3, DH), ALU.mult))
            v.settle()
            mk = lambda k: mix[:, :, k].rearrange("p t h d -> p t (h d)")
            v.step(V.tensor_tensor(mk(0), mk(0), mk(1), ALU.add))
            v.step(V.tensor_tensor(mk(2), mk(2), mk(3), ALU.add))
            v.settle()
            v.link(V.tensor_tensor(o_tok, mk(0), mk(2), ALU.add))
            v.link(V.tensor_tensor(o_sq, o_tok, o_tok, ALU.mult))
            oh = o_tok.rearrange("p t (h d) -> p (t h) d", h=H)
            v.link(V.tensor_reduce(ss[:, 0:NT * H], o_sq.rearrange("p t (h d) -> p (t h) d", h=H), AX_X, ALU.add))
            V.tensor_scalar(ss[:, 0:NT * H], ss[:, 0:NT * H], 1.0 / DH, 1e-5, ALU.mult, ALU.add).then_inc(S["mix_ss"], 1)
            dve.wait_ge(S["mix_root"], 1)
            v.link(V.reciprocal(unit[:, 0:NT * H], ss_sd[:, 0:NT * H]))
            V.tensor_tensor(oh, oh, spread(unit[:, 0:NT * H], 2, DH), ALU.mult).then_inc(S["mix_ready"], 1)
            dve.wait_ge(stored, (b + 1) * 16)
            add_hidden(dve, v, S["o_ps"], 2, 3, emb)

        def add_hidden(dve, v, ready, first, second, to):
            for half in range(2):
                dve.wait_ge(ready, half + 1)
                t2 = slice(2 * half, 2 * half + 2)
                v.step(nc.vector.tensor_tensor(hid[:, t2, :], to[:, t2, :],
                                               B[(first, second)[half]][:, :].rearrange("p (t c) -> p t c", t=2), ALU.add))
                moments(v, hid, range(2 * half, 2 * half + 2))

        def attn_gpsimd(pool):
            for lv in range(1, LEVELS):
                for t in range(NT):
                    n = (lv - 1) * NT + t
                    pool.wait_ge(S["gram_ready"], 2 * (t // 2) + 2)
                    if lv > 1:
                        pool.wait_ge(S["p_ps"], n - NT + 1)
                    nc.gpsimd.tensor_tensor(L_T[:, t], M_T[:, t], spread(level_mask[:, lv, :], 1, H), ALU.mult)\
                        .then_inc(S["lm_ready"], 1)

        BLOCKS_OF_TILE = P // TB
        SIM_AND_DOWN = [("sim", n) for n in range(4)]
        SIM_AND_DOWN += [("down", n) for n in range(6)] + [("sim", 4), ("sim", 5)]
        SIM_AND_DOWN += [("down", n) for n in range(6, 12)] + [("sim", 6), ("sim", 7)]
        SIM_AND_DOWN += [("down", n) for n in range(12, XC)]

        def peer_vector(dve, v):
            V = nc.vector
            dve.wait_ge(S["ln_out"], 2 * NT)
            V.scalar_tensor_tensor(xn[:, :, :], xn[:, :, :], float(D) ** 0.5, spread(gamma[:, :], 1, NT),
                                   ALU.mult, ALU.mult).then_inc(S["ln_out"], 1)
            for t in range(NT):
                dve.wait_ge(S["sim_ready"], 2 * t + 2)
                segs = [(c // PH, c % PH, sim[:, t % 2, c, :]) for c in range(2 * PH)]
                for p, h, x in segs:
                    v.step(V.max(val[:, p, t, h, 0:8], x))
                v.settle()
                for p, h, x in segs:
                    v.step(V.max_index(key[:, p, t, h, 0:8], val[:, p, t, h, 0:8], x))
                v.settle()
                for p, h, x in segs:
                    v.step(V.match_replace(x, val[:, p, t, h, 0:8], x, LOWEST))
                v.settle()
                for p, h, x in segs:
                    v.step(V.max(val[:, p, t, h, 8:16], x))
                v.settle()
                for p, h, x in segs[:-1]:
                    v.step(V.max_index(key[:, p, t, h, 8:16], val[:, p, t, h, 8:16], x))
                p, h, x = segs[-1]
                V.max_index(key[:, p, t, h, 8:16], val[:, p, t, h, 8:16], x).then_inc(S["sim_used"], 1)
            dve.wait_ge(S["sim_used"], NT)
            G = NT * PH
            vx, vy = (val[:, p].rearrange("p t h k -> p (t h) k") for p in range(2))
            for i in range(8):
                n = ROWLEN[i]
                v.step(V.tensor_tensor(cand[:, :, ROWAT[i]:ROWAT[i] + n], vy[:, :, 0:n],
                                       vx[:, :, i:i + 1].broadcast_to([P, G, n]), ALU.add))
            v.step(V.tensor_tensor(cand[:, :, ROWAT[8]:PAIRS], vx[:, :, 8:16],
                                   vy[:, :, 0:1].broadcast_to([P, G, 8]), ALU.add))
            v.step(V.tensor_copy(keyx, key[:, 0].rearrange("p t h k -> p k (t h)")))
            v.step(V.tensor_copy(keyy, key[:, 1].rearrange("p t h k -> p k (t h)")))
            v.settle()
            v.step(V.tensor_copy(key_d[:, 0:1, :], keyx[:, 0:1, :]))
            v.step(V.tensor_tensor(key_d[:, 1:TOPK, :], keyx[:, 1:TOPK, :], keyx[:, 0:TOPK - 1, :], ALU.subtract))
            for g in range(G):
                v.step(V.max(top[:, g, 0:8], cand[:, g, :]))
            v.settle()
            for g in range(G):
                v.step(V.max_index(pos[:, g, 0:8], top[:, g, 0:8], cand[:, g, :]))
            v.settle()
            for g in range(G):
                v.step(V.match_replace(cand[:, g, :], top[:, g, 0:8], cand[:, g, :], LOWEST))
            v.settle()
            for g in range(G):
                v.step(V.max(top[:, g, 8:16], cand[:, g, :]))
            v.settle()
            for g in range(G):
                v.step(V.max_index(pos[:, g, 8:16], top[:, g, 8:16], cand[:, g, :]))
            v.settle()
            v.step(V.tensor_copy(pos_b, pos.rearrange("p g k -> p k g")))
            V.tensor_tensor(e_w, top, top[:, :, 0:1].broadcast_to([P, G, TOPK]), ALU.subtract).then_inc(S["score_ready"], 1)
            v.settle()

            def look_up(out, at, op, consts, table):
                for m in range(TOPK):
                    v.step(V.tensor_scalar(look[:, m], flat(at), float(consts[m]), None, op))
                v.settle()
                look4 = look.rearrange("p m (k g) -> p m k g", g=G)
                v.link(V.tensor_tensor(look4, look4, spread(table, 2, TOPK), ALU.mult))
                add_up(out, TOPK)

            def add_up(out, n):
                while n > 1:
                    n //= 2
                    pairs = look[:, 0:2 * n].rearrange("p (m two) x -> p m two x", two=2)
                    if n > 1:
                        v.link(V.tensor_tensor(look[:, 0:n], pairs[:, :, 0], pairs[:, :, 1], ALU.add))
                    else:
                        a, b = (look[:, i].rearrange("p (k t h) -> p k t h", k=TOPK, t=NT) for i in range(2))
                        v.link(V.tensor_tensor(out, a, b, ALU.add))

            flat = lambda x: x.rearrange("p k g -> p (k g)")
            single = TOPK // 2
            for m in range(1, single):
                v.step(V.tensor_scalar(look[:, m], flat(pos_b), float(ROWAT[m]), float(ROWLEN[m - 1]), ALU.is_ge, ALU.mult))
            v.step(V.tensor_scalar(look[:, 0], flat(pos_b), -float(ROWAT[single]) , 0.0, ALU.add, ALU.max))
            v.step(V.tensor_scalar(look[:, single], flat(pos_b), float(ROWAT[single]), float(ROWLEN[single - 1]),
                                   ALU.is_ge, ALU.mult))
            v.settle()
            v.link(V.tensor_tensor(look[:, 0], look[:, 0], look[:, single], ALU.add))
            add_up(col_b.rearrange("p k (t h) -> p k t h", t=NT), single)
            dve.wait_ge(S["score_exp"], 1)
            v.link(V.tensor_reduce(e_s, e_w, AX_X, ALU.add))
            v.link(V.reciprocal(e_r, e_s))
            V.tensor_tensor(e_gate.rearrange("p t k h -> p t h k"), e_w.rearrange("p (t h) k -> p t h k", t=NT),
                            spread(e_r, 2, TOPK).rearrange("p (t h) k -> p t h k", t=NT), ALU.mult)\
                .then_inc(S["entry_ready"], 1)
            v.link(V.tensor_tensor(col_b, pos_b, col_b, ALU.subtract))
            look_up(e_x.rearrange("p t k h -> p k t h"), pos_b, ALU.is_ge, ROWAT, key_d)
            look_up(e_y.rearrange("p t k h -> p k t h"), col_b, ALU.is_equal, range(TOPK), keyy)
            v.link(V.tensor_scalar(e_far, e_y, float(YC), None, ALU.is_ge))
            v.step(V.scalar_tensor_tensor(e_x, e_far, float(NK), e_x, ALU.mult, ALU.add))
            V.scalar_tensor_tensor(e_y, e_far, -float(YC), e_y, ALU.mult, ALU.add).then_inc(S["entry_ready"], 1)
            dve.wait_ge(S["entry_ps"], 1)
            v.link(V.tensor_copy(entT_w[:, 0, :], B[6][:, :]))
            v.link(V.tensor_tensor(w_rest, B[6][:, :], entT_w[:, 0, :], ALU.subtract))
            v.link(V.tensor_copy(entT_w[:, 1, :], w_rest))
            v.link(V.tensor_tensor(w_rest, w_rest, entT_w[:, 1, :], ALU.subtract))
            v.link(V.tensor_copy(entT_w[:, 2, :], w_rest))
            dve.wait_ge(S["entT_ready"], 2)
            def gate(n):
                dve.wait_ge(S["cell_ps"], n + 1)
                part = grid[:, :, n * TB:(n + 1) * TB].rearrange("p j t -> p t j")
                V.tensor_tensor(part, B[n % 4][:, :].rearrange("p (t j) -> p t j", t=TB), part, ALU.mult)\
                    .then_inc(S["cell_ready"], 1)

            def add_tile(t):
                dve.wait_ge(S["up_ps"], t + 1)
                V.tensor_tensor(hid[:, t, :], hid[:, t, :], B[6 + t % 2][:, 0:D], ALU.add).then_inc(S["hid_peer"], 1)
                dve.wait_ge(S["hid_peer"], t + 1)
                moments(v, hid, (t,))

            for n in range(T // TB):
                hx, hy, hw = hots[n % 2]
                tt = slice(n * TB, (n + 1) * TB)
                if n >= 2:
                    dve.wait_ge(S["cell_ps"], n - 1)
                v.step(V.tensor_tensor(hy, spread(entT_y[:, tt], 1, YC), iota_y[:, :, :], ALU.is_equal))
                v.step(V.tensor_tensor(hx, spread(entT_x[:, tt], 1, P), iota_x[:, :, :], ALU.is_equal))
                v.settle()
                for i in range(3):
                    ins_ = V.tensor_tensor(hw[:, i], hy, spread(entT_w[:, i, tt], 1, YC), ALU.mult)
                    if i < 2:
                        v.step(ins_)
                    else:
                        ins_.then_inc(S["hot_ready"], 1)
                if n == 0:
                    dve.wait_ge(S["down_act"], XC)
                else:
                    gate(n - 1)
                if n in (BLOCKS_OF_TILE * 2 + 3, BLOCKS_OF_TILE * 3 + 3):
                    add_tile(n // BLOCKS_OF_TILE - 2)
            gate(T // TB - 1)
            add_tile(2)
            add_tile(3)
            dve.wait_ge(S["hid_peer"], NT)

        def peer_scalar(act):
            turn_scalar(act, xT, 2, 0, 1)
            for kind, n in SIM_AND_DOWN:
                if kind == "sim":
                    act.wait_ge(S["sim_ps"], n + 1)
                    if n >= 4:
                        act.wait_ge(S["sim_used"], n // 2 - 1)
                    nc.scalar.copy(sim[:, (n // 2) % 2, (n % 2) * PH:(n % 2 + 1) * PH, :],
                                   B[2 + n % 2][:, :].rearrange("p (h k) -> p h k", h=PH)).then_inc(S["sim_ready"], 1)
                else:
                    act.wait_ge(S["down_ps"], n + 1)
                    nc.scalar.activation(grid[:, n, :], B[n % 2][:, :], ACT.Gelu).then_inc(S["down_act"], 1)
            act.wait_ge(S["score_ready"], 1)
            nc.scalar.activation(e_w, e_w, ACT.Exp).then_inc(S["score_exp"], 1)
            for i, entT in enumerate((entT_x, entT_y)):
                act.wait_ge(S["entry_ps"], i + 2)
                nc.scalar.copy(entT, B[4 + i][:, :]).then_inc(S["entT_ready"], 1)

        def peer_tensor(pe):
            pe.wait_ge(S["ln_out"], 2 * NT + 1)
            turn_tensor(pe, xn, 2, 0, 1)
            turned(pe, 2)
            for kind, n in SIM_AND_DOWN:
                if kind == "sim":
                    t, half = n // 2, n % 2
                    if n >= 2:
                        pe.wait_ge(S["sim_ready"], n - 1)
                    for k in range(KD):
                        last = nc.tensor.matmul(B[2 + n % 2][:, :], xT[:, k, t * P:(t + 1) * P],
                                                w_sim[:, k, half * 512:(half + 1) * 512],
                                                start=(k == 0), stop=(k == KD - 1))
                    last.then_inc(S["sim_ps"], 1)
                else:
                    pe.wait_ge(tab_in[(n // 2) % 2], 16 * (n // 4 + 1))
                    if n >= 2:
                        pe.wait_ge(S["down_act"], n - 1)
                    for k in range(KD):
                        last = nc.tensor.matmul(B[n % 2][:, :], tab_d[:, (n // 2) % 2, n % 2, k, :], xT[:, k, :],
                                                start=(k == 0), stop=(k == KD - 1))
                    last.then_inc(S["down_ps"], 1)
            for i, e in enumerate((e_gate, e_x, e_y)):
                pe.wait_ge(S["entry_ready"], (1, 2, 2)[i])
                for t in range(NT):
                    last = nc.tensor.transpose(B[(6, 4, 5)[i]][:, t * P:(t + 1) * P], e[:, t].rearrange("p k h -> p (k h)"), ident[:, :])
                last.then_inc(S["entry_ps"], 1)
            pe.wait_ge(S["sim_ready"], 2 * NT)
            pe.wait_ge(S["down_act"], XC)

            def up(s):
                t, j0 = s // BLOCKS_OF_TILE, (s % BLOCKS_OF_TILE) * 4
                if j0 == 0:
                    pe.wait_ge(S["cell_ready"], BLOCKS_OF_TILE * (t + 1))
                    if t == 0:
                        pe.wait_ge(S["up_in"], 16 * 4)
                    if t >= 2:
                        pe.wait_ge(S["hid_peer"], t - 1)
                for j in range(j0, j0 + 4):
                    last = nc.tensor.matmul(B[6 + t % 2][:, 0:D], grid[:, j, t * P:(t + 1) * P], tab_u[:, j, :],
                                            start=(j == 0), stop=(j == XC - 1))
                if j0 + 4 == XC:
                    last.then_inc(S["up_ps"], 1)

            delay = BLOCKS_OF_TILE + 1
            for n in range(T // TB):
                hx, hy, hw = hots[n % 2]
                pe.wait_ge(S["hot_ready"], n + 1)
                if n >= 4:
                    pe.wait_ge(S["cell_ready"], n - 3)
                for t in range(TB):
                    for i in range(3):
                        last = nc.tensor.matmul(B[n % 4][:, t * YC:(t + 1) * YC], hx[:, :, t], hw[:, i, :, t],
                                                start=(i == 0), stop=(i == 2))
                last.then_inc(S["cell_ps"], 1)
                if n >= delay:
                    up(n - delay)
            for s in range(T // TB - delay, T // TB):
                up(s)

        def peer_sync(sp):
            sp.wait_ge(S["unit_ready"], 1)
            for j in range(XC // 2):
                if j >= 2:
                    sp.wait_ge(S["down_ps"], 2 * (j - 1))
                sp.dma_start(tab_d[:, j % 2], ins["downT"][:, 2 * j:2 * j + 2]).then_inc(tab_in[j % 2], 16)
            sp.wait_ge(S["entry_ps"], 3)
            for q in range(4):
                part = slice(q * XC // 4, (q + 1) * XC // 4)
                sp.dma_start(tab_u[:, part], ins["up"][:, part]).then_inc(S["up_in"], 16)

        def moe_sync(sp):
            for n in attn_names:
                sp.sem_clear(S[n])
            sp.wait_ge(S["up_ps"], NT)
            sp.dma_start(w1_shared, ins["W1"][NE:NE + 2].rearrange("e p k n -> p e k n")).then_inc(S["shared_in"], 16)
            sp.dma_start(w2_shared, ins["W2"][NE:NE + 2].rearrange("e p k n -> p e k n")).then_inc(S["shared_in"], 16)
            sp.wait_ge(S["sel_ready"], 1)
            for n in peer_names:
                sp.sem_clear(S[n])

        def ssm_tensor(pe):
            pe.wait_ge(late_loads, n_late[0])
            pe.wait_ge(S["ln_out"], 3 * NT + 1)
            turn_tensor(pe, xn, 3, 0, 1)
            turned(pe, 3)
            for e in range(2 * DI // P):
                if e >= 4:
                    pe.wait_ge(S["xz_ready"], e - 3)
                for k in range(KD):
                    last = nc.tensor.matmul(B[2 + e % 4][:, :], w_in[:, k, e * P:(e + 1) * P], xT[:, k, :],
                                            start=(k == 0), stop=(k == KD - 1))
                last.then_inc(S["xz_ps"], 1)
            pe.wait_ge(S["xz_ready"], 4)
            for k in range(DI // P):
                last = nc.tensor.matmul(B[6][0:DS, :], w_B[:, k, :], xz[:, k, :], start=(k == 0), stop=(k == DI // P - 1))
            last.then_inc(S["state_ps"], 1)
            pe.wait_ge(S["state_ready"], 1)
            pe.wait_ge(S["xz_ready"], 8)
            for e in range(DI // P):
                nc.tensor.matmul(B[2 + e][:, :], w_C[:, e * P:(e + 1) * P], states, start=True, stop=True)\
                    .then_inc(S["c_ps"], 1)
            pe.wait_ge(S["y_ready"], DI // P)
            for t in range(NT):
                for k in range(DI // P):
                    last = nc.tensor.matmul(B[t // 2][:, (t % 2) * D:(t % 2 + 1) * D], y[:, k, t * P:(t + 1) * P],
                                            w_out[:, k, :], start=(k == 0), stop=(k == DI // P - 1))
                if t % 2:
                    last.then_inc(S["so_ps"], 1)

        def ssm_scalar(act):
            act.wait_ge(late_loads, n_late[0])
            turn_scalar(act, xT, 3, 0, 1)
            for e in range(2 * DI // P):
                act.wait_ge(S["xz_ps"], e + 1)
                nc.scalar.activation(xz[:, e, :], B[2 + e % 4][:, :], ACT.Silu, bias=b_in[:, e:e + 1])\
                    .then_inc(S["xz_ready"], 1)

        def ssm_vector(dve, v):
            dve.wait_ge(late_loads, n_late[0])
            V = nc.vector
            dve.wait_ge(S["ln_out"], 3 * NT + 1)
            v.step(V.tensor_tensor(hid[:, :, :], hid[:, :, :], spread(b_out[:, :], 1, NT), ALU.add))
            dve.wait_ge(S["state_ps"], 1)
            v.link(V.tensor_scalar(drive, B[6][0:DS, :], 0.1, None, ALU.mult))
            V.tensor_tensor_scan(states, decay[:, :], drive, 0.0, ALU.mult, ALU.add).then_inc(S["state_ready"], 1)
            dve.wait_ge(S["xz_ready"], 8)
            for e in range(DI // P):
                dve.wait_ge(S["c_ps"], e + 1)
                v.link(V.scalar_tensor_tensor(y[:, e, :], xz[:, e, :], skip_D[:, e:e + 1], B[2 + e][:, :],
                                              ALU.mult, ALU.add))
                V.tensor_tensor(y[:, e, :], y[:, e, :], xz[:, DI // P + e, :], ALU.mult).then_inc(S["y_ready"], 1)
            add_hidden(dve, v, S["so_ps"], 0, 1, hid)

        def moe_tensor(pe):
            pe.wait_ge(S["ln_out"], 4 * NT + 1)
            turn_tensor(pe, xn, 4, 2, 3)
            turned(pe, 4)
            for t in range(NT):
                for k in range(KD):
                    last = nc.tensor.matmul(B[6][:, t * NE:(t + 1) * NE], xT[:, k, t * P:(t + 1) * P], gate_w[:, k, :],
                                            start=(k == 0), stop=(k == KD - 1))
            last.then_inc(S["gl_ps"], 1)

            def first(e):
                for c in range(FC):
                    for k in range(KD):
                        last = nc.tensor.matmul(B[c][:, :], w1_shared[:, e, k, c * P:(c + 1) * P], xT[:, k, :],
                                                start=(k == 0), stop=(k == KD - 1))
                    last.then_inc(S["e1_ps"], 1)

            def second(e):
                pe.wait_ge(S["e1_ready"], FC * (e + 1))
                for t in range(NT):
                    if NT * e + t >= 2:
                        pe.wait_ge(S["e2_used"], NT * e + t - 1)
                    for k in range(FC):
                        last = nc.tensor.matmul(B[4 + t % 2][:, 0:D], moe_h[:, e % 2, k, t * P:(t + 1) * P],
                                                w2_shared[:, e, k, :], start=(k == 0), stop=(k == FC - 1))
                    last.then_inc(S["e2_ps"], 1)

            pe.wait_ge(S["shared_in"], 32)
            first(0)
            pe.wait_ge(S["sel_ready"], 1)
            for t in range(NT):
                cols = slice(t * NE, (t + 1) * NE)
                last = nc.tensor.matmul(B[7][:, cols], strict[:, :], sel_b[:, t, 0:NE], start=True, stop=(t == 0))
                for u in range(t):
                    last = nc.tensor.matmul(B[7][:, cols], ones_b[:, :], sel_b[:, u, 0:NE], start=False, stop=(u == t - 1))
            for t in range(NT):
                last = nc.tensor.matmul(B[7][:, NT * NE:(NT + 1) * NE], ones_b[:, :], sel_b[:, t, 0:NE],
                                        start=(t == 0), stop=(t == NT - 1))
            last.then_inc(S["rank_ps"], 1)
            pe.wait_ge(S["gate_ready"], 1)
            for t in range(NT):
                last = nc.tensor.transpose(B[6][0:NE + 1, t * P:(t + 1) * P], gated[:, t, :], ident[:, :])
            last.then_inc(S["gate_ps"], 1)
            pe.wait_ge(S["gateT_ready"], 1)
            for t in range(NT):
                last = nc.tensor.matmul(B[4 + t // 2][:, (t % 2) * D:(t % 2 + 1) * D], gatedT[:, t * P:(t + 1) * P],
                                        b2_all[:, :], start=True, stop=True)
                if t % 2:
                    last.then_inc(S["bias_ps"], 1)
            pe.wait_ge(S["e1_ready"], FC)
            first(1)
            pe.wait_ge(S["hid_out"], 2)
            second(0)
            embed_turn_tensor(pe, S["embedded"], 0)
            second(1)
            embed_tensor(pe, S["embedded"], 0)

        def moe_scalar(act):
            turn_scalar(act, xT, 4, 2, 3)
            act.wait_ge(S["gl_ready"], 1)
            nc.scalar.activation(ge, gl, ACT.Exp).then_inc(S["gl_exp"], 1)
            for e in range(2):
                for k in range(FC):
                    act.wait_ge(S["e1_ps"], FC * e + k + 1)
                    nc.scalar.activation(moe_h[:, e % 2, k, :], B[k][:, :], ACT.Gelu,
                                         bias=b1_shared[:, e, k:k + 1]).then_inc(S["e1_ready"], 1)
                if e == 1:
                    embed_scalar(act, S["embedded"], 0)
                if e == 0:
                    act.wait_ge(S["gate_ps"], 1)
                    nc.scalar.copy(gatedT, B[6][0:NE + 1, :]).then_inc(S["gateT_ready"], 1)

        def moe_vector(dve, v, b):
            V = nc.vector
            dve.wait_ge(S["ln_out"], 4 * NT + 1)
            v.step(V.tensor_tensor(hid[:, :, :], hid[:, :, :], xn[:, :, :], ALU.add))
            v.step(V.memset(garr, -1.0))
            v.step(V.memset(gtake, -1.0))
            v.step(V.memset(gated, 1.0))
            dve.wait_ge(S["gl_ps"], 1)
            v.link(V.tensor_tensor(gl, B[6][:, 0:NT * NE].rearrange("p (t e) -> p t e", t=NT),
                                   spread(gate_b[:, :], 1, NT), ALU.add))
            v.link(V.tensor_reduce(gm, gl, AX_X, ALU.max))
            V.tensor_tensor(gl, gl, spread(gm, 2, NE), ALU.subtract).then_inc(S["gl_ready"], 1)
            dve.wait_ge(S["gl_exp"], 1)
            v.link(V.tensor_reduce(gs, ge, AX_X, ALU.add))
            v.link(V.reciprocal(gr, gs))
            v.link(V.tensor_tensor(garr[:, :, 0:NE], ge, spread(gr, 2, NE), ALU.mult))
            v.link(V.tensor_copy(ge, garr[:, :, 0:NE]))
            for t in range(NT):
                v.step(V.max(gtop[:, t, :], garr[:, t, :]))
            v.settle()
            v.link(V.tensor_copy(gtake[:, :, 0:TAKE], gtop[:, :, 0:TAKE]))
            for t in range(NT):
                v.step(V.match_replace(garr[:, t, :], gtake[:, t, :], garr[:, t, :], -2.0))
            v.settle()
            v.step(V.tensor_scalar(sel, garr[:, :, 0:NE], -2.0, None, ALU.is_equal))
            V.tensor_scalar(sel_b[:, :, 0:NE], garr[:, :, 0:NE], -2.0, None, ALU.is_equal).then_inc(S["sel_ready"], 1)
            V.scalar_tensor_tensor(gated[:, :, 0:NE], garr[:, :, 0:NE], -2.0, ge, ALU.is_equal, ALU.mult)\
                .then_inc(S["gate_ready"], 1)
            v.settle()
            v.link(V.tensor_tensor_scan(nth.rearrange("p t e -> p (t e)"), restart[:, :, :].rearrange("p t e -> p (t e)"),
                                        sel.rearrange("p t e -> p (t e)"), 0.0, ALU.mult, ALU.add))
            for k in range(TAKE):
                v.step(V.scalar_tensor_tensor(hot3[:, :, k, :], nth, float(k + 1), sel, ALU.is_equal, ALU.mult))
            dve.wait_ge(S["rank_ps"], 1)
            v.link(V.tensor_tensor(rank, B[7][:, 0:NT * NE].rearrange("p (t e) -> p t e", t=NT),
                                   spread(count[:, :], 1, NT), ALU.add))
            v.step(V.tensor_tensor(count[:, :], count[:, :], B[7][:, NT * NE:(NT + 1) * NE], ALU.add))
            v.step(V.tensor_tensor(slot, rank, spread(region_at[:, :], 1, NT), ALU.add))
            v.settle()
            dve.wait_ge(S["gate_ready"], 1)
            for what, to in ((slot, slot3), (rank, rank3), (gated[:, :, 0:NE], gate3)):
                v.link(V.tensor_tensor(pick3, hot3, spread(what, 2, TAKE), ALU.mult))
                v.link(V.tensor_reduce(to, pick3, AX_X, ALU.add))
                if what is slot:
                    V.tensor_copy(slot_u, slot3).then_inc(S["slot_ready"], 1)
            tiles = bass.ds(b * NT, NT)
            v.step(V.tensor_copy(all_hot[:, tiles], hot3))
            v.step(V.tensor_copy(all_rank[:, tiles], rank3))
            v.step(V.tensor_copy(all_gate[:, tiles], gate3))
            for half in range(2):
                dve.wait_ge(S["bias_ps"], half + 1)
                t2 = slice(2 * half, 2 * half + 2)
                V.tensor_tensor(hid[:, t2, :], hid[:, t2, :], B[4 + half][:, :].rearrange("p (t c) -> p t c", t=2),
                                ALU.add).then_inc(S["hid_out"], 1)
            dve.wait_ge(S["hid_out"], 2)
            embed_rows_vector(dve, v, (b + 2) * (16 * 4 * NT), S["embedded"])
            for e in range(2):
                for t in range(NT):
                    n = NT * e + t
                    dve.wait_ge(S["e2_ps"], n + 1)
                    if e:
                        dve.wait_ge(S["e2_used"], n - NT + 1)
                    V.tensor_tensor(hid[:, t, :], B[4 + t % 2][:, 0:D], hid[:, t, :], ALU.add)\
                        .then_inc(S["e2_used"], 1)
            dve.wait_ge(S["e2_used"], 2 * NT)
            embed_vector(dve, v, S["embedded"], 0)

        def moe_gpsimd(pool, b):
            pool.wait_ge(S["slot_ready"], 1)
            for t in range(NT):
                for k in range(TAKE):
                    nc.gpsimd.indirect_dma_start(rows_d, bass.IndirectOffsetOnAxis(ap=slot_u[:, t, k:k + 1], axis=0),
                                                 xn[:, t, :], None).then_inc(scattered, 16)
            pool.wait_ge(scattered, (b + 1) * (16 * NT * TAKE))

        LEAD = RING + 1
        LOOPS = (TILES - RING - LEAD) // RING
        TAIL = LEAD + LOOPS * RING

        def routed_vector_tables(dve, v):
            V = nc.vector
            v.step(V.memset(one_row, 1.0))
            v.link(V.tensor_scalar(n_tiles, count[:, :], float(TILE - 1), None, ALU.add))
            v.link(V.tensor_copy(t_int, n_tiles))
            v.link(V.tensor_scalar(t_int, t_int, TILE.bit_length() - 1, None, ALU.arith_shift_right))
            v.link(V.tensor_copy(n_tiles, t_int))
            v.link(V.tensor_tensor_scan(t_sum, one_row, n_tiles, 0.0, ALU.mult, ALU.add))
            v.step(V.tensor_tensor(t_start, t_sum, n_tiles, ALU.subtract))
            v.step(V.scalar_tensor_tensor(t_ahead, n_tiles, float(TILE), count[:, :], ALU.mult, ALU.subtract))
            v.step(V.tensor_scalar(t_step, t_sum[:, NE - 1:NE], -1.0, None, ALU.add))
            v.settle()
            v.step(V.tensor_scalar(t_min, tile_no[:, :], t_step, None, ALU.min))
            v.link(V.tensor_tensor(t_row0, region_at[:, :], t_ahead, ALU.subtract))
            v.link(V.scalar_tensor_tensor(t_row0, t_start, -float(TILE), t_row0, ALU.mult, ALU.add))
            v.step(V.tensor_copy(t_jump[:, 0:1], t_row0[:, 0:1]))
            v.step(V.tensor_tensor(t_jump[:, 1:NE], t_row0[:, 1:NE], t_row0[:, 0:NE - 1], ALU.subtract))
            v.step(V.tensor_tensor(t_ge, spread(t_min, 2, NE), spread(t_start, 1, TILES), ALU.is_ge))
            v.settle()
            v.step(V.tensor_reduce(t_exp, t_ge, AX_X, ALU.add))
            v.link(V.tensor_tensor(t_gs, t_ge, spread(t_jump, 1, TILES), ALU.mult))
            v.step(V.tensor_scalar(t_exp, t_exp, -1.0, None, ALU.add))
            v.link(V.tensor_reduce(t_row, t_gs, AX_X, ALU.add))
            v.step(V.tensor_copy(tile_exp, t_exp))
            v.link(V.scalar_tensor_tensor(t_row, t_min, float(TILE), t_row, ALU.mult, ALU.add))
            V.tensor_copy(tile_row, t_row).then_inc(routed, 1)
            v.link(V.scalar_tensor_tensor(t_sum, t_start, float(TILE), t_ahead, ALU.mult, ALU.add))
            v.link(V.tensor_tensor(y_pick.rearrange("p t k e -> p (t k) e"), all_hot[:, :, :, :].rearrange("p t k e -> p (t k) e"),
                                   spread(t_sum, 1, BATCH * NT * TAKE), ALU.mult))
            v.link(V.tensor_reduce(y_slot, y_pick, AX_X, ALU.add))
            v.link(V.tensor_tensor(y_slot, y_slot, all_rank[:, :, :], ALU.add))
            V.tensor_copy(y_slot_u, y_slot).then_inc(routed, 1)

        def load_rows(act, n, p):
            row = act.value_load(tile_row[0:1, bass.ds(n, 1)] if not isinstance(n, int) else tile_row[0:1, n:n + 1],
                                 min_val=0, max_val=NE * REGION - TILE)
            act.dma_start(r_x[:, p], rows_d[bass.ds(row, TILE)].rearrange("(h p) c -> p h c", p=P)).then_inc(x_in[p], 16)

        def load_expert(act, n, p):
            e = act.value_load(tile_exp[0:1, bass.ds(n, 1)] if not isinstance(n, int) else tile_exp[0:1, n:n + 1],
                               min_val=0, max_val=NE - 1)
            act.dma_start(r_w1[:, p], ins["W1"][bass.ds(e, 1)].rearrange("a p k n -> p (a k) n")).then_inc(rw_in[p], 16)
            act.dma_start(r_w2[:, p], ins["W2"][bass.ds(e, 1)].rearrange("a p k n -> p (a k) n")).then_inc(rw_in[p], 16)
            act.dma_start(r_b1[:, p], ins["b1"][bass.ds(e, 1)].rearrange("a p k -> p (a k)")).then_inc(rw_in[p], 16)

        def expert_tensor(pe, n, p, r):
            if not isinstance(n, int) or n + 1 < TILES:
                turn_rows(pe, n + 1, (p + 1) % RING, r + (p + 1) // RING)
            pe.wait_ge(rw_in[p], 48 * r)
            pe.wait_ge(xt_ready, n + 1)
            for c in range(FC):
                bank = B[1 + 2 * p + c // 2]
                for k in range(KD):
                    last = nc.tensor.matmul(bank[:, (c % 2) * TILE:(c % 2 + 1) * TILE], r_w1[:, p, k, c * P:(c + 1) * P],
                                            r_xT[:, p, k, :], start=(k == 0), stop=(k == KD - 1))
                if c % 2:
                    last.then_inc(m1_ps, 1)

        def turn_rows(pe, n, p, r):
            pe.wait_ge(x_in[p], 16 * r)
            if not isinstance(n, int) or n > 0:
                pe.wait_ge(xt_ready, n)
            for k in range(KD):
                for h in range(HALF):
                    last = nc.tensor.transpose(B[0][:, k * TILE + h * P:k * TILE + (h + 1) * P],
                                               r_x[:, p, h, k * P:(k + 1) * P], ident[:, :])
            last.then_inc(xt_ps, 1)

        def second_product(pe, n, p):
            pe.wait_ge(m1_ready, FC * (n + 1))
            if not isinstance(n, int) or n > 0:
                pe.wait_ge(m2_ready, n)
            for h in range(HALF):
                for k in range(FC):
                    last = nc.tensor.matmul(B[7][:, h * D:(h + 1) * D], r_h[:, p, k, h * P:(h + 1) * P], r_w2[:, p, k, :],
                                            start=(k == 0), stop=(k == FC - 1))
            last.then_inc(m2_ps, 1)

        def routed_tensor(pe):
            turn_rows(pe, 0, 0, 1)
            for n in range(LEAD):
                expert_tensor(pe, n, n % RING, n // RING + 1)
                if n:
                    second_product(pe, n - 1, (n - 1) % RING)
            with pe.Fori(0, LOOPS) as i:
                for q in range(RING):
                    p = (LEAD + q) % RING
                    expert_tensor(pe, i * RING + LEAD + q, p, i + 1 + (LEAD + q) // RING)
                    second_product(pe, i * RING + LEAD + q - 1, (p - 1) % RING)
            for n in range(TAIL, TILES):
                expert_tensor(pe, n, n % RING, n // RING + 1)
                second_product(pe, n - 1, (n - 1) % RING)
            second_product(pe, TILES - 1, (TILES - 1) % RING)

        def activate(act, n, p, rows_ahead=True, expert_ahead=True):
            for c in range(FC):
                act.wait_ge(m1_ps, 2 * n + c // 2 + 1)
                nc.scalar.activation(r_h[:, p, c, :], B[1 + 2 * p + c // 2][:, (c % 2) * TILE:(c % 2 + 1) * TILE], ACT.Gelu,
                                     bias=r_b1[:, p, c:c + 1]).then_inc(m1_ready, 1)
            if rows_ahead:
                act.wait_ge(xt_ps, n + 1)
                load_rows(act, n + 3, p)
            if expert_ahead:
                act.wait_ge(m2_ps, n)
                load_expert(act, n + 2, (p + 2) % RING)

        def routed_scalar(act):
            act.wait_ge(routed, 1)
            for n in range(RING):
                load_rows(act, n, n)
                load_expert(act, n, n)
            for n in range(LEAD):
                activate(act, n, n % RING, expert_ahead=n > 0)
            with act.Fori(0, LOOPS) as i:
                for q in range(RING):
                    activate(act, i * RING + LEAD + q, (LEAD + q) % RING)
            for n in range(TAIL, TILES):
                activate(act, n, n % RING, n + RING < TILES, n + 2 < TILES)

        def expert_vector(dve, n, p):
            dve.wait_ge(xt_ps, n + 1)
            nc.vector.tensor_copy(r_xT[:, p].rearrange("p k n -> p (k n)"), B[0][:, :]).then_inc(xt_ready, 1)

        def output_vector(dve, n, p, r):
            dve.wait_ge(m2_ps, n + 1)
            if not isinstance(n, int) or n >= RING:
                dve.wait_ge(y_stored[p], 16 * (r - 1))
            nc.vector.tensor_copy(r_y[:, p].rearrange("p h c -> p (h c)"), B[7][:, :]).then_inc(m2_ready, 1)

        def routed_vector(dve, v):
            routed_vector_tables(dve, v)
            expert_vector(dve, 0, 0)
            for n in range(LEAD):
                expert_vector(dve, n + 1, (n + 1) % RING)
                if n:
                    output_vector(dve, n - 1, (n - 1) % RING, (n - 1) // RING + 1)
            with dve.Fori(0, LOOPS) as i:
                for q in range(RING):
                    n = i * RING + LEAD + q
                    expert_vector(dve, n + 1, (LEAD + q + 1) % RING)
                    output_vector(dve, n - 1, (LEAD + q - 1) % RING, i + (LEAD + q - 1) // RING + 1)
            for n in range(TAIL, TILES):
                if n + 1 < TILES:
                    expert_vector(dve, n + 1, (n + 1) % RING)
                output_vector(dve, n - 1, (n - 1) % RING, (n - 1) // RING + 1)
            output_vector(dve, TILES - 1, (TILES - 1) % RING, (TILES - 1) // RING + 1)
            dve.wait_ge(base_in, 16 * BATCH)
            for b in range(BATCH):
                dve.wait_ge(gathered[b], 16 * NT * TAKE)
                for k in range(TAKE):
                    for t in range(b * NT, (b + 1) * NT):
                        ins_ = nc.vector.scalar_tensor_tensor(f_base[:, t], f_rows[:, t, k], all_gate[:, t, k:k + 1],
                                                              f_base[:, t], ALU.mult, ALU.add)
                        if k == TAKE - 1:
                            ins_.then_inc(mixed, 1)
                        else:
                            v.step(ins_)
                    if k < TAKE - 1:
                        v.settle()

        def routed_sync(sp):
            sp.wait_ge(routed, 2)
            full = TILES // RING
            with sp.Fori(0, full) as i:
                for p in range(RING):
                    store_tile(sp, i * RING + p, p)
            for n in range(full * RING, TILES):
                store_tile(sp, n, n % RING)
            sp.wait_ge(stored, 16 * (BATCH + 1))
            for b in range(BATCH):
                sp.dma_start(f_base[:, b * NT:(b + 1) * NT], base_d[b]).then_inc(base_in, 16)
            for b in range(BATCH):
                sp.wait_ge(mixed, (b + 1) * NT)
                sp.dma_start(out[b].rearrange("(t p) c -> p t c", p=P), f_base[:, b * NT:(b + 1) * NT]).then_inc(final_out, 16)
            sp.wait_ge(final_out, 16 * BATCH)

        def store_tile(sp, n, p):
            sp.wait_ge(m2_ready, n + 1)
            sp.dma_start(outs_d[bass.ds(n * TILE, TILE)].rearrange("(h p) c -> p h c", p=P), r_y[:, p]).then_inc(y_stored[p], 16)

        def routed_gpsimd(pool):
            pool.wait_ge(routed, 2)
            for p in range(RING):
                pool.wait_ge(y_stored[p], 16 * ((TILES - 1 - p) // RING + 1))
            for t in range(BATCH * NT):
                for k in range(TAKE):
                    nc.gpsimd.indirect_dma_start(f_rows[:, t, k], None, outs_d,
                                                 bass.IndirectOffsetOnAxis(ap=y_slot_u[:, t, k:k + 1], axis=0))\
                        .then_inc(gathered[t // NT], 16)

        def finish_sequence(eng, b):
            eng.sem_inc(iter_done, 1)
            eng.wait_ge(go_on, b + 1)

        E, A_, PE_, S_, M_ = (c in stages for c in "EAPSM")

        @block.sync
        def _(sp):
            ids_sync(sp, 0, first_ids)
            setup_sync(sp)
            sp.wait_ge(first_rows, 4)
            sp.sem_inc(stored, 16)
            with sp.Fori(0, BATCH) as b:
                if A_:
                    attn_sync(sp, b)
                if PE_:
                    peer_sync(sp)
                if M_:
                    moe_sync(sp)
                sp.wait_ge(iter_done, 1)
                if M_:
                    sp.dma_start(base_d[bass.ds(b, 1)].rearrange("a p t c -> p (a t) c"), hid[:, :, :])\
                        .then_inc(stored, 16)
                else:
                    sp.dma_start(out[bass.ds(b, 1)].rearrange("a (t p) c -> p (a t) c", p=P), hid[:, :, :])\
                        .then_inc(stored, 16)
                sp.wait_ge(iter_done, 4)
                for n in names:
                    if not (A_ and M_ and n in attn_names + peer_names):
                        sp.sem_clear(S[n])
                sp.sem_clear(iter_done)
                sp.sem_inc(go_on, 1)
            if M_:
                routed_sync(sp)

        @block.gpsimd
        def _(pool):
            pool.wait_ge(first_rows, 4)
            gather_rows(pool)
            with pool.Fori(0, BATCH) as b:
                if A_:
                    attn_gpsimd(pool)
                if PE_:
                    pool.wait_ge(S["rows_ready"], 4)
                    pool.wait_ge(S["up_ps"], NT)
                    gather_rows(pool)
                if M_:
                    moe_gpsimd(pool, b)
                if PE_:
                    pool.wait_ge(rows_in, (b + 2) * (16 * 4 * NT))
                pool.wait_ge(iter_done, 1)
                finish_sequence(pool, b)
            if M_:
                routed_gpsimd(pool)

        @block.tensor
        def _(pe):
            setup_tensor(pe)
            pe.wait_ge(loads, n_loads[0])
            embed_turn_tensor(pe, first_embedded, 0)
            embed_tensor(pe, first_embedded, 0)
            pe.wait_ge(made, MADE)
            with pe.Fori(0, BATCH) as b:
                if A_:
                    pe.wait_ge(S["ln_out"], NT)
                    turn_tensor(pe, xn, 0, 0, 1)
                    attn_tensor(pe)
                if PE_:
                    peer_tensor(pe)
                if S_:
                    ssm_tensor(pe)
                if M_:
                    moe_tensor(pe)
                pe.wait_ge(iter_done, 1)
                finish_sequence(pe, b)
            if M_:
                routed_tensor(pe)

        @block.scalar
        def _(act):
            setup_scalar(act)
            embed_scalar(act, first_embedded, 0)
            act.wait_ge(made, MADE)
            with act.Fori(0, BATCH) as b:
                if A_:
                    norm_scalar(act, 0)
                    turn_scalar(act, xT, 0, 0, 1)
                    attn_scalar(act)
                if PE_:
                    norm_scalar(act, 1)
                    peer_scalar(act)
                if S_:
                    norm_scalar(act, 2)
                    ssm_scalar(act)
                if M_:
                    norm_scalar(act, 3)
                    moe_scalar(act)
                act.wait_ge(iter_done, 1)
                finish_sequence(act, b)
            if M_:
                routed_scalar(act)

        @block.vector
        def _(dve):
            nc.vector.memset(zeros, 0.0).then_inc(zeros_ready, 1)
            v = Chain(dve, first_step)
            ids_vector(dve, v, first_ids, first_rows)
            embed_rows_vector(dve, v, 16 * 4 * NT, first_embedded)
            setup_vector(dve)
            embed_vector(dve, v, first_embedded, 0)
            dve.wait_ge(made, MADE)
            with dve.Fori(0, BATCH) as b:
                v = Chain(dve, S["dve_step"])
                if A_:
                    norm_vector(dve, v, 0, emb)
                    attn_vector(dve, v, b)
                if PE_:
                    norm_vector(dve, v, 1, hid, rms=True)
                    peer_vector(dve, v)
                if S_:
                    norm_vector(dve, v, 2, hid)
                    ssm_vector(dve, v)
                if M_:
                    norm_vector(dve, v, 3, hid)
                    moe_vector(dve, v, b)
                finish_sequence(dve, b)
            if M_:
                routed_vector(dve, Chain(dve, mix_step))


def kernel(**inputs):
    import concourse.bacc as _bacc
    from concourse.bass_utils import run_bass_kernel_spmd as _run

    nc = _bacc.Bacc("TRN2", target_bir_lowering=False, num_devices=1)
    arrays = arrange(inputs)
    ins = {n: nc.dram_tensor(f"in_{n}", a.shape, mybir.dt.from_np(a.dtype), kind="ExternalInput").ap()
           for n, a in arrays.items()}
    out = nc.dram_tensor("out_0", (BATCH, T, D), F32, kind="ExternalOutput").ap()
    build(nc, ins, out)
    r = _run(nc, [{f"in_{n}": a for n, a in arrays.items()}], core_ids=[0])
    return r.results[0]["out_0"]


def arrange(inputs):
    g = {n: np.asarray(a) for n, a in inputs.items()}
    a, p, q, m = (lambda n, pre=pre: g[pre + n] for pre in ("L0_attn_", "L0_ffn_", "L1_attn_", "L1_ffn_"))
    cols = lambda v: v.reshape(-1, P).T
    tokens = g["x"].reshape(BATCH, NT, P).transpose(0, 2, 1)
    z = {"x": np.concatenate([tokens, tokens[:1]])}
    for i in range(4):
        z[f"emb{i}"] = g[f"L0_tok_emb{i}"]
    z["proj"] = np.concatenate([g["L0_tok_proj1"], g["L0_tok_proj2"], g["L0_tok_proj3"]])
    for n in "qkv":
        z[f"{n}_wT"] = a(f"{n}_w").T
        z[f"{n}_cw"] = a(f"{n}_cw")
    z["b_wT"] = a("b_w").T
    z["fir_short"] = a("fir_short_w").reshape(D, SHORT)
    z["fir_long"] = np.zeros((D, 3 * LONG), np.float32)
    z["fir_long"][:, LONG:2 * LONG] = a("fir_long_w").reshape(D, LONG)[:, ::-1]
    z["long_w"] = a("fir_long_w").reshape(D, LONG)[P:]
    z["mlp1_aT"] = a("mlp1_w")[:, :D].T
    z["mlp1_sT"] = np.zeros((H, H * 16, D), np.float32)
    for h in range(H):
        z["mlp1_sT"][h, 16 * h:16 * h + 16] = a("mlp1_w")[:, D:].T
    z["mlp1_b"], z["mlp2_wT"], z["mlp2_b"] = cols(a("mlp1_b")), np.zeros((H, D, H * 4), np.float32), a("mlp2_b")
    for h in range(H):
        z["mlp2_wT"][h, :, 4 * h:4 * h + 4] = a("mlp2_w").T
    z["logit_temp"], z["conv_res"], z["o_wT"] = a("logit_temp"), a("conv_res_logit"), a("o_w").T
    z["norm_w"] = np.tile(a("norm_w"), 2).reshape(P, 1)
    z["gamma"], z["wq"] = p("gamma"), p("wq")
    z["keysT"] = p("keys").transpose(2, 0, 3, 1).reshape(2 * PH, P, NK)
    rows = lambda t: t[:NX].reshape(NK, 2, YC, D).transpose(2, 1, 0, 3).reshape(XC, P, D)
    z["downT"] = rows(p("table_down")).reshape(XC, P, KD, P).transpose(3, 0, 2, 1)
    z["up"] = rows(p("table_up")).transpose(1, 0, 2)
    z["W_inT"], z["b_in"], z["W_BT"], z["W_CT"] = q("W_in").T, cols(q("b_in")), q("W_B").T, q("W_C").T
    z["D"], z["W_outT"], z["b_out"] = cols(q("D")), q("W_out").T, q("b_out")
    z["gW"], z["gb"] = m("gW"), m("gb")
    w1 = np.concatenate([m("rW1"), m("sW1").reshape(D, 2, FF).transpose(1, 0, 2)])
    w2 = np.concatenate([m("rW2"), m("sW2").reshape(2, FF, D)])
    z["W1"] = w1.reshape(NE + 2, KD, P, FF).transpose(0, 2, 1, 3)
    z["W2"] = w2.reshape(NE + 2, FC, P, D).transpose(0, 2, 1, 3)
    z["b1"] = np.concatenate([m("rb1"), m("sb1").reshape(2, FF)]).reshape(NE + 2, FC, P).transpose(0, 2, 1)
    z["b2"] = np.concatenate([m("rb2"), m("sb2")])
    z["c_ident"] = np.eye(P, dtype=np.float32)
    i, j = np.arange(P)[:, None], np.arange(P)[None, :]
    z["c_levels"] = np.stack([((i >> (lv + 1)) == (j >> (lv + 1))) & ((i >> lv) & 1 == 0) & ((j >> lv) & 1 == 1)
                              for lv in range(LEVELS)]).astype(np.float32)
    z["c_causal"] = (i <= j).astype(np.float32)
    z["c_flips"] = np.stack([i + j == P - 1, i + j == P // 2 - 1, i + j == P + P // 2 - 1], 1).astype(np.float32)
    z["c_iota"] = np.arange(P, dtype=np.float32)
    z["c_region"] = (np.arange(NE) * REGION + TILE).astype(np.float32)
    z["c_restart"] = np.tile(np.arange(NE) > 0, NT).astype(np.float32)
    return {n: np.ascontiguousarray(v) for n, v in z.items()}
```
